# Optimizing a Trainium2 kernel written in Bass

```python
import numpy as np
import jax
import jax.numpy as jnp

def _softmax(x, axis=-1):
    return jax.nn.softmax(x, axis=axis)

def _gelu(x):
    return jax.nn.gelu(x, approximate=True)

def _silu(x):
    return jax.nn.silu(x)

def _sigmoid(x):
    return jax.nn.sigmoid(x)

def _layernorm(x, axis=-1, eps=1e-05):
    m = jnp.mean(x, axis=axis, keepdims=True)
    v = jnp.var(x, axis=axis, keepdims=True)
    return (x - m) / jnp.sqrt(v + eps)

def _scatter_add(tgt, idx, src, axis=0):
    return tgt.at[idx].add(src)

def _segment_sum(src, seg, n):
    return jax.ops.segment_sum(src, seg, n)
kernel_name = 'mk_hybrid_d1_jaxref_r8_a56867'

def setup_inputs(seed: int=0):
    np.random.seed(seed)
    _w = jnp.asarray

    def _L0_attn_a_setup():
        import jax, jax.numpy as jnp
        import numpy as np
        key = jax.random.key(seed)
        k1, k2, k3, k4 = jax.random.split(key, 4)
        batch, n_channels, t = (4, 256, 256)
        n_blocks, block_size, ks = (128, 64, 16)
        n_block_row = n_channels // block_size
        x = jax.random.normal(k1, (batch, n_channels, t), dtype=jnp.float32)
        block_values = jax.random.normal(k2, (n_blocks, block_size, block_size, ks), dtype=jnp.float32) * 0.05
        cols = jax.random.randint(k3, (n_blocks,), 0, n_block_row, dtype=jnp.int32)
        rows = jax.random.randint(k4, (n_blocks,), 0, n_block_row, dtype=jnp.int32)
        return {'x': x, 'block_values': block_values, 'cols': cols, 'rows': rows}
    _L0_attn_a_in = _L0_attn_a_setup()

    def _L0_attn_b_setup():
        import jax, jax.numpy as jnp
        import numpy as np
        B, T, D_MODEL = (2, 256, 256)
        N_HEADS, N_KV_HEADS, HEAD_DIM = (16, 4, 128)
        N_REP = N_HEADS // N_KV_HEADS
        EPS = 1e-06

        def _qknorm(t, scale):
            norm = jax.lax.rsqrt(jnp.mean(t * t, axis=-1, keepdims=True) + EPS)
            return t * norm * scale
        key = jax.random.key(seed)
        ks = jax.random.split(key, 5)
        return {'x': jax.random.normal(ks[0], (B, T, D_MODEL), dtype=jnp.float32), 'Wq': jax.random.normal(ks[1], (N_HEADS * HEAD_DIM, D_MODEL), dtype=jnp.float32) * 0.02, 'Wk': jax.random.normal(ks[2], (N_KV_HEADS * HEAD_DIM, D_MODEL), dtype=jnp.float32) * 0.02, 'Wv': jax.random.normal(ks[3], (N_KV_HEADS * HEAD_DIM, D_MODEL), dtype=jnp.float32) * 0.02, 'Wo': jax.random.normal(ks[4], (D_MODEL, N_HEADS * HEAD_DIM), dtype=jnp.float32) * 0.02, 'q_scale': jnp.ones((HEAD_DIM,), dtype=jnp.float32), 'k_scale': jnp.ones((HEAD_DIM,), dtype=jnp.float32)}
    _L0_attn_b_in = _L0_attn_b_setup()

    def _L0_ffn_setup():
        import jax, jax.numpy as jnp
        import numpy as np
        from jax import lax
        H = 256
        I = 176
        E = 16
        TOP_K = 6
        IS = 2 * I

        def _swiglu(x, w13_, w2_):
            gu = x @ w13_.T
            g, u = jnp.split(gu, 2, axis=-1)
            return jax.nn.silu(g) * u @ w2_.T
        key = jax.random.key(seed)
        ks = jax.random.split(key, 6)
        return {'hidden_states': jax.random.normal(ks[0], (1, 256, H), jnp.float32), 'gate_w': jax.random.normal(ks[1], (E, H), jnp.float32) * 0.02, 'w13': jax.random.normal(ks[2], (E, 2 * I, H), jnp.float32) * 0.02, 'w2': jax.random.normal(ks[3], (E, H, I), jnp.float32) * 0.02, 'sw13': jax.random.normal(ks[4], (2 * IS, H), jnp.float32) * 0.02, 'sw2': jax.random.normal(ks[5], (H, IS), jnp.float32) * 0.02}
    _L0_ffn_in = _L0_ffn_setup()
    _d = {'L0_attn_a_x': _L0_attn_a_in['x'], 'L0_attn_a_block_values': _L0_attn_a_in['block_values'], 'L0_attn_a_cols': _L0_attn_a_in['cols'], 'L0_attn_a_rows': _L0_attn_a_in['rows'], 'L0_attn_b_Wq': _L0_attn_b_in['Wq'], 'L0_attn_b_Wk': _L0_attn_b_in['Wk'], 'L0_attn_b_Wv': _L0_attn_b_in['Wv'], 'L0_attn_b_Wo': _L0_attn_b_in['Wo'], 'L0_attn_b_q_scale': _L0_attn_b_in['q_scale'], 'L0_attn_b_k_scale': _L0_attn_b_in['k_scale'], 'L0_ffn_gate_w': _L0_ffn_in['gate_w'], 'L0_ffn_w13': _L0_ffn_in['w13'], 'L0_ffn_w2': _L0_ffn_in['w2'], 'L0_ffn_sw13': _L0_ffn_in['sw13'], 'L0_ffn_sw2': _L0_ffn_in['sw2']}
    _x0 = _d['L0_attn_a_x']
    _d['L0_attn_a_x'] = jax.random.normal(jax.random.fold_in(jax.random.key(seed), 1), (2, 512, 256), dtype=_x0.dtype)
    del _x0
    return _d

def reference(L0_attn_a_x, L0_attn_a_block_values, L0_attn_a_cols, L0_attn_a_rows, L0_attn_b_Wq, L0_attn_b_Wk, L0_attn_b_Wv, L0_attn_b_Wo, L0_attn_b_q_scale, L0_attn_b_k_scale, L0_ffn_gate_w, L0_ffn_w13, L0_ffn_w2, L0_ffn_sw13, L0_ffn_sw2):

    def _L0_attn_a_ref(x, block_values, cols, rows):
        import jax, jax.numpy as jnp
        import numpy as np
        batch, n_channels, t = x.shape
        n_blocks, bs, _, ks = block_values.shape
        n_block_row = -(-n_channels // bs)
        pad = n_block_row * bs - n_channels
        if pad > 0:
            x = jnp.pad(x, ((0, 0), (0, pad), (0, 0)))
        xb = x.reshape(batch, n_block_row, bs, t)
        x_unfold = xb[:, cols].reshape(batch, n_blocks * bs, t)
        W = block_values.reshape(n_blocks * bs, bs, ks)
        o = jax.lax.conv_general_dilated(x_unfold, W, window_strides=(1,), padding=[(ks - 1, 0)], dimension_numbers=('NCH', 'OIH', 'NCH'), feature_group_count=n_blocks)
        o = o.reshape(batch, n_blocks, bs, t)
        y = jnp.zeros((batch, n_block_row, bs, t), o.dtype).at[:, rows].add(o)
        y = y.reshape(batch, n_block_row * bs, t)
        return y[:, :n_channels, :]

    def _L0_attn_b_ref(x, Wq, Wk, Wv, Wo, q_scale, k_scale):
        import jax, jax.numpy as jnp
        import numpy as np
        B, T, D_MODEL = (2, 256, 256)
        N_HEADS, N_KV_HEADS, HEAD_DIM = (16, 4, 128)
        N_REP = N_HEADS // N_KV_HEADS
        EPS = 1e-06

        def _qknorm(t, scale):
            norm = jax.lax.rsqrt(jnp.mean(t * t, axis=-1, keepdims=True) + EPS)
            return t * norm * scale
        b, t, _ = x.shape
        q = (x @ Wq.T).reshape(b, t, N_HEADS, HEAD_DIM).transpose(0, 2, 1, 3)
        k = (x @ Wk.T).reshape(b, t, N_KV_HEADS, HEAD_DIM).transpose(0, 2, 1, 3)
        v = (x @ Wv.T).reshape(b, t, N_KV_HEADS, HEAD_DIM).transpose(0, 2, 1, 3)
        q = _qknorm(q, q_scale)
        k = _qknorm(k, k_scale)
        k = jnp.repeat(k, N_REP, axis=1)
        v = jnp.repeat(v, N_REP, axis=1)
        scale = 1.0 / np.sqrt(HEAD_DIM).astype(np.float32)
        scores = jnp.einsum('bhtd,bhsd->bhts', q, k) * scale
        causal = jnp.tril(jnp.ones((t, t), dtype=bool))
        scores = jnp.where(causal, scores, jnp.finfo(scores.dtype).min)
        attn = jax.nn.softmax(scores, axis=-1)
        out = jnp.einsum('bhts,bhsd->bhtd', attn, v)
        out = out.transpose(0, 2, 1, 3).reshape(b, t, N_HEADS * HEAD_DIM)
        return out @ Wo.T

    def _L0_ffn_ref(hidden_states, gate_w, w13, w2, sw13, sw2):
        import jax, jax.numpy as jnp
        import numpy as np
        from jax import lax
        H = 256
        I = 176
        E = 16
        TOP_K = 6
        IS = 2 * I

        def _swiglu(x, w13_, w2_):
            gu = x @ w13_.T
            g, u = jnp.split(gu, 2, axis=-1)
            return jax.nn.silu(g) * u @ w2_.T
        B, S, Hd = hidden_states.shape
        x = hidden_states.reshape(-1, Hd)
        T = x.shape[0]
        scores = jax.nn.softmax(x @ gate_w.T, axis=-1)
        topk_w, topk_ids = lax.top_k(scores, TOP_K)
        topk_w = topk_w / (topk_w.sum(-1, keepdims=True) + 1e-20)
        combine = jnp.einsum('tk,tke->te', topk_w, jax.nn.one_hot(topk_ids, E, dtype=topk_w.dtype))

        def body(acc, ew):
            w13_e, w2_e, c_e = ew
            y = _swiglu(x, w13_e, w2_e)
            return (acc + c_e[:, None] * y, None)
        out, _ = lax.scan(body, jnp.zeros_like(x), (w13, w2, combine.T))
        out = out + _swiglu(x, sw13, sw2)
        return out.reshape(B, S, Hd)
    x = L0_attn_a_x
    x = x + _L0_attn_a_ref(_layernorm(x, axis=-1), L0_attn_a_block_values, L0_attn_a_cols, L0_attn_a_rows)
    x = x + _L0_ffn_ref(_layernorm(x, axis=-1), L0_ffn_gate_w, L0_ffn_w13, L0_ffn_w2, L0_ffn_sw13, L0_ffn_sw2)
    x = x + _L0_attn_b_ref(_layernorm(x, axis=-1), L0_attn_b_Wq, L0_attn_b_Wk, L0_attn_b_Wv, L0_attn_b_Wo, L0_attn_b_q_scale, L0_attn_b_k_scale)
    x = x + _L0_ffn_ref(_layernorm(x, axis=-1), L0_ffn_gate_w, L0_ffn_w13, L0_ffn_w2, L0_ffn_sw13, L0_ffn_sw2)
    return x

_drawn_inputs = setup_inputs


def setup_inputs(seed=0):
    import zlib

    import numpy as np

    out = dict(_drawn_inputs(seed))
    spreads = {'L0_attn_b_q_scale': (1.0, 0.6), 'L0_attn_b_k_scale': (1.0, 0.6)}
    factors = {'L0_attn_b_Wq': 8.0,
     'L0_attn_b_Wk': 8.0,
     'L0_attn_b_Wv': 6.618,
     'L0_attn_b_Wo': 6.627,
     'L0_ffn_gate_w': 8.0,
     'L0_ffn_w13': 8.0,
     'L0_ffn_w2': 8.0,
     'L0_ffn_sw13': 8.0,
     'L0_ffn_sw2': 8.0}
    for name, (base, spread) in spreads.items():
        noise = np.random.default_rng([zlib.crc32(name.encode()), seed]).standard_normal(out[name].shape)
        drawn = base * np.exp(spread * noise) if base else spread * noise
        out[name] = jnp.asarray(drawn.astype(out[name].dtype))
    for name, factor in factors.items():
        out[name] = (out[name] * factor).astype(out[name].dtype)
    return out
```

```python
from contextlib import ExitStack

import concourse.bass as bass
from concourse import mybir

F32 = mybir.dt.float32
F32R = mybir.dt.float32r
BF16 = mybir.dt.bfloat16
I32 = mybir.dt.int32
ALU = mybir.AluOpType
ACT = mybir.ActivationFunctionType
AX_X = mybir.AxisListType.X

P = 128
B, C, D = 2, 512, 256
NT = B * C // P
GC = C // P
KH = D // P
NBLK, BS, KS = 128, 64, 16
NCB = C // BS
NST = KS // 2
HO = BS // 2
XPITCH = 272
NE, EI, TOPK = 16, 176, 6
NRT = NE * EI // P
SI = 2 * EI
SHARED = (SI - 2 * P, P, P)
NSH = len(SHARED)
NTILE = NSH + NRT
HALF = B * C // 2
NH, NKV, HD = 16, 4, 128
REP = NH // NKV
NU = B * REP
NQ = C // P
POFF = [P * (j * (j + 1) // 2) for j in range(NQ + 1)]
TOFF = [P * sum(NQ - i for i in range(k)) for k in range(NQ + 1)]
LN_EPS = 1e-5
QK_EPS = 1e-6
MASKED = -1e30


def layernorm_engines(tag, ctx, nc, cm, pm, ps):
    sb = lambda n, s, d: ctx.enter_context(nc.sbuf_tensor(f"{tag}_{n}", s, d))
    stats, moments = sb("stats", [P, NT, 6], F32), sb("moments", [P, NT, 2], F32)
    var_eps, rstd = sb("var_eps", [P, NT], F32), sb("rstd", [P, NT], F32)
    xn = sb("xn", [P, NT, D], F32)
    xt_hi, xt_lo = sb("xt_hi", [P, KH, B * C], F32R), sb("xt_lo", [P, KH, B * C], F32R)
    s = {n: cm(f"{tag}_{n}") for n in
         ("stats_done", "moments_done", "var_ready", "rstd_ready", "xn_ready", "xt_ready", "xt_hi_done", "xt_lo_done")}
    X = pm["X"]

    HT = NT // 2

    def vector(v):
        for half in range(2):
            tiles = range(half * HT, half * HT + HT)
            for t in tiles:
                v.bn_stats(stats[:, t, :], X[:, t, :]).then_inc(s["stats_done"], 1)
            for t in tiles:
                v.wait_ge(s["stats_done"], t + 1)
                v.bn_aggr(moments[:, t, :], stats[:, t, :]).then_inc(s["moments_done"], 1)
            v.wait_ge(s["moments_done"], half * HT + HT)
            v.tensor_scalar(var_eps[:, half * HT:half * HT + HT], moments[:, half * HT:half * HT + HT, 1], LN_EPS, None,
                            ALU.add).then_inc(s["var_ready"], 1)
        for t in range(NT):
            if t % HT == 0:
                v.wait_ge(s["rstd_ready"], t // HT + 1)
            v.tensor_scalar(xn[:, t, :], X[:, t, :], moments[:, t, 0:1], rstd[:, t:t + 1],
                            ALU.subtract, ALU.mult).then_inc(s["xn_ready"], 1)
        for b in range(KH * 2):
            half, kh = divmod(b, KH)
            v.wait_ge(s["xt_hi_done"], b + 1)
            dst = slice(half * HALF, half * HALF + HALF)
            v.tensor_tensor(xt_lo[:, kh, dst], ps[b][:], xt_hi[:, kh, dst].bitcast(F32),
                            ALU.subtract).then_inc(s["xt_lo_done"], 1)

    def pool(g):
        for half in range(2):
            part = slice(half * HT, half * HT + HT)
            g.wait_ge(s["var_ready"], half + 1)
            g.tensor_tensor(rstd[:, part], var_eps[:, part], pm["minus_half"][:, part], ALU.pow)\
             .then_inc(s["rstd_ready"], 1)

    def tensor(t):
        for b in range(KH * 2):
            half, kh = divmod(b, KH)
            t.wait_ge(s["xn_ready"], HT * half + HT)
            for j in range(HT):
                m = t.transpose(ps[b][:, j * P:(j + 1) * P], xn[:, HT * half + j, kh * P:(kh + 1) * P], pm["ident"][:])
            m.then_inc(s["xt_ready"], 1)

    def scalar(a):
        for b in range(KH * 2):
            half, kh = divmod(b, KH)
            a.wait_ge(s["xt_ready"], b + 1)
            a.activation(xt_hi[:, kh, half * HALF:half * HALF + HALF], ps[b][:], ACT.Copy).then_inc(s["xt_hi_done"], 1)

    return xt_hi, xt_lo, s["xt_lo_done"], dict(vector=vector, pool=pool, tensor=tensor, scalar=scalar)


def conv_phase(nc, cm, pm, ps, ins, wconv):
    with ExitStack() as ctx:
        sb = lambda n, s, d: ctx.enter_context(nc.sbuf_tensor(f"cv_{n}", s, d))
        x_dup = sb("x_dup", [P, B, NCB, D], F32)
        xc_hi, xc_lo = sb("xc_hi", [P, NCB, B, XPITCH], F32R), sb("xc_lo", [P, NCB, B, XPITCH], F32R)
        raw = [sb(f"raw{i}", [P, HO * P], F32) for i in range(4)]
        ws_hi = [sb(f"ws_hi{i}", [P, NCB * NCB, BS], F32R) for i in range(2)]
        ws_lo = [sb(f"ws_lo{i}", [P, NCB * NCB, BS], F32R) for i in range(2)]
        colrow = sb("colrow", [P, 2], I32)
        colrow_f = sb("colrow_f", [P, 2], F32)
        pair = sb("pair", [P, 1], F32)
        high = sb("high", [P, 1], F32)
        pair_iota, pair_iota_f = sb("pair_iota", [P, NCB * NCB], I32), sb("pair_iota_f", [P, NCB * NCB], F32)
        onehot = sb("onehot", [P, NCB * NCB], F32)
        ones = sb("ones", [P, 1], F32)
        zeros = sb("zeros", [P, D * B], BF16)
        any_high = sb("any_high", [1, 1], I32)
        stats, moments = sb("stats", [P, B * NCB, 6], F32), sb("moments", [P, B * NCB, 2], F32)
        var_eps, rstd = sb("var_eps", [P, B * NCB], F32), sb("rstd", [P, B * NCB], F32)
        s = {n: cm(f"cv_{n}") for n in (
            "x_in", "xd_in", "cr_in", "iota_done", "const_done", "cr_conv", "pair_part", "pair_ready", "onehot_ready",
            "count_ready", "flag_ready", "stats_done", "moments_done", "var_ready", "rstd_ready", "xn_ready",
            "pads_ready", "xc_hi_done", "xc_lo_done", "summed", "ws_hi_done", "ws_lo_done", "ws_free", "conv_done",
            "x_added")}
        raw_in = [cm(f"cv_raw_in{i}") for i in range(4)]
        X = pm["X"]
        block = ctx.enter_context(nc.Block())
        BANKS = 4
        OB = HO // BANKS

        @block.sync
        def _(sp):
            sp.dma_start(colrow[:, 0:1], ins["cols"].rearrange("(n a) -> n a", a=1)).then_inc(s["cr_in"], 16)
            sp.dma_start(colrow[:, 1:2], ins["rows"].rearrange("(n a) -> n a", a=1)).then_inc(s["cr_in"], 16)
            for b in range(B):
                for k in range(2):
                    sp.dma_start(x_dup[k * BS:(k + 1) * BS, b, :, :],
                                 ins["x"][b].rearrange("(c i) t -> i c t", i=BS)).then_inc(s["xd_in"], 16)
            for h in range(4):
                sp.dma_start(raw[h][:], wconv[h]).then_inc(raw_in[h], 16)
            sp.dma_start(X[:], ins["x"].rearrange("b (g p) t -> p (b g) t", p=P)).then_inc(s["x_in"], 16)
            with sp.Fori(1, NST // 2) as i:
                for h in range(4):
                    sp.wait_ge(s["summed"], i * 4 * BANKS + (h - 4 + 1) * BANKS)
                    sp.dma_start(raw[h][:], wconv[bass.ds(i * 4 + h, 1)].rearrange("a n f -> (a n) f"))\
                      .then_inc(raw_in[h], 16)

        @block.scalar
        def _(a):

            def round_input(b, k):
                a.wait_ge(s["pads_ready"], 2)
                a.wait_ge(s["xn_ready"], NCB * (b + 1))
                lo = KS - 1 - k
                a.activation(xc_hi[k * BS:(k + 1) * BS, :, b, lo:lo + D], x_dup[k * BS:(k + 1) * BS, b, :, :],
                             ACT.Copy).then_inc(s["xc_hi_done"], 1)

            def round_stage(st, slot):
                a.wait_ge(s["ws_free"], st + 1)
                for q in range(2 * BANKS):
                    a.wait_ge(s["summed"], st * 2 * BANKS + q + 1)
                    h, bk = divmod(q, BANKS)
                    o0 = h * HO + bk * OB
                    a.activation(ws_hi[slot][:, :, o0:o0 + OB].rearrange("p c o -> p o c"),
                                 ps[bk][:].rearrange("p (o c) -> p o c", o=OB), ACT.Copy)\
                     .then_inc(s["ws_hi_done"], 1)

            round_stage(0, 0)
            for b in range(B):
                for k in range(2):
                    round_input(b, k)
            round_stage(1, 1)
            with a.Fori(1, NST // 2) as i:
                for u in range(2):
                    round_stage(i * 2 + u, u)

        @block.gpsimd
        def _(g):
            g.iota(pair_iota[:], pattern=[[1, NCB * NCB]], base=0, channel_multiplier=0).then_inc(s["iota_done"], 1)
            g.memset(ones[:], 1.0).then_inc(s["const_done"], 1)
            g.memset(zeros[:], 0.0).then_inc(s["const_done"], 1)
            g.memset(pm["minus_half"][:], -0.5).then_inc(s["const_done"], 1)
            g.memset(pm["ident"][:], 0.0).then_inc(s["const_done"], 1)
            g.memset(pm["ident_b"][:], 0.0).then_inc(s["const_done"], 1)
            g.memset(pm["causal"][:], 0.0).then_inc(s["const_done"], 1)
            for x in (xc_hi, xc_lo):
                g.memset(x[:, :, :, 0:KS - 1].bitcast(F32), 0.0).then_inc(s["pads_ready"], 1)
            g.wait_ge(s["const_done"], 6)
            for m in (pm["ident"], pm["ident_b"]):
                g.affine_select(out=m[:], in_=m[:], compare_op=ALU.not_equal, fill=1.0, base=0,
                                pattern=[[-1, P]], channel_multiplier=1)
            g.affine_select(out=pm["causal"][:], in_=pm["causal"][:], compare_op=ALU.is_ge, fill=MASKED, base=0,
                            pattern=[[-1, P]], channel_multiplier=1)
            g.wait_ge(s["var_ready"], 1)
            g.tensor_tensor(rstd[:], var_eps[:], pm["minus_half"][:, 0:B * NCB], ALU.pow).then_inc(s["rstd_ready"], 1)

        @block.vector
        def _(v):
            v.wait_ge(s["cr_in"], 32)
            v.tensor_copy(colrow_f[:], colrow[:]).then_inc(s["cr_conv"], 1)
            v.wait_ge(s["iota_done"], 1)
            v.tensor_copy(pair_iota_f[:], pair_iota[:]).then_inc(s["cr_conv"], 1)
            v.wait_ge(s["cr_conv"], 2)
            v.scalar_tensor_tensor(out=pair[:], in0=colrow_f[:, 0:1], scalar=float(NCB), in1=colrow_f[:, 1:2],
                                   op0=ALU.mult, op1=ALU.add).then_inc(s["pair_part"], 1)
            v.tensor_tensor(high[:], colrow_f[:, 0:1], colrow_f[:, 1:2], ALU.max).then_inc(s["pair_part"], 1)
            v.wait_ge(s["pair_part"], 2)
            v.tensor_scalar(onehot[:], pair_iota_f[:], pair[:, 0:1], None, ALU.is_equal).then_inc(s["onehot_ready"], 1)
            v.tensor_scalar(high[:], high[:], float(NCB // 2), None, ALU.is_ge).then_inc(s["pair_ready"], 1)
            v.wait_ge(s["count_ready"], 1)
            v.tensor_scalar(any_high[:], ps[4][0:1, 0:1], 0.5, None, ALU.is_ge).then_inc(s["flag_ready"], 1)

            v.wait_ge(s["xd_in"], 64)
            for n in range(B * NCB):
                b, c = divmod(n, NCB)
                v.bn_stats(stats[:, n, :], x_dup[:, b, c, :]).then_inc(s["stats_done"], 1)
            for n in range(B * NCB):
                v.wait_ge(s["stats_done"], n + 1)
                v.bn_aggr(moments[:, n, :], stats[:, n, :]).then_inc(s["moments_done"], 1)
            v.wait_ge(s["moments_done"], B * NCB)
            v.tensor_scalar(var_eps[:], moments[:, :, 1], LN_EPS, None, ALU.add).then_inc(s["var_ready"], 1)
            v.wait_ge(s["rstd_ready"], 1)
            for n in range(B * NCB):
                b, c = divmod(n, NCB)
                v.tensor_scalar(x_dup[:, b, c, :], x_dup[:, b, c, :], moments[:, n, 0:1], rstd[:, n:n + 1],
                                ALU.subtract, ALU.mult).then_inc(s["xn_ready"], 1)

            def low_stage(st, slot):
                for q in range(2 * BANKS):
                    v.wait_ge(s["ws_hi_done"], st * 2 * BANKS + q + 1)
                    h, bk = divmod(q, BANKS)
                    o0 = h * HO + bk * OB
                    v.tensor_tensor(ws_lo[slot][:, :, o0:o0 + OB].rearrange("p c o -> p o c"),
                                    ps[bk][:].rearrange("p (o c) -> p o c", o=OB),
                                    ws_hi[slot][:, :, o0:o0 + OB].bitcast(F32).rearrange("p c o -> p o c"),
                                    ALU.subtract).then_inc(s["ws_lo_done"], 1)

            low_stage(0, 0)
            for n in range(2 * B):
                b, k = divmod(n, 2)
                lo = KS - 1 - k
                v.wait_ge(s["xc_hi_done"], n + 1)
                v.tensor_tensor(xc_lo[k * BS:(k + 1) * BS, :, b, lo:lo + D], x_dup[k * BS:(k + 1) * BS, b, :, :],
                                xc_hi[k * BS:(k + 1) * BS, :, b, lo:lo + D].bitcast(F32),
                                ALU.subtract).then_inc(s["xc_lo_done"], 1)
            low_stage(1, 1)
            with v.Fori(1, NST // 2) as i:
                for u in range(2):
                    low_stage(i * 2 + u, u)
            v.wait_ge(s["x_in"], 16)
            for r in range(GC):
                v.wait_ge(s["conv_done"], r + 1)
                dst = X[:].rearrange("p (b g) t -> p g b t", b=B)[:, r]
                v.tensor_tensor(dst, dst, ps[4 + r][:].rearrange("p (b t) -> p b t", b=B), ALU.add)\
                 .then_inc(s["x_added"], 1)

        @block.tensor
        def _(t):
            t.wait_ge(s["pair_ready"], 1)
            t.wait_ge(s["const_done"], 2)
            t.matmul(ps[4][0:1, 0:1], high[:, 0:1], ones[:, 0:1], start=True, stop=True).then_inc(s["count_ready"], 1)
            t.wait_ge(s["flag_ready"], 1)
            flag = t.value_load(any_high[0:1, 0:1], min_val=0, max_val=1)
            t.sem_inc(s["ws_free"], 2)
            for r in range(GC):
                t.matmul(ps[4 + r][:], zeros[:, 0:P], zeros[:], start=True, stop=False)

            def sum_blocks(st, slot, use, first):
                for h in range(2):
                    t.wait_ge(raw_in[2 * slot + h], 16 * use)
                    for bk in range(BANKS):
                        if not (first and h == 0):
                            t.wait_ge(s["ws_lo_done"], st * 2 * BANKS + (h - 1) * BANKS + bk + 1)
                        for o in range(OB):
                            w0 = (bk * OB + o) * P
                            m = t.matmul(ps[bk][:, o * NCB * NCB:(o + 1) * NCB * NCB],
                                         raw[2 * slot + h][:, w0:w0 + P], onehot[:], start=True, stop=True)
                        m.then_inc(s["summed"], 1)

            def products(slot, c, r, tap):
                w = c * NCB + 2 * r
                hi, lo = (x[:, c, :, bass.ds(tap, D)] for x in (xc_hi, xc_lo))
                w_hi, w_lo = (x[slot][:, w:w + 2, :].rearrange("p c o -> p (c o)") for x in (ws_hi, ws_lo))
                for lhs, rhs in ((w_hi, hi), (w_lo, hi), (w_hi, lo)):
                    t.matmul(ps[4 + r][:], lhs, rhs, start=False, stop=False)

            def convolve(st, slot):
                t.wait_ge(s["ws_lo_done"], (st + 1) * 2 * BANKS)
                with t.If(flag != 0):
                    for c in range(NCB):
                        for r in range(GC):
                            if c >= NCB // 2 or r >= GC // 2:
                                products(slot, c, r, st * 2)
                for c in range(NCB // 2):
                    for r in range(GC // 2):
                        products(slot, c, r, st * 2)

            t.wait_ge(s["onehot_ready"], 1)
            sum_blocks(0, 0, 1, True)
            sum_blocks(1, 1, 1, False)
            t.wait_ge(s["xc_lo_done"], 2 * B)
            with t.Fori(0, NST // 2 - 1) as i:
                for u in range(2):
                    convolve(i * 2 + u, u)
                    t.sem_inc(s["ws_free"], 1)
                    sum_blocks(i * 2 + u + 2, u, i + 2, False)
            for u in range(2):
                convolve(NST - 2 + u, u)
            for r in range(GC):
                t.matmul(ps[4 + r][:], zeros[:, 0:P], zeros[:], start=False,
                         stop=True).then_inc(s["conv_done"], 1)


def ffn_phase(nc, cm, pm, ps, ins, tag, out):
    with ExitStack() as ctx:
        sb = lambda n, s, d: ctx.enter_context(nc.sbuf_tensor(f"{tag}_{n}", s, d))
        xt_hi, xt_lo, xt_done, ln = layernorm_engines(tag, ctx, nc, cm, pm, ps)
        WC = KH * 2 * P
        wraw = [sb(f"wraw{i}", [P, WC + D], F32) for i in range(2)]
        w_hi = [sb(f"w_hi{i}", [P, WC + D], F32R) for i in range(2)]
        w_lo = [sb(f"w_lo{i}", [P, WC + D], F32R) for i in range(2)]
        gw, gw_hi, gw_lo = sb("gw", [P, KH * NE], F32), sb("gw_hi", [P, KH, NE], F32R), sb("gw_lo", [P, KH, NE], F32R)
        act = [sb(f"act{i}", [P, HALF], F32) for i in range(2)]
        scaled = [sb(f"scaled{i}", [P, HALF], F32) for i in range(2)]
        h_f = [sb(f"h{i}", [P, HALF], F32) for i in range(2)]
        h_hi = [sb(f"h_hi{i}", [P, HALF], F32R) for i in range(4)]
        h_lo = [sb(f"h_lo{i}", [P, HALF], F32R) for i in range(4)]
        gate_rows = sb("gate_rows", [P, B * C], F32)
        lmax, lsh, lexp = sb("lmax", [P, NT], F32), sb("lsh", [P, NT, NE], F32), sb("lexp", [P, NT, NE], F32)
        lsum, lrec = sb("lsum", [P, NT], F32), sb("lrec", [P, NT], F32)
        NEP = NE + 2
        prob, rest = sb("prob", [P, NT, NEP], F32), sb("rest", [P, NT, NEP], F32)
        top8 = sb("top8", [P, NT, 8], F32)
        sel, ssum, srec = sb("sel", [P, NT, NE], F32), sb("ssum", [P, NT], F32), sb("srec", [P, NT], F32)
        comb = sb("comb", [P, NT, P // NE, NE], F32)
        s = {n: cm(f"{tag}_{n}") for n in (
            "gw_in", "gw_hi_done", "gw_lo_done", "w13_hi_done", "w13_lo_done", "w2_hi_done", "w2_lo_done",
            "logits_ready", "gate_v", "exp_done", "comb_ready", "gate_t", "gate_rows_ready", "gu_ready", "act_done",
            "scaled_done", "h_ready", "h_hi_done", "h_lo_done", "down_done", "y_ready", "x_added", "out_done")}
        w_in = [cm(f"{tag}_w_in{i}") for i in range(2)]
        X = pm["X"]
        pg, pu, py = ps[0:4:2], ps[1:4:2], ps[4:8]
        block = ctx.enter_context(nc.Block())

        @block.sync
        def _(sp):
            sp.dma_start(gw[:], ins["gate_w"]).then_inc(s["gw_in"], 16)

            def load(m, slot, w13, w2, rows):
                sp.dma_start(wraw[slot][:, 0:KH * 2 * rows], w13).then_inc(w_in[slot], 16)
                sp.dma_start(wraw[slot][0:rows, WC:WC + D], w2).then_inc(w_in[slot], 16)

            r0 = 0
            for m, rows in enumerate(SHARED):
                if m >= 2:
                    sp.wait_ge(s["w2_lo_done"], m - 1)
                load(m, m % 2, ins[f"sw13_{m}"], ins["sw2"][r0:r0 + rows, :], rows)
                r0 += rows
            with sp.Fori(0, NRT // 2) as i:
                for u in range(2):
                    sp.wait_ge(s["w2_lo_done"], i * 2 + (NSH + u - 1))
                    load(None, (NSH + u) % 2, ins["w13"][bass.ds(i * 2 + u, 1)].rearrange("a p f -> (a p) f"),
                         ins["w2"][bass.ds(i * 2 + u, 1)].rearrange("a p f -> (a p) f"), P)
            if out is not None:
                for q in range(4):
                    sp.wait_ge(s["x_added"], q + 1)
                    b, g0 = divmod(2 * q, GC)
                    sp.dma_start(out[b].rearrange("(g p) t -> p g t", p=P)[:, g0:g0 + 2, :],
                                 X[:, 2 * q:2 * q + 2, :]).then_inc(s["out_done"], 16)
                sp.wait_ge(s["out_done"], 64)

        def weight_views(slot, rows):
            v13 = [x[slot][:, 0:KH * 2 * rows].rearrange("p (k g f) -> p k g f", k=KH, g=2) for x in (w_hi, w_lo)]
            v2 = [x[slot][0:rows, WC:WC + D] for x in (w_hi, w_lo)]
            return v13, v2

        @block.scalar
        def _(a):
            a.wait_ge(s["gw_in"], 16)
            a.activation(gw_hi[:].rearrange("p k e -> p (k e)"), gw[:], ACT.Copy).then_inc(s["gw_hi_done"], 1)

            def round_w13(m, slot, use, rows, reuse):
                a.wait_ge(w_in[slot], 32 * use)
                if reuse:
                    a.wait_ge(s["gu_ready"], 2 * m - 2)
                a.activation(w_hi[slot][:, 0:KH * 2 * rows], wraw[slot][:, 0:KH * 2 * rows], ACT.Copy)\
                 .then_inc(s["w13_hi_done"], 1)

            def round_w2(m, slot, rows, reuse):
                if reuse:
                    a.wait_ge(s["down_done"], 2 * m - 2)
                a.activation(w_hi[slot][0:rows, WC:WC + D], wraw[slot][0:rows, WC:WC + D], ACT.Copy)\
                 .then_inc(s["w2_hi_done"], 1)

            def silu(n, half, rows, reuse):
                a.wait_ge(s["gu_ready"], n + 1)
                if reuse:
                    a.wait_ge(s["h_ready"], n - 1)
                a.activation(act[half][0:rows, :], pg[half][0:rows, :], ACT.Silu).then_inc(s["act_done"], 1)

            def round_h(n, half, slot, rows, reuse):
                a.wait_ge(s["h_ready"], n + 1)
                if reuse:
                    a.wait_ge(s["down_done"], n - 3)
                a.activation(h_hi[slot][0:rows, :], h_f[half][0:rows, :], ACT.Copy).then_inc(s["h_hi_done"], 1)

            def tile(m, par, u0, next_use, rows, next_rows):
                silu(2 * m, 0, rows, not isinstance(m, int) or m >= 1)
                if next_use is not None:
                    round_w13(m + 1, 1 - par, next_use, next_rows, not isinstance(m, int) or m >= 1)
                round_h(2 * m, 0, u0, rows, not isinstance(m, int) or m >= 2)
                round_w2(m, par, rows, not isinstance(m, int) or m >= 2)
                silu(2 * m + 1, 1, rows, not isinstance(m, int) or m >= 1)
                round_h(2 * m + 1, 1, u0 + 1, rows, not isinstance(m, int) or m >= 2)

            rows_of = list(SHARED) + [P] * NRT
            round_w13(0, 0, 1, rows_of[0], False)
            ln["scalar"](a)
            a.wait_ge(s["gate_v"], 2)
            a.activation(lexp[:], lsh[:], ACT.Exp).then_inc(s["exp_done"], 1)
            for m in range(NSH):
                tile(m, m % 2, 2 * (m % 2), (m + 1) // 2 + 1, rows_of[m], rows_of[m + 1])
            with a.Fori(0, NRT // 2 - 1) as i:
                for u in range(2):
                    par = (NSH + u) % 2
                    tile(i * 2 + (NSH + u), par, 2 * par, i + ((NSH + u + 1) // 2 + 1), P, P)
            for m in range(NTILE - 2, NTILE):
                tile(m, m % 2, 2 * (m % 2), (m + 1) // 2 + 1 if m + 1 < NTILE else None, P, P)

        @block.gpsimd
        def _(g):
            g.memset(prob[:], -1.0).then_inc(s["gate_t"], 1)

            def low_w13(m, slot, rows):
                g.wait_ge(s["w13_hi_done"], m + 1)
                n = KH * 2 * rows
                g.tensor_tensor(w_lo[slot][:, 0:n], wraw[slot][:, 0:n], w_hi[slot][:, 0:n].bitcast(F32),
                                ALU.subtract).then_inc(s["w13_lo_done"], 1)

            def low_w2(m, slot, rows):
                g.wait_ge(s["w2_hi_done"], m + 1)
                g.tensor_tensor(w_lo[slot][0:rows, WC:WC + D], wraw[slot][0:rows, WC:WC + D],
                                w_hi[slot][0:rows, WC:WC + D].bitcast(F32), ALU.subtract)\
                 .then_inc(s["w2_lo_done"], 1)

            def scale(n, half):
                g.wait_ge(s["act_done"], n + 1)
                g.tensor_tensor(scaled[half][:], act[half][:], gate_rows[:, half * HALF:(half + 1) * HALF],
                                ALU.mult).then_inc(s["scaled_done"], 1)

            def tile(m, par, routed, has_next, rows, next_rows):
                if routed:
                    scale(2 * m, 0)
                if has_next:
                    low_w13(m + 1, 1 - par, next_rows)
                low_w2(m, par, rows)
                if routed:
                    scale(2 * m + 1, 1)

            rows_of = list(SHARED) + [P] * NRT
            low_w13(0, 0, rows_of[0])
            ln["pool"](g)
            for m in range(NSH):
                tile(m, m % 2, False, True, rows_of[m], rows_of[m + 1])
            g.wait_ge(s["gate_rows_ready"], 2)
            with g.Fori(0, NRT // 2 - 1) as i:
                for u in range(2):
                    tile(i * 2 + (NSH + u), (NSH + u) % 2, True, True, P, P)
            for m in range(NTILE - 2, NTILE):
                tile(m, m % 2, True, m + 1 < NTILE, P, P)

        @block.vector
        def _(v):
            v.wait_ge(s["gw_hi_done"], 1)
            v.tensor_tensor(gw_lo[:].rearrange("p k e -> p (k e)"), gw[:],
                            gw_hi[:].rearrange("p k e -> p (k e)").bitcast(F32), ALU.subtract)\
             .then_inc(s["gw_lo_done"], 1)
            ln["vector"](v)
            step = s["gate_v"]

            def spread(x, n=NE):
                return x[:].unsqueeze(2).to_broadcast([P, NT, n])

            def gate_shift():
                v.wait_ge(s["logits_ready"], 1)
                logits = py[3][:, 0:NT * NE].rearrange("p (t e) -> p t e", t=NT)
                v.tensor_reduce(lmax[:], logits, AX_X, ALU.max).then_inc(step, 1)
                v.wait_ge(step, 1)
                v.tensor_tensor(lsh[:], logits, spread(lmax), ALU.subtract).then_inc(step, 1)

            def gate_softmax():
                v.wait_ge(s["exp_done"], 1)
                v.tensor_reduce(lsum[:], lexp[:], AX_X, ALU.add).then_inc(step, 1)
                v.wait_ge(step, 3)
                v.reciprocal(lrec[:], lsum[:]).then_inc(step, 1)
                v.wait_ge(step, 4)
                v.wait_ge(s["gate_t"], 1)
                v.tensor_tensor(prob[:, :, 0:NE], lexp[:], spread(lrec), ALU.mult).then_inc(step, 1)
                v.wait_ge(step, 5)
                for t in range(NT):
                    v.max(top8[:, t, :], prob[:, t, 0:NE]).then_inc(step, 1)

            def gate_select():
                v.wait_ge(step, 5 + NT)
                v.memset(top8[:, :, TOPK:8], -1.0).then_inc(step, 1)
                v.wait_ge(step, 6 + NT)
                for t in range(NT):
                    v.match_replace(out=rest[:, t, :], in_to_replace=top8[:, t, :], in_values=prob[:, t, :],
                                    imm_value=0.0).then_inc(step, 1)
                v.wait_ge(step, 6 + 2 * NT)
                v.tensor_tensor(sel[:], prob[:, :, 0:NE], rest[:, :, 0:NE], ALU.subtract).then_inc(step, 1)

            def gate_weights():
                v.wait_ge(step, 7 + 2 * NT)
                v.tensor_reduce(ssum[:], sel[:], AX_X, ALU.add).then_inc(step, 1)
                v.wait_ge(step, 8 + 2 * NT)
                v.tensor_scalar(ssum[:], ssum[:], 1e-20, None, ALU.add).then_inc(step, 1)
                v.wait_ge(step, 9 + 2 * NT)
                v.reciprocal(srec[:], ssum[:]).then_inc(step, 1)
                v.wait_ge(step, 10 + 2 * NT)
                v.tensor_tensor(sel[:], sel[:], spread(srec), ALU.mult).then_inc(step, 1)
                v.wait_ge(step, 11 + 2 * NT)
                v.tensor_copy(comb[:], sel[:].unsqueeze(2).to_broadcast([P, NT, P // NE, NE]))\
                 .then_inc(s["comb_ready"], 1)

            def unit(n, half, slot, rows, routed):
                if routed:
                    v.wait_ge(s["scaled_done"], n - (2 * NSH - 1))
                    src = scaled
                else:
                    v.wait_ge(s["act_done"], n + 1)
                    src = act
                if not isinstance(n, int) or n >= 2:
                    v.wait_ge(s["h_hi_done"], n - 1)
                    v.wait_ge(s["h_lo_done"], n - 1)
                v.tensor_tensor(h_f[half][0:rows, :], src[half][0:rows, :], pu[half][0:rows, :], ALU.mult)\
                 .then_inc(s["h_ready"], 1)
                v.wait_ge(s["h_hi_done"], n + 1)
                v.wait_ge(s["h_ready"], n + 1)
                v.tensor_tensor(h_lo[slot][0:rows, :], h_f[half][0:rows, :], h_hi[slot][0:rows, :].bitcast(F32),
                                ALU.subtract).then_inc(s["h_lo_done"], 1)

            gate_shift()
            gate_softmax()
            unit(0, 0, 0, SHARED[0], False)
            gate_select()
            unit(1, 1, 1, SHARED[0], False)
            gate_weights()
            for n in range(2, 2 * NSH):
                unit(n, n % 2, n % 4, SHARED[n // 2], False)
            for half in range(2):
                v.wait_ge(s["gate_t"], half + 2)
                v.tensor_copy(gate_rows[:, half * HALF:(half + 1) * HALF], (pg, pu)[half][0][:])\
                 .then_inc(s["gate_rows_ready"], 1)
            with v.Fori(0, NRT // 2) as i:
                for k in range(4):
                    n = 2 * NSH + k
                    unit(i * 4 + n, n % 2, n % 4, P, True)
            for q in range(4):
                v.wait_ge(s["y_ready"], q + 1)
                dst = X[:, 2 * q:2 * q + 2, :].rearrange("p t d -> p (t d)")
                v.tensor_tensor(dst, dst, py[q][:], ALU.add).then_inc(s["x_added"], 1)

        @block.tensor
        def _(t):
            ln["tensor"](t)

            def gate_logits():
                t.wait_ge(s["gw_lo_done"], 1)
                t.wait_ge(xt_done, 2 * KH)
                for tt in range(NT):
                    tok = slice(tt * P, (tt + 1) * P)
                    steps = [(x[:, k, tok], w[:, k, :]) for k in range(KH)
                             for x, w in ((xt_hi, gw_hi), (xt_lo, gw_hi), (xt_hi, gw_lo))]
                    for q, (x, w) in enumerate(steps):
                        m = t.matmul(py[3][:, tt * NE:(tt + 1) * NE], x, w, start=q == 0, stop=q == len(steps) - 1)
                m.then_inc(s["logits_ready"], 1)

            def gate_up(n, half, m, slot, rows, reuse):
                if half == 0:
                    t.wait_ge(s["w13_lo_done"], m + 1)
                if reuse:
                    t.wait_ge(s["h_ready"], n - 1)
                (vhi, vlo), _ = weight_views(slot, rows)
                tok = slice(half * HALF, (half + 1) * HALF)
                for gu, bank in enumerate((pg, pu)):
                    steps = [(w[:, k, gu, :], x[:, k, tok]) for k in range(KH)
                             for w, x in ((vhi, xt_hi), (vlo, xt_hi), (vhi, xt_lo))]
                    for q, (w, x) in enumerate(steps):
                        mm = t.matmul(bank[half][0:rows, :], w, x, start=q == 0, stop=q == len(steps) - 1)
                mm.then_inc(s["gu_ready"], 1)

            def down(n, half, m, slot, hslot, rows, first, last):
                if half == 0:
                    t.wait_ge(s["w2_lo_done"], m + 1)
                t.wait_ge(s["h_lo_done"], n + 1)
                _, (vhi, vlo) = weight_views(slot, rows)
                for j in range(4):
                    tok = slice(j * P, (j + 1) * P)
                    bank = py[2 * half + j // 2][:, (j % 2) * D:(j % 2 + 1) * D]
                    trio = ((h_hi, vhi), (h_lo, vhi), (h_hi, vlo))
                    for q, (h, w) in enumerate(trio):
                        mm = t.matmul(bank, h[hslot][0:rows, tok], w, start=first and q == 0 and j % 2 == 0,
                                      stop=last and q == 2, skip_group_check=True)
                    if last and j % 2:
                        mm.then_inc(s["y_ready"], 1)
                if not last:
                    mm.then_inc(s["down_done"], 1)

            for n in range(2 * NSH):
                if n < 2:
                    t.wait_ge(xt_done, KH * (n + 1))
                gate_up(n, n % 2, n // 2, (n // 2) % 2, SHARED[n // 2], n >= 2)
                if n == 0:
                    gate_logits()
                if n == 1:
                    t.wait_ge(s["gate_v"], 2)
                if n >= 2:
                    down(n - 2, n % 2, n // 2 - 1, (n // 2 - 1) % 2, (n - 2) % 4, SHARED[n // 2 - 1], n < 4, False)
            t.wait_ge(s["comb_ready"], 1)
            t.wait_ge(s["h_ready"], 2 * NSH - 1)
            for half, bank in enumerate((pg[0], pu[0])):
                for j in range(4):
                    mm = t.transpose(bank[:, j * P:(j + 1) * P],
                                     comb[:, 4 * half + j, :, :].rearrange("p r e -> p (r e)"), pm["ident"][:])
                mm.then_inc(s["gate_t"], 1)
            t.wait_ge(s["gate_rows_ready"], 2)
            with t.Fori(0, NRT // 2) as i:
                for k in range(4):
                    n, d = 2 * NSH + k, 2 * NSH + k - 2
                    gate_up(i * 4 + n, n % 2, i * 2 + n // 2, (n // 2) % 2, P, True)
                    down(i * 4 + d, d % 2, i * 2 + d // 2, (d // 2) % 2, d % 4, P, False, False)
            for n in range(2 * NTILE - 2, 2 * NTILE):
                down(n, n % 2, n // 2, (n // 2) % 2, n % 4, P, False, True)


def attention_phase(nc, cm, pm, ps, ins):
    with ExitStack() as ctx:
        sb = lambda n, s, d: ctx.enter_context(nc.sbuf_tensor(f"at_{n}", s, d))
        xt_hi, xt_lo, xt_done, ln = layernorm_engines("at", ctx, nc, cm, pm, ps)
        GW = (REP + 2) * HD
        wraw = sb("wraw", [P, KH * GW], F32)
        wq_hi, wq_lo = sb("wq_hi", [P, KH, REP * HD], F32R), sb("wq_lo", [P, KH, REP * HD], F32R)
        wkv_hi, wkv_lo = sb("wkv_hi", [P, KH, 2 * HD], F32R), sb("wkv_lo", [P, KH, 2 * HD], F32R)
        oraw = sb("oraw", [P, REP * D], F32)
        wo_hi, wo_lo = sb("wo_hi", [P, REP, D], F32R), sb("wo_lo", [P, REP, D], F32R)
        scales, kq_scale = sb("scales", [P, 2], F32), sb("kq_scale", [P, 1], F32)
        ones = sb("ones", [P, 1], F32)
        ksum, ksum_eps, krs = sb("ksum", [P, NT], F32), sb("ksum_eps", [P, NT], F32), sb("krs", [P, NT], F32)
        ksq = sb("ksq", [P, NT, HD], F32)
        kn = sb("kn", [P, NT, HD], F32)
        kt_hi, kt_lo = sb("kt_hi", [P, B, C], F32R), sb("kt_lo", [P, B, C], F32R)
        v_hi, v_lo = sb("v_hi", [P, NT, HD], F32R), sb("v_lo", [P, NT, HD], F32R)
        qt_hi, qt_lo = sb("qt_hi", [P, 2, C], F32R), sb("qt_lo", [P, 2, C], F32R)
        qsq = sb("qsq", [P, 2, C], F32)
        qsum, qrs = sb("qsum", [P, 2, NQ], F32), sb("qrs", [P, 2, NQ], F32)
        smax, sbias = sb("smax", [P, 2, NQ], F32), sb("sbias", [P, 2, NQ], F32)
        rsum, rrec = sb("rsum", [P, 2, NQ], F32), sb("rrec", [P, 2, NQ], F32)
        prob = sb("prob", [P, 2, POFF[NQ]], F32)
        pt_hi, pt_lo = sb("pt_hi", [P, 2, TOFF[NQ]], F32R), sb("pt_lo", [P, 2, TOFF[NQ]], F32R)
        ot_hi, ot_lo = sb("ot_hi", [P, NU, C], F32R), sb("ot_lo", [P, NU, C], F32R)
        s = {n: cm(f"at_{n}") for n in (
            "scale_in", "scale_ready", "ones_ready", "w_in", "o_in", "acc_free", "wq_hi_done", "wq_lo_done", "wkv_hi_done", "wkv_lo_done",
            "wo_hi_done", "wo_lo_done", "kv_ready", "ksum_done", "ksum_eps_done", "krs_done", "kn_done", "kt_ready",
            "kt_hi_done", "kt_lo_done", "v_hi_done", "v_lo_done", "q_ready", "qsq_done", "qt_hi_done", "qt_lo_done",
            "qsum_ready", "qsum_done", "qrs_done", "s_ready", "max_done", "bias_done", "exp_done", "rec_done",
            "prob_done", "pt_ready", "pt_hi_done", "pt_lo_done", "o_ready", "ot_hi_done", "ot_lo_done", "y_ready")}
        X = pm["X"]
        raw_q = wraw[:].rearrange("p (k f) -> p k f", k=KH)[:, :, 0:REP * HD]
        raw_kv = wraw[:].rearrange("p (k f) -> p k f", k=KH)[:, :, REP * HD:GW]
        S_BANK = ((0, 0), (0, P), (1, 0), (2, 0))
        QSUM_COL = 3 * P
        Q_BANK, T_BANK, O_BANK, Y_BANK = 3, 4, 7, 4
        T_CUTS = (0, TOFF[1], TOFF[2], TOFF[4])
        block = ctx.enter_context(nc.Block())

        def steps_of(k):
            return (k if k < NU else None, k - 1 if 1 <= k <= NU else None, k - 2 if 2 <= k <= NU else None,
                    k + 1 if k + 1 < NU else None)

        @block.sync
        def _(sp):
            sp.dma_start(scales[:, 0:1], ins["q_scale"].rearrange("(d a) -> d a", a=1)).then_inc(s["scale_in"], 16)
            sp.dma_start(scales[:, 1:2], ins["k_scale"].rearrange("(d a) -> d a", a=1)).then_inc(s["scale_in"], 16)
            sp.dma_start(wraw[:], ins["wqkv"][0]).then_inc(s["w_in"], 16)
            sp.dma_start(oraw[:], ins["wo"][0]).then_inc(s["o_in"], 16)
            with sp.Fori(1, NKV) as g:
                sp.wait_ge(s["wq_lo_done"], g)
                sp.dma_start(wraw[:], ins["wqkv"][bass.ds(g, 1)].rearrange("a p f -> (a p) f")).then_inc(s["w_in"], 16)
                sp.wait_ge(s["wo_lo_done"], g)
                sp.dma_start(oraw[:], ins["wo"][bass.ds(g, 1)].rearrange("a p f -> (a p) f")).then_inc(s["o_in"], 16)

        @block.scalar
        def _(a):
            def round_kv_weights(g):
                a.wait_ge(s["w_in"], g * 16 + 16)
                a.activation(wkv_hi[:], raw_kv, ACT.Copy).then_inc(s["wkv_hi_done"], 1)

            def round_q_weights(g):
                a.activation(wq_hi[:], raw_q, ACT.Copy).then_inc(s["wq_hi_done"], 1)

            def square_keys(g, banks):
                for q in banks:
                    a.wait_ge(s["kv_ready"], g * 4 + (q + 1))
                    kv = ps[q][:].rearrange("p (t f) -> p t f", t=2)
                    for j in range(2):
                        tt = 2 * q + j
                        a.activation(ksq[:, tt, :], kv[:, j, 0:HD], ACT.Square, accum_out=ksum[:, tt:tt + 1])\
                         .then_inc(s["ksum_done"], 1)

            def round_values(g):
                for q in range(4):
                    kv = ps[q][:].rearrange("p (t f) -> p t f", t=2)
                    a.activation(v_hi[:, 2 * q:2 * q + 2, :], kv[:, :, HD:2 * HD], ACT.Copy).then_inc(s["v_hi_done"], 1)

            def query(g, u):
                a.wait_ge(s["q_ready"], g * NU + (u + 1))
                a.activation(qsq[:, u % 2, :], ps[Q_BANK][:], ACT.Square).then_inc(s["qsq_done"], 1)
                a.activation(qt_hi[:, u % 2, :], ps[Q_BANK][:], ACT.Copy).then_inc(s["qt_hi_done"], 1)

            def open_group(g):
                for b in range(B):
                    a.wait_ge(s["kt_ready"], g * B + (b + 1))
                    a.activation(kt_hi[:, b, :], ps[b][:], ACT.Copy, scale=kq_scale[:, 0:1]).then_inc(s["kt_hi_done"], 1)
                query(g, 0)

            def output(g, u):
                a.wait_ge(s["o_ready"], g * NU + (u + 1))
                a.activation(ot_hi[:, u, :], ps[O_BANK][:], ACT.Copy).then_inc(s["ot_hi_done"], 1)

            def group(g, last):
                for k in range(NU + 1):
                    score, turn, value, ahead = steps_of(k)
                    if score is not None:
                        sl = score % 2
                        for j in reversed(range(NQ)):
                            if j % 2:
                                a.wait_ge(s["bias_done"], g * 2 * NU + (2 * score + (NQ - j + 1) // 2))
                            bank, col = S_BANK[j]
                            n = P * (j + 1)
                            a.activation(prob[:, sl, POFF[j]:POFF[j + 1]], ps[bank][:, col:col + n], ACT.Exp,
                                         bias=sbias[:, sl, j:j + 1], scale=qrs[:, sl, j:j + 1],
                                         accum_out=rsum[:, sl, j:j + 1]).then_inc(s["exp_done"], 1)
                    if ahead is not None:
                        query(g, ahead)
                    if k == NU and not last:
                        square_keys(g + 1, (0, 1))
                    if value is not None:
                        output(g, value)
                    if turn is not None:
                        for c in range(3):
                            a.wait_ge(s["pt_ready"], g * 3 * NU + (3 * turn + c + 1))
                            n = T_CUTS[c + 1] - T_CUTS[c]
                            a.activation(pt_hi[:, turn % 2, T_CUTS[c]:T_CUTS[c + 1]], ps[T_BANK + c][:, 0:n], ACT.Copy)\
                             .then_inc(s["pt_hi_done"], 1)
                    if k == 1:
                        a.wait_ge(s["o_in"], g * 16 + 16)
                        a.wait_ge(s["acc_free"], g * 4 + 4)
                        a.activation(wo_hi[:].rearrange("p h d -> p (h d)"), oraw[:], ACT.Copy)\
                         .then_inc(s["wo_hi_done"], 1)
                    if k == 2 and not last:
                        round_kv_weights(g + 1)
                    if k == NU - 1 and not last:
                        round_q_weights(g + 1)
                if not last:
                    square_keys(g + 1, (2, 3))
                output(g, NU - 1)
                if not last:
                    round_values(g + 1)
                    open_group(g + 1)

            round_kv_weights(0)
            round_q_weights(0)
            ln["scalar"](a)
            square_keys(0, range(4))
            round_values(0)
            a.wait_ge(s["scale_ready"], 1)
            open_group(0)
            with a.Fori(0, NKV - 1) as g:
                group(g, False)
            group(NKV - 1, True)

        @block.gpsimd
        def _(p):
            p.memset(ones[:], 1.0).then_inc(s["ones_ready"], 1)

            def low_kv_weights(g):
                p.wait_ge(s["wkv_hi_done"], g + 1)
                p.tensor_tensor(wkv_lo[:], raw_kv, wkv_hi[:].bitcast(F32), ALU.subtract).then_inc(s["wkv_lo_done"], 1)

            def low_q_weights(g):
                p.wait_ge(s["wq_hi_done"], g + 1)
                p.tensor_tensor(wq_lo[:], raw_q, wq_hi[:].bitcast(F32), ALU.subtract).then_inc(s["wq_lo_done"], 1)

            low_kv_weights(0)
            ln["pool"](p)
            low_q_weights(0)

            def key_factors(g):
                p.wait_ge(s["ksum_eps_done"], g + 1)
                p.tensor_tensor(krs[:], ksum_eps[:], pm["minus_half"][:, 0:NT], ALU.pow).then_inc(s["krs_done"], 1)

            def query_factor(g, u):
                p.wait_ge(s["qsum_done"], g * NU + (u + 1))
                p.tensor_tensor(qrs[:, u % 2, :], qsum[:, u % 2, :], pm["minus_half"][:, 0:NQ], ALU.pow)\
                 .then_inc(s["qrs_done"], 1)

            def group(g, last):
                for u in range(1, NU):
                    query_factor(g, u)
                    if u == 2:
                        p.wait_ge(s["wo_hi_done"], g + 1)
                        p.tensor_tensor(wo_lo[:].rearrange("p h d -> p (h d)"), oraw[:],
                                        wo_hi[:].rearrange("p h d -> p (h d)").bitcast(F32), ALU.subtract)\
                         .then_inc(s["wo_lo_done"], 1)
                    if u == 4 and not last:
                        low_kv_weights(g + 1)
                if not last:
                    low_q_weights(g + 1)
                    key_factors(g + 1)
                    query_factor(g + 1, 0)

            key_factors(0)
            query_factor(0, 0)
            with p.Fori(0, NKV - 1) as g:
                group(g, False)
            group(NKV - 1, True)

        @block.vector
        def _(v):
            def key_sums(g):
                v.wait_ge(s["ksum_done"], g * NT + NT)
                v.tensor_scalar(ksum_eps[:], ksum[:], 1.0 / HD, QK_EPS, ALU.mult, ALU.add)\
                 .then_inc(s["ksum_eps_done"], 1)

            def keys_and_values(g):
                v.wait_ge(s["krs_done"], g + 1)
                for tt in range(NT):
                    if tt % 2 == 0:
                        v.wait_ge(s["v_hi_done"], g * 4 + (tt // 2 + 1))
                    kv = ps[tt // 2][:].rearrange("p (t f) -> p t f", t=2)
                    v.tensor_scalar(kn[:, tt, :], kv[:, tt % 2, 0:HD], krs[:, tt:tt + 1], None, ALU.mult)\
                     .then_inc(s["kn_done"], 1)
                for q in range(4):
                    kv = ps[q][:].rearrange("p (t f) -> p t f", t=2)
                    v.tensor_tensor(v_lo[:, 2 * q:2 * q + 2, :], kv[:, :, HD:2 * HD],
                                    v_hi[:, 2 * q:2 * q + 2, :].bitcast(F32), ALU.subtract).then_inc(s["v_lo_done"], 1)

            def query_low(g, u):
                v.wait_ge(s["qt_hi_done"], g * NU + (u + 1))
                v.tensor_tensor(qt_lo[:, u % 2, :], ps[Q_BANK][:], qt_hi[:, u % 2, :].bitcast(F32), ALU.subtract)\
                 .then_inc(s["qt_lo_done"], 1)

            def query_sum(g, u):
                v.wait_ge(s["qsum_ready"], g * NU + (u + 1))
                v.tensor_scalar(qsum[:, u % 2, :], ps[1][:, QSUM_COL:QSUM_COL + NQ], HD * QK_EPS, None, ALU.add)\
                 .then_inc(s["qsum_done"], 1)

            def open_group(g):
                for b in range(B):
                    v.wait_ge(s["kt_hi_done"], g * B + (b + 1))
                    v.scalar_tensor_tensor(out=kt_lo[:, b, :], in0=ps[b][:], scalar=kq_scale[:, 0:1],
                                           in1=kt_hi[:, b, :].bitcast(F32), op0=ALU.mult, op1=ALU.subtract)\
                     .then_inc(s["kt_lo_done"], 1)
                query_low(g, 0)

            def output_low(g, u):
                v.wait_ge(s["ot_hi_done"], g * NU + (u + 1))
                v.tensor_tensor(ot_lo[:, u, :], ps[O_BANK][:], ot_hi[:, u, :].bitcast(F32),
                                ALU.subtract).then_inc(s["ot_lo_done"], 1)

            def transposed_low(g, u, cuts):
                for c in cuts:
                    v.wait_ge(s["pt_hi_done"], g * 3 * NU + (3 * u + c + 1))
                    n = T_CUTS[c + 1] - T_CUTS[c]
                    dst = slice(T_CUTS[c], T_CUTS[c + 1])
                    v.tensor_tensor(pt_lo[:, u % 2, dst], ps[T_BANK + c][:, 0:n],
                                    pt_hi[:, u % 2, dst].bitcast(F32), ALU.subtract)\
                     .then_inc(s["pt_lo_done"], 1)

            def add_output(g, q):
                v.wait_ge(s["y_ready"], g * 4 + (q + 1))
                dst = X[:, 2 * q:2 * q + 2, :].rearrange("p t d -> p (t d)")
                v.tensor_tensor(dst, dst, ps[Y_BANK + q][:], ALU.add).then_inc(s["acc_free"], 1)

            def maxima(g, u, tiles):
                sl = u % 2
                for j in tiles:
                    bank, col = S_BANK[j]
                    v.wait_ge(s["s_ready"], g * NU * NQ + (NQ * u + (NQ if j < 2 else NQ - j)))
                    v.tensor_reduce(smax[:, sl, j:j + 1], ps[bank][:, col:col + P * (j + 1)], AX_X, ALU.max)\
                     .then_inc(s["max_done"], 1)
                v.wait_ge(s["qrs_done"], g * NU + (u + 1))
                v.wait_ge(s["max_done"], g * NU * NQ + (NQ * u + NQ - j))
                v.scalar_tensor_tensor(out=sbias[:, sl, j:j + 2], in0=smax[:, sl, j:j + 2], scalar=-1.0,
                                       in1=qrs[:, sl, j:j + 2], op0=ALU.mult, op1=ALU.mult)\
                 .then_inc(s["bias_done"], 1)

            def group(g, last):
                for k in range(NU + 1):
                    score, turn, value, ahead = steps_of(k)
                    if score is not None:
                        maxima(g, score, (3, 2))
                    if value is not None:
                        transposed_low(g, value, (0,))
                    if score is not None:
                        maxima(g, score, (1, 0))
                    if value is not None:
                        transposed_low(g, value, (1, 2))
                    if score is not None:
                        sl = score % 2
                        v.wait_ge(s["exp_done"], g * NU * NQ + NQ * (score + 1))
                        v.reciprocal(rrec[:, sl, :], rsum[:, sl, :]).then_inc(s["rec_done"], 1)
                        v.wait_ge(s["rec_done"], g * NU + (score + 1))
                        for j in range(NQ):
                            pj = prob[:, sl, POFF[j]:POFF[j + 1]]
                            v.tensor_scalar(pj, pj, rrec[:, sl, j:j + 1], None, ALU.mult).then_inc(s["prob_done"], 1)
                    if ahead is not None:
                        query_low(g, ahead)
                    if value is not None:
                        output_low(g, value)
                    if ahead is not None:
                        query_sum(g, ahead)
                transposed_low(g, NU - 1, (0, 1, 2))
                if not last:
                    key_sums(g + 1)
                output_low(g, NU - 1)
                if not last:
                    keys_and_values(g + 1)
                for q in range(3):
                    add_output(g, q)
                if not last:
                    open_group(g + 1)
                add_output(g, 3)
                if not last:
                    query_sum(g + 1, 0)

            v.wait_ge(s["scale_in"], 32)
            v.tensor_tensor(kq_scale[:], scales[:, 0:1], scales[:, 1:2], ALU.mult).then_inc(s["scale_ready"], 1)
            ln["vector"](v)
            v.sem_inc(s["acc_free"], 4)
            key_sums(0)
            keys_and_values(0)
            open_group(0)
            query_sum(0, 0)
            with v.Fori(0, NKV - 1) as g:
                v.wait_ge(s["acc_free"], g * 4 + 4)
                group(g, False)
            v.wait_ge(s["acc_free"], 4 * NKV)
            group(NKV - 1, True)

        @block.tensor
        def _(t):
            ln["tensor"](t)
            t.wait_ge(xt_done, 4)
            t.wait_ge(s["ones_ready"], 1)

            def triple(dst, lhs, rhs, start, stop):
                (lh, ll), (rh, rl) = lhs, rhs
                for q, (l, r) in enumerate(((lh, rh), (ll, rh), (lh, rl))):
                    m = t.matmul(dst, l, r, start=start and q == 0, stop=stop and q == 2)
                return m

            def keys_and_values(g, banks):
                for q in banks:
                    for j in range(2):
                        tok = slice((2 * q + j) * P, (2 * q + j + 1) * P)
                        for k in range(KH):
                            m = triple(ps[q][:, j * 2 * HD:(j + 1) * 2 * HD],
                                       (xt_hi[:, k, tok], xt_lo[:, k, tok]),
                                       (wkv_hi[:, k, :], wkv_lo[:, k, :]), k == 0, k == KH - 1)
                    m.then_inc(s["kv_ready"], 1)

            def query(g, u):
                b, h = divmod(u, REP)
                if u >= 1:
                    t.wait_ge(s["qt_lo_done"], g * NU + u)
                tok = slice(b * C, (b + 1) * C)
                col = slice(h * HD, (h + 1) * HD)
                for k in range(KH):
                    m = triple(ps[Q_BANK][:], (wq_hi[:, k, col], wq_lo[:, k, col]),
                               (xt_hi[:, k, tok], xt_lo[:, k, tok]), k == 0, k == KH - 1)
                m.then_inc(s["q_ready"], 1)

            def query_sum(g, u):
                t.wait_ge(s["qsq_done"], g * NU + (u + 1))
                if u >= 1:
                    t.wait_ge(s["exp_done"], g * NU * NQ + (NQ * (u - 1) + 2))
                for j in range(NQ):
                    m = t.matmul(ps[1][:, QSUM_COL + j:QSUM_COL + j + 1], qsq[:, u % 2, j * P:(j + 1) * P],
                                 ones[:, 0:1], start=True, stop=True)
                m.then_inc(s["qsum_ready"], 1)

            def open_group(g):
                t.wait_ge(s["v_lo_done"], g * 4 + 4)
                for b in range(B):
                    for j in range(NQ):
                        m = t.transpose(ps[b][:, j * P:(j + 1) * P], kn[:, b * NQ + j, :], pm["ident"][:])
                    m.then_inc(s["kt_ready"], 1)
                t.wait_ge(s["wq_lo_done"], g + 1)
                query(g, 0)

            def group(g, last):
                def scores(u):
                    b, sl = u // REP, u % 2
                    t.wait_ge(s["qt_lo_done"], g * NU + (u + 1))
                    for j in reversed(range(NQ)):
                        bank, col = S_BANK[j]
                        if u >= 1 and j >= 1:
                            done = NQ * (u - 1) + (NQ if j == 1 else NQ - j)
                            t.wait_ge(s["exp_done"], g * NU * NQ + done)
                        if j == 2:
                            t.wait_ge(s["qsum_done"], g * NU + (u + 1))
                        q = slice(j * P, (j + 1) * P)
                        n = P * (j + 1)
                        triple(ps[bank][:, col:col + n], (qt_hi[:, sl, q], qt_lo[:, sl, q]),
                               (kt_hi[:, b, 0:n], kt_lo[:, b, 0:n]), True, False)
                        t.matmul(ps[bank][:, col + n - P:col + n], pm["ident_b"][:], pm["causal"][:],
                                 start=False, stop=True).then_inc(s["s_ready"], 1)

                def transposes(u):
                    sl = u % 2
                    t.wait_ge(s["prob_done"], g * NU * NQ + NQ * (u + 1))
                    for i in range(NQ):
                        bank = T_BANK + min(i, 2)
                        if u >= 1 and i < 3:
                            t.wait_ge(s["pt_lo_done"], g * 3 * NU + (3 * (u - 1) + i + 1))
                        base = TOFF[i] - T_CUTS[min(i, 2)]
                        for j in range(i, NQ):
                            c = base + (j - i) * P
                            p0 = POFF[j] + i * P
                            m = t.transpose(ps[bank][:, c:c + P], prob[:, sl, p0:p0 + P], pm["ident"][:])
                        if i != 2:
                            m.then_inc(s["pt_ready"], 1)

                def values(u):
                    b, sl = u // REP, u % 2
                    if u >= 1:
                        t.wait_ge(s["ot_lo_done"], g * NU + u)
                    for i in range(NQ):
                        if i < 3:
                            t.wait_ge(s["pt_lo_done"], g * 3 * NU + (3 * u + i + 1))
                        src = slice(TOFF[i], TOFF[i + 1])
                        m = triple(ps[O_BANK][:, i * P:C], (v_hi[:, b * NQ + i, :], v_lo[:, b * NQ + i, :]),
                                   (pt_hi[:, sl, src], pt_lo[:, sl, src]), i == 0, i == NQ - 1)
                    m.then_inc(s["o_ready"], 1)

                for k in range(NU + 1):
                    score, turn, value, ahead = steps_of(k)
                    if score is not None:
                        scores(score)
                    if ahead is not None:
                        query(g, ahead)
                    if k == 1:
                        t.wait_ge(s["acc_free"], g * 4 + 4)
                    if k == NU and not last:
                        t.wait_ge(s["wkv_lo_done"], g + 2)
                        t.wait_ge(s["exp_done"], g * NU * NQ + NU * NQ)
                        keys_and_values(g + 1, (0, 1))
                    if value is not None:
                        values(value)
                    if turn is not None:
                        transposes(turn)
                    if ahead is not None:
                        query_sum(g, ahead)
                if not last:
                    keys_and_values(g + 1, (2, 3))
                values(NU - 1)
                t.wait_ge(s["wo_lo_done"], g + 1)
                for q in range(4):
                    if q == 3 and not last:
                        open_group(g + 1)
                    b, j0 = divmod(2 * q, NQ)
                    t.wait_ge(s["ot_lo_done"], g * NU + (REP * (b + 1)))
                    if q == 0:
                        t.wait_ge(s["pt_lo_done"], g * 3 * NU + 3 * NU)
                    for j in range(2):
                        tok = slice((j0 + j) * P, (j0 + j + 1) * P)
                        for h in range(REP):
                            m = triple(ps[Y_BANK + q][:, j * D:(j + 1) * D],
                                       (ot_hi[:, b * REP + h, tok], ot_lo[:, b * REP + h, tok]),
                                       (wo_hi[:, h, :], wo_lo[:, h, :]), h == 0, h == REP - 1)
                    m.then_inc(s["y_ready"], 1)
                if not last:
                    t.wait_ge(s["kt_lo_done"], g * B + 2 * B)
                    query_sum(g + 1, 0)

            t.wait_ge(s["wkv_lo_done"], 1)
            keys_and_values(0, range(4))
            open_group(0)
            t.wait_ge(s["kt_lo_done"], B)
            query_sum(0, 0)
            with t.Fori(0, NKV - 1) as g:
                group(g, False)
            group(NKV - 1, True)


def build(nc, ins, out):
    with ExitStack() as ctx:
        cm = lambda n: ctx.enter_context(nc.semaphore(n))
        sb = lambda n, s, d: ctx.enter_context(nc.sbuf_tensor(n, s, d))
        ps = [ctx.enter_context(nc.psum_tensor(f"bank{i}", [P, 512], F32)) for i in range(8)]
        pm = {
            "X": sb("X", [P, NT, D], F32),
            "ident": sb("ident", [P, P], F32),
            "ident_b": sb("ident_b", [P, P], BF16),
            "causal": sb("causal", [P, P], BF16),
            "minus_half": sb("minus_half", [P, B * NCB], F32),
        }
        conv_phase(nc, cm, pm, ps, ins, ins["wconv"])
        ffn_phase(nc, cm, pm, ps, ins, "f1", None)
        attention_phase(nc, cm, pm, ps, ins)
        ffn_phase(nc, cm, pm, ps, ins, "f2", out)


def kernel(**inputs):
    import numpy as np
    import concourse.bacc as bacc
    from concourse.bass_utils import run_bass_kernel_spmd as run

    a = {k.replace("L0_", ""): np.asarray(v) for k, v in inputs.items()}
    routed13 = a["ffn_w13"].reshape(NE, 2, EI, KH, P)
    shared13 = a["ffn_sw13"].reshape(2, SI, KH, P)
    layouts = {
        "x": a["attn_a_x"],
        "cols": a["attn_a_cols"],
        "rows": a["attn_a_rows"],
        "wconv": a["attn_a_block_values"].reshape(NBLK, 2, HO, BS, NST, 2).transpose(4, 1, 0, 2, 5, 3)
                 .reshape(2 * NST, NBLK, HO * P),
        "gate_w": a["ffn_gate_w"].reshape(NE, KH, P).transpose(2, 1, 0).reshape(P, KH * NE),
        "w13": routed13.transpose(1, 2, 0, 3, 4).reshape(2, NRT, P, KH, P).transpose(1, 4, 3, 0, 2)
               .reshape(NRT, P, KH * 2 * P),
        "w2": a["ffn_w2"].transpose(2, 0, 1).reshape(NRT, P, D),
        "sw2": a["ffn_sw2"].T,
        "q_scale": a["attn_b_q_scale"],
        "k_scale": a["attn_b_k_scale"],
        "wqkv": np.concatenate([a["attn_b_Wq"].reshape(NKV, REP * HD, KH, P), a["attn_b_Wk"].reshape(NKV, HD, KH, P),
                                a["attn_b_Wv"].reshape(NKV, HD, KH, P)], axis=1).transpose(0, 3, 2, 1)
                .reshape(NKV, P, KH * (REP + 2) * HD),
        "wo": a["attn_b_Wo"].reshape(D, NKV, REP, HD).transpose(1, 3, 2, 0).reshape(NKV, HD, REP * D),
    }
    r0 = 0
    for m, rows in enumerate(SHARED):
        layouts[f"sw13_{m}"] = shared13[:, r0:r0 + rows].transpose(3, 2, 0, 1).reshape(P, KH * 2 * rows)
        r0 += rows

    nc = bacc.Bacc("TRN2", target_bir_lowering=False, num_devices=1)
    arrays, ins = {}, {}
    for name, value in layouts.items():
        value = np.ascontiguousarray(value)
        arrays[f"in_{name}"] = value
        ins[name] = nc.dram_tensor(f"in_{name}", value.shape, mybir.dt.from_np(value.dtype), kind="ExternalInput").ap()
    out = nc.dram_tensor("out", (B, C, D), F32, kind="ExternalOutput").ap()
    build(nc, ins, out)
    return run(nc, [arrays], core_ids=[0]).results[0]["out"]
```

```python
from contextlib import ExitStack

import concourse.bass as bass
from concourse import mybir

F32 = mybir.dt.float32
F32R = mybir.dt.float32r
BF16 = mybir.dt.bfloat16
I32 = mybir.dt.int32
ALU = mybir.AluOpType
ACT = mybir.ActivationFunctionType
AX_X = mybir.AxisListType.X

P = 128
B, C, D = 2, 512, 256
NT = B * C // P
GC = C // P
KH = D // P
NBLK, BS, KS = 128, 64, 16
NCB = C // BS
NST = KS // 2
HO = BS // 2
XPITCH = 272
NE, EI, TOPK = 16, 176, 6
NRT = NE * EI // P
SI = 2 * EI
SHARED = (SI - 2 * P, P, P)
NSH = len(SHARED)
NTILE = NSH + NRT
HALF = B * C // 2
NH, NKV, HD = 16, 4, 128
REP = NH // NKV
NU = B * REP
NQ = C // P
POFF = [P * (j * (j + 1) // 2) for j in range(NQ + 1)]
TOFF = [P * sum(NQ - i for i in range(k)) for k in range(NQ + 1)]
LN_EPS = 1e-5
QK_EPS = 1e-6
MASKED = -1e30


def keep_busy(t, pm, bank, count):
    for _ in range(count):
        t.matmul(bank[:], pm["zeros"][:, 0:P], pm["zeros"][:], start=True, stop=True)


def layernorm_engines(tag, busy, ctx, nc, cm, pm, ps):
    sb = lambda n, s, d: ctx.enter_context(nc.sbuf_tensor(f"{tag}_{n}", s, d))
    stats, moments = sb("stats", [P, NT, 6], F32), sb("moments", [P, NT, 2], F32)
    var_eps, rstd = sb("var_eps", [P, NT], F32), sb("rstd", [P, NT], F32)
    xn = sb("xn", [P, NT, D], F32)
    xt_hi, xt_lo = sb("xt_hi", [P, KH, B * C], F32R), sb("xt_lo", [P, KH, B * C], F32R)
    s = {n: cm(f"{tag}_{n}") for n in
         ("stats_done", "moments_done", "var_ready", "rstd_ready", "xn_ready", "xt_ready", "xt_hi_done", "xt_lo_done")}
    X = pm["X"]

    HT = NT // 2

    def vector(v, between=None):
        def statistics(tiles):
            for t in tiles:
                v.bn_stats(stats[:, t, :], X[:, t, :]).then_inc(s["stats_done"], 1)

        def variances(half):
            for t in range(half * HT, half * HT + HT):
                v.wait_ge(s["stats_done"], t + 1)
                v.bn_aggr(moments[:, t, :], stats[:, t, :]).then_inc(s["moments_done"], 1)
            v.wait_ge(s["moments_done"], half * HT + HT)
            v.tensor_scalar(var_eps[:, half * HT:half * HT + HT], moments[:, half * HT:half * HT + HT, 1], LN_EPS, None,
                            ALU.add).then_inc(s["var_ready"], 1)

        def normalize(half):
            v.wait_ge(s["rstd_ready"], half + 1)
            for t in range(half * HT, half * HT + HT):
                v.tensor_scalar(xn[:, t, :], X[:, t, :], moments[:, t, 0:1], rstd[:, t:t + 1],
                                ALU.subtract, ALU.mult).then_inc(s["xn_ready"], 1)

        def low_half(half):
            for kh in range(KH):
                b = half * KH + kh
                v.wait_ge(s["xt_hi_done"], b + 1)
                dst = slice(half * HALF, half * HALF + HALF)
                v.tensor_tensor(xt_lo[:, kh, dst], ps[4 + b][:], xt_hi[:, kh, dst].bitcast(F32),
                                ALU.subtract).then_inc(s["xt_lo_done"], 1)

        statistics(range(HT))
        variances(0)
        statistics(range(HT, HT + 3))
        normalize(0)
        statistics(range(HT + 3, NT))
        variances(1)
        low_half(0)
        if between is not None:
            between()
        normalize(1)
        low_half(1)

    def pool(g, halves=range(2)):
        for half in halves:
            part = slice(half * HT, half * HT + HT)
            g.wait_ge(s["var_ready"], half + 1)
            g.tensor_tensor(rstd[:, part], var_eps[:, part], pm["minus_half"][:, part], ALU.pow)\
             .then_inc(s["rstd_ready"], 1)

    def tensor(t, half):
        if half == 0:
            keep_busy(t, pm, ps[0], busy)
        t.wait_ge(s["xn_ready"], HT * half + HT)
        for kh in range(KH):
            b = half * KH + kh
            for j in range(HT):
                m = t.transpose(ps[4 + b][:, j * P:(j + 1) * P], xn[:, HT * half + j, kh * P:(kh + 1) * P], pm["ident"][:])
            m.then_inc(s["xt_ready"], 1)

    def scalar(a, halves=range(2)):
        for b in range(halves[0] * KH, halves[-1] * KH + KH):
            half, kh = divmod(b, KH)
            a.wait_ge(s["xt_ready"], b + 1)
            a.activation(xt_hi[:, kh, half * HALF:half * HALF + HALF], ps[4 + b][:], ACT.Copy)\
             .then_inc(s["xt_hi_done"], 1)

    return xt_hi, xt_lo, s["xt_hi_done"], s["xt_lo_done"], dict(vector=vector, pool=pool, tensor=tensor, scalar=scalar)


def conv_phase(nc, cm, pm, ps, ins, wconv):
    with ExitStack() as ctx:
        sb = lambda n, s, d: ctx.enter_context(nc.sbuf_tensor(f"cv_{n}", s, d))
        x_dup = sb("x_dup", [P, B, NCB, D], F32)
        xc_hi, xc_lo = sb("xc_hi", [P, NCB, B, XPITCH], F32R), sb("xc_lo", [P, NCB, B, XPITCH], F32R)
        raw = [sb(f"raw{i}", [P, HO * P], F32) for i in range(4)]
        ws_hi = [sb(f"ws_hi{i}", [P, NCB * NCB, BS], F32R) for i in range(2)]
        ws_lo = [sb(f"ws_lo{i}", [P, NCB * NCB, BS], F32R) for i in range(2)]
        colrow = sb("colrow", [P, 2], I32)
        colrow_f = sb("colrow_f", [P, 2], F32)
        pair = sb("pair", [P, 1], F32)
        high = sb("high", [P, 1], F32)
        pair_iota, pair_iota_f = sb("pair_iota", [P, NCB * NCB], I32), sb("pair_iota_f", [P, NCB * NCB], F32)
        onehot = sb("onehot", [P, NCB * NCB], F32)
        ones = pm["ones"]
        zeros = pm["zeros"]
        any_high = sb("any_high", [1, 1], I32)
        stats, moments = sb("stats", [P, B * NCB, 6], F32), sb("moments", [P, B * NCB, 2], F32)
        var_eps, rstd = sb("var_eps", [P, B * NCB], F32), sb("rstd", [P, B * NCB], F32)
        s = {n: cm(f"cv_{n}") for n in (
            "x_in", "zeros_ready", "ones_ready", "xd_in", "cr_in", "iota_done", "const_done", "cr_conv", "pair_part", "pair_ready", "onehot_ready",
            "count_ready", "flag_ready", "stats_done", "moments_done", "var_ready", "rstd_ready", "xn_ready",
            "pads_ready", "xc_hi_done", "xc_lo_done", "summed", "ws_hi_done", "ws_lo_done", "ws_free", "conv_done",
            "x_added")}
        raw_in = [cm(f"cv_raw_in{i}") for i in range(4)]
        PARTS = (4, 2, 2, 2)
        first_in = [[cm(f"cv_first_in{i}_{q}") for q in range(n)] for i, n in enumerate(PARTS)]
        X = pm["X"]
        block = ctx.enter_context(nc.Block())
        WARM = 32
        BANKS = 4
        OB = HO // BANKS

        @block.sync
        def _(sp):
            sp.dma_start(colrow[:, 0:1], ins["cols"].rearrange("(n a) -> n a", a=1)).then_inc(s["cr_in"], 16)
            sp.dma_start(colrow[:, 1:2], ins["rows"].rearrange("(n a) -> n a", a=1)).then_inc(s["cr_in"], 16)
            for b in range(B):
                for k in range(2):
                    sp.dma_start(x_dup[k * BS:(k + 1) * BS, b, :, :],
                                 ins["x"][b].rearrange("(c i) t -> i c t", i=BS)).then_inc(s["xd_in"], 16)
            for h in range(4):
                n = HO * P // PARTS[h]
                for q in range(PARTS[h]):
                    part = slice(q * n, (q + 1) * n)
                    sp.dma_start(raw[h][:, part], wconv[h][:, part]).then_inc(first_in[h][q], 16)
            with sp.Fori(1, NST // 2) as i:
                for h in range(4):
                    sp.wait_ge(s["summed"], i * 4 * BANKS + (h - 4 + 1) * BANKS)
                    sp.dma_start(raw[h][:], wconv[bass.ds(i * 4 + h, 1)].rearrange("a n f -> (a n) f"))\
                      .then_inc(raw_in[h], 16)
            sp.dma_start(X[:], ins["x"].rearrange("b (g p) t -> p (b g) t", p=P)).then_inc(s["x_in"], 16)

        @block.scalar
        def _(a):

            def round_input(b, k):
                a.wait_ge(s["pads_ready"], 2)
                a.wait_ge(s["xn_ready"], NCB * (b + 1))
                lo = KS - 1 - k
                a.activation(xc_hi[k * BS:(k + 1) * BS, :, b, lo:lo + D], x_dup[k * BS:(k + 1) * BS, b, :, :],
                             ACT.Copy).then_inc(s["xc_hi_done"], 1)

            def round_stage(st, slot, banks=range(2 * BANKS)):
                if 0 in banks:
                    a.wait_ge(s["ws_free"], st + 1)
                for q in banks:
                    a.wait_ge(s["summed"], st * 2 * BANKS + q + 1)
                    h, bk = divmod(q, BANKS)
                    o0 = h * HO + bk * OB
                    a.activation(ws_hi[slot][:, :, o0:o0 + OB].rearrange("p c o -> p o c"),
                                 ps[bk][:].rearrange("p (o c) -> p o c", o=OB), ACT.Copy)\
                     .then_inc(s["ws_hi_done"], 1)

            round_stage(0, 0, range(0, 4))
            round_input(0, 0)
            round_stage(0, 0, range(4, 5))
            round_input(0, 1)
            round_stage(0, 0, range(5, 7))
            round_input(1, 0)
            round_stage(0, 0, range(7, 8))
            round_stage(1, 1, range(0, 1))
            round_input(1, 1)
            round_stage(1, 1, range(1, 8))
            with a.Fori(1, NST // 2) as i:
                for u in range(2):
                    round_stage(i * 2 + u, u)

        def split_input(engine, b, k):
            lo = KS - 1 - k
            engine.wait_ge(s["xc_hi_done"], 2 * b + k + 1)
            engine.tensor_tensor(xc_lo[k * BS:(k + 1) * BS, :, b, lo:lo + D], x_dup[k * BS:(k + 1) * BS, b, :, :],
                                 xc_hi[k * BS:(k + 1) * BS, :, b, lo:lo + D].bitcast(F32),
                                 ALU.subtract).then_inc(s["xc_lo_done"], 1)

        @block.gpsimd
        def _(g):
            g.iota(pair_iota[:], pattern=[[1, NCB * NCB]], base=0, channel_multiplier=0).then_inc(s["iota_done"], 1)
            g.memset(pm["minus_half"][:], -0.5).then_inc(s["const_done"], 1)
            g.memset(pm["ident"][:], 0.0).then_inc(s["const_done"], 1)
            g.memset(pm["ident_b"][:], 0.0).then_inc(s["const_done"], 1)
            g.memset(pm["causal"][:], 0.0).then_inc(s["const_done"], 1)
            for x in (xc_hi, xc_lo):
                g.memset(x[:, :, :, 0:KS - 1].bitcast(F32), 0.0).then_inc(s["pads_ready"], 1)
            g.wait_ge(s["const_done"], 4)
            for m in (pm["ident"], pm["ident_b"]):
                g.affine_select(out=m[:], in_=m[:], compare_op=ALU.not_equal, fill=1.0, base=0,
                                pattern=[[-1, P]], channel_multiplier=1)
            g.affine_select(out=pm["causal"][:], in_=pm["causal"][:], compare_op=ALU.is_ge, fill=MASKED, base=0,
                            pattern=[[-1, P]], channel_multiplier=1)
            for b in range(B):
                part = slice(b * NCB, (b + 1) * NCB)
                g.wait_ge(s["var_ready"], b + 1)
                g.tensor_tensor(rstd[:, part], var_eps[:, part], pm["minus_half"][:, part], ALU.pow)\
                 .then_inc(s["rstd_ready"], 1)
            g.wait_ge(s["rstd_ready"], B)
            for b in range(B):
                split_input(g, b, 1)

        @block.vector
        def _(v):
            v.memset(zeros[:], 0.0).then_inc(s["zeros_ready"], 1)
            v.memset(ones[:], 1.0).then_inc(s["ones_ready"], 1)
            v.wait_ge(s["cr_in"], 32)
            v.tensor_copy(colrow_f[:], colrow[:]).then_inc(s["cr_conv"], 1)
            v.wait_ge(s["iota_done"], 1)
            v.tensor_copy(pair_iota_f[:], pair_iota[:]).then_inc(s["cr_conv"], 1)
            v.wait_ge(s["cr_conv"], 2)
            v.scalar_tensor_tensor(out=pair[:], in0=colrow_f[:, 0:1], scalar=float(NCB), in1=colrow_f[:, 1:2],
                                   op0=ALU.mult, op1=ALU.add).then_inc(s["pair_part"], 1)
            v.tensor_tensor(high[:], colrow_f[:, 0:1], colrow_f[:, 1:2], ALU.max).then_inc(s["pair_part"], 1)
            v.wait_ge(s["pair_part"], 2)
            v.tensor_scalar(onehot[:], pair_iota_f[:], pair[:, 0:1], None, ALU.is_equal).then_inc(s["onehot_ready"], 1)
            v.tensor_scalar(high[:], high[:], float(NCB // 2), None, ALU.is_ge).then_inc(s["pair_ready"], 1)
            v.wait_ge(s["count_ready"], 1)
            v.tensor_scalar(any_high[:], ps[0][0:1, 0:1], 0.5, None, ALU.is_ge).then_inc(s["flag_ready"], 1)

            def low_stage(st, slot, banks=range(2 * BANKS)):
                for q in banks:
                    v.wait_ge(s["ws_hi_done"], st * 2 * BANKS + q + 1)
                    h, bk = divmod(q, BANKS)
                    o0 = h * HO + bk * OB
                    v.tensor_tensor(ws_lo[slot][:, :, o0:o0 + OB].rearrange("p c o -> p o c"),
                                    ps[bk][:].rearrange("p (o c) -> p o c", o=OB),
                                    ws_hi[slot][:, :, o0:o0 + OB].bitcast(F32).rearrange("p c o -> p o c"),
                                    ALU.subtract).then_inc(s["ws_lo_done"], 1)

            v.wait_ge(s["xd_in"], 64)
            for b in range(B):
                tiles = range(b * NCB, (b + 1) * NCB)
                for n in tiles:
                    v.bn_stats(stats[:, n, :], x_dup[:, b, n % NCB, :]).then_inc(s["stats_done"], 1)
                for n in tiles:
                    v.wait_ge(s["stats_done"], n + 1)
                    v.bn_aggr(moments[:, n, :], stats[:, n, :]).then_inc(s["moments_done"], 1)
                v.wait_ge(s["moments_done"], (b + 1) * NCB)
                part = slice(b * NCB, (b + 1) * NCB)
                v.tensor_scalar(var_eps[:, part], moments[:, part, 1], LN_EPS, None, ALU.add)\
                 .then_inc(s["var_ready"], 1)
            low_stage(0, 0, range(3))
            for b in range(B):
                v.wait_ge(s["rstd_ready"], b + 1)
                for c in range(NCB):
                    n = b * NCB + c
                    v.tensor_scalar(x_dup[:, b, c, :], x_dup[:, b, c, :], moments[:, n, 0:1], rstd[:, n:n + 1],
                                    ALU.subtract, ALU.mult).then_inc(s["xn_ready"], 1)
                low_stage(0, 0, range(3 + b, 4 + b))
            low_stage(0, 0, range(5, 6))
            split_input(v, 0, 0)
            low_stage(0, 0, range(6, 8))
            split_input(v, 1, 0)
            low_stage(1, 1)
            with v.Fori(1, NST // 2) as i:
                for u in range(2):
                    low_stage(i * 2 + u, u)
            v.wait_ge(s["x_in"], 16)
            for r in range(GC):
                v.wait_ge(s["conv_done"], r + 1)
                dst = X[:].rearrange("p (b g) t -> p g b t", b=B)[:, r]
                v.tensor_tensor(dst, dst, ps[4 + r][:].rearrange("p (b t) -> p b t", b=B), ALU.add)\
                 .then_inc(s["x_added"], 1)

        @block.tensor
        def _(t):
            t.wait_ge(s["zeros_ready"], 1)

            def open_accumulators(steps):
                for n in steps:
                    t.matmul(ps[4 + n % GC][:], zeros[:, 0:P], zeros[:], start=n < GC, stop=False)

            open_accumulators(range(2 * GC))
            t.wait_ge(s["pair_ready"], 1)
            t.wait_ge(s["ones_ready"], 1)
            t.matmul(ps[0][0:1, 0:1], high[:, 0:1], ones[:, 0:1], start=True, stop=True).then_inc(s["count_ready"], 1)
            open_accumulators(range(2 * GC, WARM))
            t.sem_inc(s["ws_free"], 2)

            def sum_blocks(st, slot, use, first):
                for h in range(2):
                    if use is not None:
                        t.wait_ge(raw_in[2 * slot + h], 16 * use)
                    for bk in range(BANKS):
                        if use is None:
                            t.wait_ge(first_in[2 * slot + h][bk * PARTS[2 * slot + h] // BANKS], 16)
                        if not (first and h == 0):
                            t.wait_ge(s["ws_lo_done"], st * 2 * BANKS + (h - 1) * BANKS + bk + 1)
                        for o in range(OB):
                            w0 = (bk * OB + o) * P
                            m = t.matmul(ps[bk][:, o * NCB * NCB:(o + 1) * NCB * NCB],
                                         raw[2 * slot + h][:, w0:w0 + P], onehot[:], start=True, stop=True)
                        m.then_inc(s["summed"], 1)

            def products(slot, c, r, tap):
                w = c * NCB + 2 * r
                hi, lo = (x[:, c, :, bass.ds(tap, D)] for x in (xc_hi, xc_lo))
                w_hi, w_lo = (x[slot][:, w:w + 2, :].rearrange("p c o -> p (c o)") for x in (ws_hi, ws_lo))
                for lhs, rhs in ((w_hi, hi), (w_lo, hi), (w_hi, lo)):
                    t.matmul(ps[4 + r][:], lhs, rhs, start=False, stop=False)

            def convolve(st, slot):
                t.wait_ge(s["ws_lo_done"], (st + 1) * 2 * BANKS)
                with t.If(flag != 0):
                    for c in range(NCB):
                        for r in range(GC):
                            if c >= NCB // 2 or r >= GC // 2:
                                products(slot, c, r, st * 2)
                for c in range(NCB // 2):
                    for r in range(GC // 2):
                        products(slot, c, r, st * 2)

            t.wait_ge(s["onehot_ready"], 1)
            t.wait_ge(s["flag_ready"], 1)
            sum_blocks(0, 0, None, True)
            sum_blocks(1, 1, None, False)
            flag = t.value_load(any_high[0:1, 0:1], min_val=0, max_val=1)
            t.wait_ge(s["xc_lo_done"], 2 * B)
            with t.Fori(0, NST // 2 - 1) as i:
                for u in range(2):
                    convolve(i * 2 + u, u)
                    t.sem_inc(s["ws_free"], 1)
                    sum_blocks(i * 2 + u + 2, u, i + 1, False)
            for u in range(2):
                convolve(NST - 2 + u, u)
            for r in range(GC):
                t.matmul(ps[4 + r][:], zeros[:, 0:P], zeros[:], start=False,
                         stop=True).then_inc(s["conv_done"], 1)


def ffn_phase(nc, cm, pm, ps, ins, tag, out):
    with ExitStack() as ctx:
        sb = lambda n, s, d: ctx.enter_context(nc.sbuf_tensor(f"{tag}_{n}", s, d))
        xt_hi, xt_lo, xt_hi_done, xt_done, ln = layernorm_engines(tag, 14 if out is None else 20, ctx, nc, cm, pm, ps)
        WC = KH * 2 * P
        wraw = [sb(f"wraw{i}", [P, WC + D], F32) for i in range(2)]
        w_hi = [sb(f"w_hi{i}", [P, WC + D], F32R) for i in range(2)]
        w_lo = [sb(f"w_lo{i}", [P, WC + D], F32R) for i in range(2)]
        gw, gw_hi, gw_lo = sb("gw", [P, KH * NE], F32), sb("gw_hi", [P, KH, NE], F32R), sb("gw_lo", [P, KH, NE], F32R)
        act = [sb(f"act{i}", [P, HALF], F32) for i in range(2)]
        scaled = [sb(f"scaled{i}", [P, HALF], F32) for i in range(2)]
        h_f = [sb(f"h{i}", [P, HALF], F32) for i in range(2)]
        h_hi = [sb(f"h_hi{i}", [P, HALF], F32R) for i in range(4)]
        h_lo = [sb(f"h_lo{i}", [P, HALF], F32R) for i in range(4)]
        gate_rows = sb("gate_rows", [P, B * C], F32)
        lmax, lsh, lexp = sb("lmax", [P, NT], F32), sb("lsh", [P, NT, NE], F32), sb("lexp", [P, NT, NE], F32)
        lsum, lrec = sb("lsum", [P, NT], F32), sb("lrec", [P, NT], F32)
        NEP = NE + 2
        prob, rest = sb("prob", [P, NT, NEP], F32), sb("rest", [P, NT, NEP], F32)
        top8 = sb("top8", [P, NT, 8], F32)
        sel, ssum, srec = sb("sel", [P, NT, NE], F32), sb("ssum", [P, NT], F32), sb("srec", [P, NT], F32)
        logits_t = sb("logits_t", [NE, B * C], F32)
        comb = sb("comb", [P, NT, P // NE, NE], F32)
        s = {n: cm(f"{tag}_{n}") for n in (
            "gw_in", "gw_hi_done", "gw_lo_done", "w13_hi_done", "w13_lo_done", "w2_hi_done", "w2_lo_done",
            "sentinels_ready", "gate_t", "gate_a", "gate_v", "comb_ready", "gate_rows_ready", "gu_ready", "act_done",
            "scaled_done", "h_ready", "h_hi_done", "h_lo_done", "down_done", "y_ready", "x_added", "out_done")}
        LOGITS_T, LOGITS, TOKEN_WEIGHTS = 0, 2, 3
        LOGITS_COPIED, EXPONENTS = 0, 3
        SHIFTED = 2
        w_in = [cm(f"{tag}_w_in{i}") for i in range(2)]
        X = pm["X"]
        pg, pu, py = ps[0:4:2], ps[1:4:2], ps[4:8]
        block = ctx.enter_context(nc.Block())

        @block.sync
        def _(sp):
            sp.dma_start(gw[:], ins["gate_w"]).then_inc(s["gw_in"], 16)

            def load(m, slot, w13, w2, rows):
                sp.dma_start(wraw[slot][:, 0:KH * 2 * rows], w13).then_inc(w_in[slot], 16)
                sp.dma_start(wraw[slot][0:rows, WC:WC + D], w2).then_inc(w_in[slot], 16)

            r0 = 0
            for m, rows in enumerate(SHARED):
                if m >= 2:
                    sp.wait_ge(s["w2_lo_done"], m - 1)
                load(m, m % 2, ins[f"sw13_{m}"], ins["sw2"][r0:r0 + rows, :], rows)
                r0 += rows
            with sp.Fori(0, NRT // 2) as i:
                for u in range(2):
                    sp.wait_ge(s["w2_lo_done"], i * 2 + (NSH + u - 1))
                    load(None, (NSH + u) % 2, ins["w13"][bass.ds(i * 2 + u, 1)].rearrange("a p f -> (a p) f"),
                         ins["w2"][bass.ds(i * 2 + u, 1)].rearrange("a p f -> (a p) f"), P)
            if out is not None:
                for q in range(4):
                    sp.wait_ge(s["x_added"], q + 1)
                    b, g0 = divmod(2 * q, GC)
                    sp.dma_start(out[b].rearrange("(g p) t -> p g t", p=P)[:, g0:g0 + 2, :],
                                 X[:, 2 * q:2 * q + 2, :]).then_inc(s["out_done"], 16)
                sp.wait_ge(s["out_done"], 64)

        def weight_views(slot, rows):
            v13 = [x[slot][:, 0:KH * 2 * rows].rearrange("p (k g f) -> p k g f", k=KH, g=2) for x in (w_hi, w_lo)]
            v2 = [x[slot][0:rows, WC:WC + D] for x in (w_hi, w_lo)]
            return v13, v2

        @block.scalar
        def _(a):
            a.wait_ge(s["gw_in"], 16)
            a.activation(gw_hi[:].rearrange("p k e -> p (k e)"), gw[:], ACT.Copy).then_inc(s["gw_hi_done"], 1)

            def round_w13(m, slot, use, rows, reuse):
                a.wait_ge(w_in[slot], 32 * use)
                if reuse:
                    a.wait_ge(s["gu_ready"], 2 * m - 2)
                a.activation(w_hi[slot][:, 0:KH * 2 * rows], wraw[slot][:, 0:KH * 2 * rows], ACT.Copy)\
                 .then_inc(s["w13_hi_done"], 1)

            def round_w2(m, slot, rows, reuse):
                if reuse:
                    a.wait_ge(s["down_done"], 2 * m - 2)
                a.activation(w_hi[slot][0:rows, WC:WC + D], wraw[slot][0:rows, WC:WC + D], ACT.Copy)\
                 .then_inc(s["w2_hi_done"], 1)

            def silu(n, half, rows, reuse):
                a.wait_ge(s["gu_ready"], n + 1)
                if reuse:
                    a.wait_ge(s["h_ready"], n - 1)
                a.activation(act[half][0:rows, :], pg[half][0:rows, :], ACT.Silu).then_inc(s["act_done"], 1)

            def round_h(n, half, slot, rows, reuse):
                a.wait_ge(s["h_ready"], n + 1)
                if reuse:
                    a.wait_ge(s["down_done"], n - 3)
                a.activation(h_hi[slot][0:rows, :], h_f[half][0:rows, :], ACT.Copy).then_inc(s["h_hi_done"], 1)

            def tile(m, par, u0, next_use, rows, next_rows, opened=False):
                if not opened:
                    silu(2 * m, 0, rows, not isinstance(m, int) or m >= 1)
                if next_use is not None and not opened:
                    round_w13(m + 1, 1 - par, next_use, next_rows, not isinstance(m, int) or m >= 1)
                round_h(2 * m, 0, u0, rows, not isinstance(m, int) or m >= 2)
                round_w2(m, par, rows, not isinstance(m, int) or m >= 2)
                silu(2 * m + 1, 1, rows, not isinstance(m, int) or m >= 1)
                if isinstance(m, int) and m == NSH - 1:
                    a.wait_ge(s["gate_t"], TOKEN_WEIGHTS + 1)
                    a.activation(gate_rows[:, 0:HALF], pg[0][:], ACT.Copy).then_inc(s["gate_rows_ready"], 1)
                round_h(2 * m + 1, 1, u0 + 1, rows, not isinstance(m, int) or m >= 2)

            rows_of = list(SHARED) + [P] * NRT
            round_w13(0, 0, 1, rows_of[0], False)
            ln["scalar"](a)
            silu(0, 0, rows_of[0], False)
            round_w13(1, 1, 1, rows_of[1], False)
            for half in range(2):
                a.wait_ge(s["gate_t"], LOGITS_T + half + 1)
                a.activation(logits_t[:, half * HALF:(half + 1) * HALF], py[half][0:NE, :], ACT.Copy)\
                 .then_inc(s["gate_a"], 1)
            for m in range(NSH):
                if m == 1:
                    a.wait_ge(s["gate_v"], SHIFTED)
                    a.activation(lexp[:], lsh[:], ACT.Exp).then_inc(s["gate_a"], 1)
                tile(m, m % 2, 2 * (m % 2), (m + 1) // 2 + 1, rows_of[m], rows_of[m + 1], opened=m == 0)
            with a.Fori(0, NRT // 2 - 1) as i:
                for u in range(2):
                    par = (NSH + u) % 2
                    tile(i * 2 + (NSH + u), par, 2 * par, i + ((NSH + u + 1) // 2 + 1), P, P)
            for m in range(NTILE - 2, NTILE):
                tile(m, m % 2, 2 * (m % 2), (m + 1) // 2 + 1 if m + 1 < NTILE else None, P, P)

        @block.gpsimd
        def _(g):
            g.memset(prob[:], -1.0).then_inc(s["sentinels_ready"], 1)

            def low_w13(m, slot, rows):
                g.wait_ge(s["w13_hi_done"], m + 1)
                n = KH * 2 * rows
                g.tensor_tensor(w_lo[slot][:, 0:n], wraw[slot][:, 0:n], w_hi[slot][:, 0:n].bitcast(F32),
                                ALU.subtract).then_inc(s["w13_lo_done"], 1)

            def low_w2(m, slot, rows):
                g.wait_ge(s["w2_hi_done"], m + 1)
                g.tensor_tensor(w_lo[slot][0:rows, WC:WC + D], wraw[slot][0:rows, WC:WC + D],
                                w_hi[slot][0:rows, WC:WC + D].bitcast(F32), ALU.subtract)\
                 .then_inc(s["w2_lo_done"], 1)

            def scale(n, half):
                g.wait_ge(s["act_done"], n + 1)
                g.tensor_tensor(scaled[half][:], act[half][:], gate_rows[:, half * HALF:(half + 1) * HALF],
                                ALU.mult).then_inc(s["scaled_done"], 1)

            def tile(m, par, routed, has_next, rows, next_rows):
                if routed:
                    scale(2 * m, 0)
                if has_next:
                    low_w13(m + 1, 1 - par, next_rows)
                low_w2(m, par, rows)
                if routed:
                    scale(2 * m + 1, 1)

            rows_of = list(SHARED) + [P] * NRT
            ln["pool"](g, (0,))
            low_w13(0, 0, rows_of[0])
            ln["pool"](g, (1,))
            for m in range(NSH):
                tile(m, m % 2, False, True, rows_of[m], rows_of[m + 1])
            g.wait_ge(s["gate_rows_ready"], 2)
            with g.Fori(0, NRT // 2 - 1) as i:
                for u in range(2):
                    tile(i * 2 + (NSH + u), (NSH + u) % 2, True, True, P, P)
            for m in range(NTILE - 2, NTILE):
                tile(m, m % 2, True, m + 1 < NTILE, P, P)

        @block.vector
        def _(v):
            def low_gate_weights():
                v.wait_ge(s["gw_hi_done"], 1)
                v.tensor_tensor(gw_lo[:].rearrange("p k e -> p (k e)"), gw[:],
                                gw_hi[:].rearrange("p k e -> p (k e)").bitcast(F32), ALU.subtract)\
                 .then_inc(s["gw_lo_done"], 1)

            ln["vector"](v, low_gate_weights)
            step = s["gate_v"]

            def spread(x, n=NE):
                return x[:].unsqueeze(2).to_broadcast([P, NT, n])

            def gate_shift():
                v.wait_ge(s["gate_t"], LOGITS + 1)
                logits = py[3][:, 0:NT * NE].rearrange("p (t e) -> p t e", t=NT)
                v.tensor_reduce(lmax[:], logits, AX_X, ALU.max).then_inc(step, 1)
                v.wait_ge(step, 1)
                v.tensor_tensor(lsh[:], logits, spread(lmax), ALU.subtract).then_inc(step, 1)

            def gate_softmax():
                v.wait_ge(s["gate_a"], EXPONENTS)
                v.tensor_reduce(lsum[:], lexp[:], AX_X, ALU.add).then_inc(step, 1)
                v.wait_ge(step, 3)
                v.reciprocal(lrec[:], lsum[:]).then_inc(step, 1)
                v.wait_ge(step, 4)
                v.wait_ge(s["sentinels_ready"], 1)
                v.tensor_tensor(prob[:, :, 0:NE], lexp[:], spread(lrec), ALU.mult).then_inc(step, 1)
                v.wait_ge(step, 5)
                for t in range(NT):
                    v.max(top8[:, t, :], prob[:, t, 0:NE]).then_inc(step, 1)

            def gate_select():
                v.wait_ge(step, 5 + NT)
                v.memset(top8[:, :, TOPK:8], -1.0).then_inc(step, 1)
                v.wait_ge(step, 6 + NT)
                for t in range(NT):
                    v.match_replace(out=rest[:, t, :], in_to_replace=top8[:, t, :], in_values=prob[:, t, :],
                                    imm_value=0.0).then_inc(step, 1)
                v.wait_ge(step, 6 + 2 * NT)
                v.tensor_tensor(sel[:], prob[:, :, 0:NE], rest[:, :, 0:NE], ALU.subtract).then_inc(step, 1)

            def gate_weights():
                v.wait_ge(step, 7 + 2 * NT)
                v.tensor_reduce(ssum[:], sel[:], AX_X, ALU.add).then_inc(step, 1)
                v.wait_ge(step, 8 + 2 * NT)
                v.tensor_scalar(ssum[:], ssum[:], 1e-20, None, ALU.add).then_inc(step, 1)
                v.wait_ge(step, 9 + 2 * NT)
                v.reciprocal(srec[:], ssum[:]).then_inc(step, 1)
                v.wait_ge(step, 10 + 2 * NT)
                v.tensor_tensor(sel[:], sel[:], spread(srec), ALU.mult).then_inc(step, 1)
                v.wait_ge(step, 11 + 2 * NT)
                v.tensor_copy(comb[:], sel[:].unsqueeze(2).to_broadcast([P, NT, P // NE, NE]))\
                 .then_inc(s["comb_ready"], 1)

            def unit(n, half, slot, rows, routed):
                if routed:
                    v.wait_ge(s["scaled_done"], n - (2 * NSH - 1))
                    src = scaled
                else:
                    v.wait_ge(s["act_done"], n + 1)
                    src = act
                if not isinstance(n, int) or n >= 2:
                    v.wait_ge(s["h_hi_done"], n - 1)
                    v.wait_ge(s["h_lo_done"], n - 1)
                v.tensor_tensor(h_f[half][0:rows, :], src[half][0:rows, :], pu[half][0:rows, :], ALU.mult)\
                 .then_inc(s["h_ready"], 1)
                v.wait_ge(s["h_hi_done"], n + 1)
                v.wait_ge(s["h_ready"], n + 1)
                v.tensor_tensor(h_lo[slot][0:rows, :], h_f[half][0:rows, :], h_hi[slot][0:rows, :].bitcast(F32),
                                ALU.subtract).then_inc(s["h_lo_done"], 1)

            unit(0, 0, 0, SHARED[0], False)
            unit(1, 1, 1, SHARED[0], False)
            gate_shift()
            gate_softmax()
            unit(2, 0, 2, SHARED[1], False)
            gate_select()
            unit(3, 1, 3, SHARED[1], False)
            gate_weights()
            for n in range(4, 2 * NSH - 1):
                unit(n, n % 2, n % 4, SHARED[n // 2], False)
            v.wait_ge(s["gate_t"], TOKEN_WEIGHTS + 2)
            v.tensor_copy(gate_rows[:, HALF:2 * HALF], pu[0][:]).then_inc(s["gate_rows_ready"], 1)
            unit(2 * NSH - 1, 1, (2 * NSH - 1) % 4, SHARED[NSH - 1], False)
            with v.Fori(0, NRT // 2) as i:
                for k in range(4):
                    n = 2 * NSH + k
                    unit(i * 4 + n, n % 2, n % 4, P, True)
            for q in range(4):
                v.wait_ge(s["y_ready"], q + 1)
                dst = X[:, 2 * q:2 * q + 2, :].rearrange("p t d -> p (t d)")
                v.tensor_tensor(dst, dst, py[q][:], ALU.add).then_inc(s["x_added"], 1)

        @block.tensor
        def _(t):

            def gate_logits(half):
                tok = slice(half * HALF, (half + 1) * HALF)
                steps = [(w[:, k, :], x[:, k, tok]) for k in range(KH)
                         for w, x in ((gw_hi, xt_hi), (gw_lo, xt_hi), (gw_hi, xt_lo))]
                for q, (w, x) in enumerate(steps):
                    m = t.matmul(py[half][0:NE, :], w, x, start=q == 0, stop=q == len(steps) - 1)
                m.then_inc(s["gate_t"], 1)

            def turn_logits():
                t.wait_ge(s["gate_a"], LOGITS_COPIED + 2)
                for tt in range(NT):
                    m = t.transpose(py[3][:, tt * NE:(tt + 1) * NE], logits_t[:, tt * P:(tt + 1) * P],
                                    pm["ident"][0:NE, 0:NE])
                m.then_inc(s["gate_t"], 1)

            def gate_weights():
                t.wait_ge(s["comb_ready"], 1)
                t.wait_ge(s["h_ready"], 2 * NSH - 1)
                for half, bank in enumerate((pg[0], pu[0])):
                    for j in range(4):
                        mm = t.transpose(bank[:, j * P:(j + 1) * P],
                                         comb[:, 4 * half + j, :, :].rearrange("p r e -> p (r e)"), pm["ident"][:])
                    mm.then_inc(s["gate_t"], 1)

            def gate_up(n, half, m, slot, rows, reuse):
                if half == 0:
                    t.wait_ge(s["w13_lo_done"], m + 1)
                if reuse:
                    t.wait_ge(s["h_ready"], n - 1)
                (vhi, vlo), _ = weight_views(slot, rows)
                tok = slice(half * HALF, (half + 1) * HALF)
                for gu, bank in enumerate((pg, pu)):
                    steps = [(w[:, k, gu, :], xt_hi[:, k, tok]) for k in range(KH) for w in (vhi, vlo)]
                    steps += [(vhi[:, k, gu, :], xt_lo[:, k, tok]) for k in range(KH)]
                    for q, (w, x) in enumerate(steps):
                        if gu == 0 and isinstance(n, int) and n < 2 and q in (0, 2 * KH):
                            t.wait_ge(xt_hi_done if q == 0 else xt_done, KH * (n + 1))
                        mm = t.matmul(bank[half][0:rows, :], w, x, start=q == 0, stop=q == len(steps) - 1)
                mm.then_inc(s["gu_ready"], 1)

            def down(n, half, m, slot, hslot, rows, first, last):
                if half == 0:
                    t.wait_ge(s["w2_lo_done"], m + 1)
                t.wait_ge(s["h_lo_done"], n + 1)
                _, (vhi, vlo) = weight_views(slot, rows)
                for j in range(4):
                    tok = slice(j * P, (j + 1) * P)
                    bank = py[2 * half + j // 2][:, (j % 2) * D:(j % 2 + 1) * D]
                    trio = ((h_hi, vhi), (h_lo, vhi), (h_hi, vlo))
                    for q, (h, w) in enumerate(trio):
                        mm = t.matmul(bank, h[hslot][0:rows, tok], w, start=first and q == 0 and j % 2 == 0,
                                      stop=last and q == 2, skip_group_check=True)
                    if last and j % 2:
                        mm.then_inc(s["y_ready"], 1)
                if not last:
                    mm.then_inc(s["down_done"], 1)

            ln["tensor"](t, 0)
            for n in range(2 * NSH):
                gate_up(n, n % 2, n // 2, (n // 2) % 2, SHARED[n // 2], n >= 2)
                if n == 0:
                    ln["tensor"](t, 1)
                    t.wait_ge(s["gw_lo_done"], 1)
                    gate_logits(0)
                    t.wait_ge(xt_done, 2 * KH)
                    gate_logits(1)
                if n == 1:
                    turn_logits()
                if n == 3:
                    t.wait_ge(s["gate_v"], SHIFTED)
                if n == 2 * NSH - 1:
                    gate_weights()
                if n >= 2:
                    down(n - 2, n % 2, n // 2 - 1, (n // 2 - 1) % 2, (n - 2) % 4, SHARED[n // 2 - 1], n < 4, False)
            t.wait_ge(s["gate_rows_ready"], 2)
            with t.Fori(0, NRT // 2) as i:
                for k in range(4):
                    n, d = 2 * NSH + k, 2 * NSH + k - 2
                    gate_up(i * 4 + n, n % 2, i * 2 + n // 2, (n // 2) % 2, P, True)
                    down(i * 4 + d, d % 2, i * 2 + d // 2, (d // 2) % 2, d % 4, P, False, False)
            for n in range(2 * NTILE - 2, 2 * NTILE):
                down(n, n % 2, n // 2, (n // 2) % 2, n % 4, P, False, True)


def attention_phase(nc, cm, pm, ps, ins):
    with ExitStack() as ctx:
        sb = lambda n, s, d: ctx.enter_context(nc.sbuf_tensor(f"at_{n}", s, d))
        xt_hi, xt_lo, _, xt_done, ln = layernorm_engines("at", 20, ctx, nc, cm, pm, ps)
        GW = (REP + 2) * HD
        wraw = sb("wraw", [P, KH * GW], F32)
        wq_hi, wq_lo = sb("wq_hi", [P, KH, REP * HD], F32R), sb("wq_lo", [P, KH, REP * HD], F32R)
        wkv_hi, wkv_lo = sb("wkv_hi", [P, KH, 2 * HD], F32R), sb("wkv_lo", [P, KH, 2 * HD], F32R)
        oraw = sb("oraw", [P, REP * D], F32)
        wo_hi, wo_lo = sb("wo_hi", [P, REP, D], F32R), sb("wo_lo", [P, REP, D], F32R)
        scales, kq_scale = sb("scales", [P, 2], F32), sb("kq_scale", [P, 1], F32)
        ones = pm["ones"]
        ksum, ksum_eps, krs = sb("ksum", [P, NT], F32), sb("ksum_eps", [P, NT], F32), sb("krs", [P, NT], F32)
        ksq = sb("ksq", [P, NT, HD], F32)
        kn = sb("kn", [P, NT, HD], F32)
        kt_hi, kt_lo = sb("kt_hi", [P, B, C], F32R), sb("kt_lo", [P, B, C], F32R)
        v_hi, v_lo = sb("v_hi", [P, NT, HD], F32R), sb("v_lo", [P, NT, HD], F32R)
        qt_hi, qt_lo = sb("qt_hi", [P, 2, C], F32R), sb("qt_lo", [P, 2, C], F32R)
        qsq = sb("qsq", [P, 2, C], F32)
        qsum, qrs = sb("qsum", [P, 2, NQ], F32), sb("qrs", [P, 2, NQ], F32)
        smax, sbias = sb("smax", [P, 2, NQ], F32), sb("sbias", [P, 2, NQ], F32)
        rsum, rrec = sb("rsum", [P, 2, NQ], F32), sb("rrec", [P, 2, NQ], F32)
        prob = sb("prob", [P, 2, POFF[NQ]], F32)
        pt_hi, pt_lo = sb("pt_hi", [P, 2, TOFF[NQ]], F32R), sb("pt_lo", [P, 2, TOFF[NQ]], F32R)
        ot_hi, ot_lo = sb("ot_hi", [P, NU, C], F32R), sb("ot_lo", [P, NU, C], F32R)
        s = {n: cm(f"at_{n}") for n in (
            "scale_in", "scale_ready", "kv_in", "w_in", "o_in", "acc_free", "wq_hi_done", "wq_lo_done", "wkv_hi_done", "wkv_lo_done",
            "wo_hi_done", "wo_lo_done", "kv_ready", "ksum_done", "ksum_eps_done", "krs_done", "kn_done", "kt_ready",
            "kt_hi_done", "kt_lo_done", "v_hi_done", "v_lo_done", "q_ready", "qsq_done", "qt_hi_done", "qt_lo_done",
            "qsum_ready", "qsum_done", "qrs_done", "s_ready", "max_done", "bias_done", "exp_done", "rec_done",
            "prob_done", "pt_ready", "pt_hi_done", "pt_lo_done", "o_ready", "ot_hi_done", "ot_lo_done", "y_ready")}
        X = pm["X"]
        raw_q = wraw[:].rearrange("p (k f) -> p k f", k=KH)[:, :, 0:REP * HD]
        raw_kv = wraw[:].rearrange("p (k f) -> p k f", k=KH)[:, :, REP * HD:GW]
        S_BANK = ((0, 0), (0, P), (1, 0), (2, 0))
        QSUM_COL = 3 * P
        Q_BANK, T_BANK, O_BANK, Y_BANK = 3, 4, 7, 4
        KV_BANK = (3, 0, 1, 2)
        T_CUTS = (0, TOFF[1], TOFF[2], TOFF[4])
        block = ctx.enter_context(nc.Block())

        def steps_of(k):
            return (k if k < NU else None, k - 1 if 1 <= k <= NU else None, k - 2 if 2 <= k <= NU else None,
                    k + 1 if k + 1 < NU else None)

        @block.sync
        def _(sp):
            sp.dma_start(raw_kv, ins["wqkv"][0].rearrange("p (k f) -> p k f", k=KH)[:, :, REP * HD:GW])\
              .then_inc(s["kv_in"], 16)
            sp.dma_start(raw_q, ins["wqkv"][0].rearrange("p (k f) -> p k f", k=KH)[:, :, 0:REP * HD])\
              .then_inc(s["w_in"], 16)
            sp.dma_start(scales[:, 0:1], ins["q_scale"].rearrange("(d a) -> d a", a=1)).then_inc(s["scale_in"], 16)
            sp.dma_start(scales[:, 1:2], ins["k_scale"].rearrange("(d a) -> d a", a=1)).then_inc(s["scale_in"], 16)
            sp.dma_start(oraw[:], ins["wo"][0]).then_inc(s["o_in"], 16)
            with sp.Fori(1, NKV) as g:
                sp.wait_ge(s["wq_lo_done"], g)
                sp.dma_start(wraw[:], ins["wqkv"][bass.ds(g, 1)].rearrange("a p f -> (a p) f")).then_inc(s["w_in"], 16)
                sp.wait_ge(s["wo_lo_done"], g)
                sp.dma_start(oraw[:], ins["wo"][bass.ds(g, 1)].rearrange("a p f -> (a p) f")).then_inc(s["o_in"], 16)

        @block.scalar
        def _(a):
            def round_kv_weights(g):
                if isinstance(g, int):
                    a.wait_ge(s["kv_in"], 16)
                else:
                    a.wait_ge(s["w_in"], g * 16 + 16)
                a.activation(wkv_hi[:], raw_kv, ACT.Copy).then_inc(s["wkv_hi_done"], 1)

            def round_q_weights(g):
                if isinstance(g, int):
                    a.wait_ge(s["w_in"], 16)
                a.activation(wq_hi[:], raw_q, ACT.Copy).then_inc(s["wq_hi_done"], 1)

            def square_keys(g, banks):
                for q in banks:
                    a.wait_ge(s["kv_ready"], g * 4 + (q + 1))
                    kv = ps[KV_BANK[q]][:].rearrange("p (t f) -> p t f", t=2)
                    for j in range(2):
                        tt = 2 * q + j
                        a.activation(ksq[:, tt, :], kv[:, j, 0:HD], ACT.Square, accum_out=ksum[:, tt:tt + 1])\
                         .then_inc(s["ksum_done"], 1)

            def round_values(g, banks=range(4)):
                for q in banks:
                    kv = ps[KV_BANK[q]][:].rearrange("p (t f) -> p t f", t=2)
                    a.activation(v_hi[:, 2 * q:2 * q + 2, :], kv[:, :, HD:2 * HD], ACT.Copy).then_inc(s["v_hi_done"], 1)

            def query(g, u):
                a.wait_ge(s["q_ready"], g * NU + (u + 1))
                a.activation(qsq[:, u % 2, :], ps[Q_BANK][:], ACT.Square).then_inc(s["qsq_done"], 1)
                a.activation(qt_hi[:, u % 2, :], ps[Q_BANK][:], ACT.Copy).then_inc(s["qt_hi_done"], 1)

            def open_group(g):
                for b in range(B):
                    a.wait_ge(s["kt_ready"], g * B + (b + 1))
                    a.activation(kt_hi[:, b, :], ps[b][:], ACT.Copy, scale=kq_scale[:, 0:1]).then_inc(s["kt_hi_done"], 1)
                query(g, 0)

            def output(g, u):
                a.wait_ge(s["o_ready"], g * NU + (u + 1))
                a.activation(ot_hi[:, u, :], ps[O_BANK][:], ACT.Copy).then_inc(s["ot_hi_done"], 1)

            def group(g, last):
                for k in range(NU + 1):
                    score, turn, value, ahead = steps_of(k)
                    if score is not None:
                        sl = score % 2
                        for j in reversed(range(NQ)):
                            if k <= 1 and j == 1:
                                query(g, ahead)
                            if j % 2:
                                a.wait_ge(s["bias_done"], g * 2 * NU + (2 * score + (NQ - j + 1) // 2))
                            bank, col = S_BANK[j]
                            n = P * (j + 1)
                            a.activation(prob[:, sl, POFF[j]:POFF[j + 1]], ps[bank][:, col:col + n], ACT.Exp,
                                         bias=sbias[:, sl, j:j + 1], scale=qrs[:, sl, j:j + 1],
                                         accum_out=rsum[:, sl, j:j + 1]).then_inc(s["exp_done"], 1)
                    if ahead is not None and k > 1:
                        query(g, ahead)
                    if k == NU and not last:
                        square_keys(g + 1, (0, 1))
                    if value is not None:
                        output(g, value)
                    if turn is not None:
                        for c in range(3):
                            a.wait_ge(s["pt_ready"], g * 3 * NU + (3 * turn + c + 1))
                            n = T_CUTS[c + 1] - T_CUTS[c]
                            a.activation(pt_hi[:, turn % 2, T_CUTS[c]:T_CUTS[c + 1]], ps[T_BANK + c][:, 0:n], ACT.Copy)\
                             .then_inc(s["pt_hi_done"], 1)
                    if k == 1:
                        a.wait_ge(s["o_in"], g * 16 + 16)
                        a.wait_ge(s["acc_free"], g * 4 + 4)
                        a.activation(wo_hi[:].rearrange("p h d -> p (h d)"), oraw[:], ACT.Copy)\
                         .then_inc(s["wo_hi_done"], 1)
                    if k == 2 and not last:
                        round_kv_weights(g + 1)
                    if k == NU - 1 and not last:
                        round_q_weights(g + 1)
                if not last:
                    square_keys(g + 1, (2, 3))
                output(g, NU - 1)
                if not last:
                    round_values(g + 1)
                    open_group(g + 1)

            round_kv_weights(0)
            ln["scalar"](a, (0,))
            round_q_weights(0)
            ln["scalar"](a, (1,))
            for banks in (range(2), range(2, 4)):
                square_keys(0, banks)
                round_values(0, banks)
            a.wait_ge(s["scale_ready"], 1)
            open_group(0)
            with a.Fori(0, NKV - 1) as g:
                group(g, False)
            group(NKV - 1, True)

        @block.gpsimd
        def _(p):
            def low_kv_weights(g):
                p.wait_ge(s["wkv_hi_done"], g + 1)
                p.tensor_tensor(wkv_lo[:], raw_kv, wkv_hi[:].bitcast(F32), ALU.subtract).then_inc(s["wkv_lo_done"], 1)

            def low_q_weights(g):
                p.wait_ge(s["wq_hi_done"], g + 1)
                p.tensor_tensor(wq_lo[:], raw_q, wq_hi[:].bitcast(F32), ALU.subtract).then_inc(s["wq_lo_done"], 1)

            ln["pool"](p, (0,))
            low_kv_weights(0)
            ln["pool"](p, (1,))
            low_q_weights(0)

            def key_factors(g):
                for b in range(B):
                    part = slice(b * NQ, (b + 1) * NQ)
                    p.wait_ge(s["ksum_eps_done"], g * B + (b + 1))
                    p.tensor_tensor(krs[:, part], ksum_eps[:, part], pm["minus_half"][:, part], ALU.pow)\
                     .then_inc(s["krs_done"], 1)

            def query_factor(g, u):
                p.wait_ge(s["qsum_done"], g * NU + (u + 1))
                p.tensor_tensor(qrs[:, u % 2, :], qsum[:, u % 2, :], pm["minus_half"][:, 0:NQ], ALU.pow)\
                 .then_inc(s["qrs_done"], 1)

            def group(g, last):
                for u in range(1, NU):
                    query_factor(g, u)
                    if u == 2:
                        p.wait_ge(s["wo_hi_done"], g + 1)
                        p.tensor_tensor(wo_lo[:].rearrange("p h d -> p (h d)"), oraw[:],
                                        wo_hi[:].rearrange("p h d -> p (h d)").bitcast(F32), ALU.subtract)\
                         .then_inc(s["wo_lo_done"], 1)
                    if u == 4 and not last:
                        low_kv_weights(g + 1)
                if not last:
                    low_q_weights(g + 1)
                    key_factors(g + 1)
                    query_factor(g + 1, 0)

            key_factors(0)
            query_factor(0, 0)
            with p.Fori(0, NKV - 1) as g:
                group(g, False)
            group(NKV - 1, True)

        @block.vector
        def _(v):
            def key_sums(g, b):
                v.wait_ge(s["ksum_done"], g * NT + NQ * (b + 1))
                part = slice(b * NQ, (b + 1) * NQ)
                v.tensor_scalar(ksum_eps[:, part], ksum[:, part], 1.0 / HD, QK_EPS, ALU.mult, ALU.add)\
                 .then_inc(s["ksum_eps_done"], 1)

            def keys_and_values(g):
                for b in range(B):
                    v.wait_ge(s["krs_done"], g * B + (b + 1))
                    for tt in range(b * NQ, (b + 1) * NQ):
                        if tt % 2 == 0:
                            v.wait_ge(s["v_hi_done"], g * 4 + (tt // 2 + 1))
                        kv = ps[KV_BANK[tt // 2]][:].rearrange("p (t f) -> p t f", t=2)
                        v.tensor_scalar(kn[:, tt, :], kv[:, tt % 2, 0:HD], krs[:, tt:tt + 1], None, ALU.mult)\
                         .then_inc(s["kn_done"], 1)
                    for q in (2 * b, 2 * b + 1):
                        kv = ps[KV_BANK[q]][:].rearrange("p (t f) -> p t f", t=2)
                        v.tensor_tensor(v_lo[:, 2 * q:2 * q + 2, :], kv[:, :, HD:2 * HD],
                                        v_hi[:, 2 * q:2 * q + 2, :].bitcast(F32), ALU.subtract)\
                         .then_inc(s["v_lo_done"], 1)

            def query_low(g, u):
                v.wait_ge(s["qt_hi_done"], g * NU + (u + 1))
                v.tensor_tensor(qt_lo[:, u % 2, :], ps[Q_BANK][:], qt_hi[:, u % 2, :].bitcast(F32), ALU.subtract)\
                 .then_inc(s["qt_lo_done"], 1)

            def query_sum(g, u):
                v.wait_ge(s["qsum_ready"], g * NU + (u + 1))
                v.tensor_scalar(qsum[:, u % 2, :], ps[1][:, QSUM_COL:QSUM_COL + NQ], HD * QK_EPS, None, ALU.add)\
                 .then_inc(s["qsum_done"], 1)

            def open_group(g):
                for b in range(B):
                    v.wait_ge(s["kt_hi_done"], g * B + (b + 1))
                    v.scalar_tensor_tensor(out=kt_lo[:, b, :], in0=ps[b][:], scalar=kq_scale[:, 0:1],
                                           in1=kt_hi[:, b, :].bitcast(F32), op0=ALU.mult, op1=ALU.subtract)\
                     .then_inc(s["kt_lo_done"], 1)
                query_low(g, 0)

            def output_low(g, u):
                v.wait_ge(s["ot_hi_done"], g * NU + (u + 1))
                v.tensor_tensor(ot_lo[:, u, :], ps[O_BANK][:], ot_hi[:, u, :].bitcast(F32),
                                ALU.subtract).then_inc(s["ot_lo_done"], 1)

            def transposed_low(g, u, cuts):
                for c in cuts:
                    v.wait_ge(s["pt_hi_done"], g * 3 * NU + (3 * u + c + 1))
                    n = T_CUTS[c + 1] - T_CUTS[c]
                    dst = slice(T_CUTS[c], T_CUTS[c + 1])
                    v.tensor_tensor(pt_lo[:, u % 2, dst], ps[T_BANK + c][:, 0:n],
                                    pt_hi[:, u % 2, dst].bitcast(F32), ALU.subtract)\
                     .then_inc(s["pt_lo_done"], 1)

            def add_output(g, q):
                v.wait_ge(s["y_ready"], g * 4 + (q + 1))
                dst = X[:, 2 * q:2 * q + 2, :].rearrange("p t d -> p (t d)")
                v.tensor_tensor(dst, dst, ps[Y_BANK + q][:], ALU.add).then_inc(s["acc_free"], 1)

            def maxima(g, u, tiles):
                sl = u % 2
                for j in tiles:
                    bank, col = S_BANK[j]
                    v.wait_ge(s["s_ready"], g * NU * NQ + (NQ * u + (NQ if j < 2 else NQ - j)))
                    v.tensor_reduce(smax[:, sl, j:j + 1], ps[bank][:, col:col + P * (j + 1)], AX_X, ALU.max)\
                     .then_inc(s["max_done"], 1)
                v.wait_ge(s["qrs_done"], g * NU + (u + 1))
                v.wait_ge(s["max_done"], g * NU * NQ + (NQ * u + NQ - j))
                v.scalar_tensor_tensor(out=sbias[:, sl, j:j + 2], in0=smax[:, sl, j:j + 2], scalar=-1.0,
                                       in1=qrs[:, sl, j:j + 2], op0=ALU.mult, op1=ALU.mult)\
                 .then_inc(s["bias_done"], 1)

            def group_steps(g, ks, pending):
                for k in ks:
                    score, turn, value, ahead = steps_of(k)
                    if value is not None:
                        transposed_low(g, value, (0,))
                    if score is not None:
                        maxima(g, score, (3, 2))
                    if value is not None:
                        transposed_low(g, value, (1,))
                    if score is not None:
                        maxima(g, score, (1, 0))
                    if value is not None:
                        transposed_low(g, value, (2,))
                    if k <= 1:
                        query_low(g, ahead)
                    if score is not None:
                        sl = score % 2
                        v.wait_ge(s["exp_done"], g * NU * NQ + NQ * (score + 1))
                        v.reciprocal(rrec[:, sl, :], rsum[:, sl, :]).then_inc(s["rec_done"], 1)
                        v.wait_ge(s["rec_done"], g * NU + (score + 1))
                        for j in range(NQ):
                            pj = prob[:, sl, POFF[j]:POFF[j + 1]]
                            v.tensor_scalar(pj, pj, rrec[:, sl, j:j + 1], None, ALU.mult).then_inc(s["prob_done"], 1)
                    if ahead is not None and k > 1:
                        query_low(g, ahead)
                    if value is not None:
                        output_low(g, value)
                    if pending:
                        add_output(g - 1, 3)
                    if ahead is not None:
                        query_sum(g, ahead)

            def group(g, last):
                group_steps(g, range(1, NU + 1), False)
                if not last:
                    key_sums(g + 1, 0)
                transposed_low(g, NU - 1, (0, 1, 2))
                if not last:
                    key_sums(g + 1, 1)
                output_low(g, NU - 1)
                if not last:
                    keys_and_values(g + 1)
                for q in range(2):
                    add_output(g, q)
                if not last:
                    open_group(g + 1)
                add_output(g, 2)
                if not last:
                    query_sum(g + 1, 0)
                    group_steps(g + 1, (0,), True)
                else:
                    add_output(g, 3)

            ln["vector"](v)
            v.wait_ge(s["scale_in"], 32)
            v.tensor_tensor(kq_scale[:], scales[:, 0:1], scales[:, 1:2], ALU.mult).then_inc(s["scale_ready"], 1)
            v.sem_inc(s["acc_free"], 4)
            for b in range(B):
                key_sums(0, b)
            keys_and_values(0)
            open_group(0)
            query_sum(0, 0)
            group_steps(0, (0,), False)
            with v.Fori(0, NKV - 1) as g:
                v.wait_ge(s["acc_free"], g * 4 + 4)
                group(g, False)
            v.wait_ge(s["acc_free"], 4 * NKV)
            group(NKV - 1, True)

        @block.tensor
        def _(t):
            ln["tensor"](t, 0)

            def triple(dst, lhs, rhs, start, stop):
                (lh, ll), (rh, rl) = lhs, rhs
                for q, (l, r) in enumerate(((lh, rh), (ll, rh), (lh, rl))):
                    m = t.matmul(dst, l, r, start=start and q == 0, stop=stop and q == 2)
                return m

            def keys_and_values(g, banks):
                for q in banks:
                    for j in range(2):
                        tok = slice((2 * q + j) * P, (2 * q + j + 1) * P)
                        for k in range(KH):
                            m = triple(ps[KV_BANK[q]][:, j * 2 * HD:(j + 1) * 2 * HD],
                                       (xt_hi[:, k, tok], xt_lo[:, k, tok]),
                                       (wkv_hi[:, k, :], wkv_lo[:, k, :]), k == 0, k == KH - 1)
                    m.then_inc(s["kv_ready"], 1)

            def query(g, u):
                b, h = divmod(u, REP)
                if u >= 1:
                    t.wait_ge(s["qt_lo_done"], g * NU + u)
                tok = slice(b * C, (b + 1) * C)
                col = slice(h * HD, (h + 1) * HD)
                for k in range(KH):
                    m = triple(ps[Q_BANK][:], (wq_hi[:, k, col], wq_lo[:, k, col]),
                               (xt_hi[:, k, tok], xt_lo[:, k, tok]), k == 0, k == KH - 1)
                m.then_inc(s["q_ready"], 1)

            def query_sum(g, u):
                t.wait_ge(s["qsq_done"], g * NU + (u + 1))
                if u >= 1:
                    t.wait_ge(s["exp_done"], g * NU * NQ + (NQ * (u - 1) + 2))
                for j in range(NQ):
                    m = t.matmul(ps[1][:, QSUM_COL + j:QSUM_COL + j + 1], qsq[:, u % 2, j * P:(j + 1) * P],
                                 ones[:, 0:1], start=True, stop=True)
                m.then_inc(s["qsum_ready"], 1)

            def open_group(g):
                for b in range(B):
                    t.wait_ge(s["v_lo_done"], g * 4 + 2 * (b + 1))
                    for j in range(NQ):
                        m = t.transpose(ps[b][:, j * P:(j + 1) * P], kn[:, b * NQ + j, :], pm["ident"][:])
                    m.then_inc(s["kt_ready"], 1)
                t.wait_ge(s["wq_lo_done"], g + 1)
                query(g, 0)

            def group_steps(g, ks, last, pending=False):
                def scores(u):
                    b, sl = u // REP, u % 2
                    t.wait_ge(s["qt_lo_done"], g * NU + (u + 1))
                    for j in reversed(range(NQ)):
                        bank, col = S_BANK[j]
                        if u >= 1 and j >= 1:
                            done = NQ * (u - 1) + (NQ if j == 1 else NQ - j)
                            t.wait_ge(s["exp_done"], g * NU * NQ + done)
                        if j == 2:
                            t.wait_ge(s["qsum_done"], g * NU + (u + 1))
                        q = slice(j * P, (j + 1) * P)
                        n = P * (j + 1)
                        triple(ps[bank][:, col:col + n], (qt_hi[:, sl, q], qt_lo[:, sl, q]),
                               (kt_hi[:, b, 0:n], kt_lo[:, b, 0:n]), True, False)
                        t.matmul(ps[bank][:, col + n - P:col + n], pm["ident_b"][:], pm["causal"][:],
                                 start=False, stop=True).then_inc(s["s_ready"], 1)

                def transposes(u):
                    sl = u % 2
                    t.wait_ge(s["prob_done"], g * NU * NQ + NQ * (u + 1))
                    for i in range(NQ):
                        bank = T_BANK + min(i, 2)
                        if u >= 1 and i < 3:
                            t.wait_ge(s["pt_lo_done"], g * 3 * NU + (3 * (u - 1) + i + 1))
                        base = TOFF[i] - T_CUTS[min(i, 2)]
                        for j in range(i, NQ):
                            c = base + (j - i) * P
                            p0 = POFF[j] + i * P
                            m = t.transpose(ps[bank][:, c:c + P], prob[:, sl, p0:p0 + P], pm["ident"][:])
                        if i != 2:
                            m.then_inc(s["pt_ready"], 1)

                def values(u):
                    b, sl = u // REP, u % 2
                    if u >= 1:
                        t.wait_ge(s["ot_lo_done"], g * NU + u)
                    for i in range(NQ):
                        if i < 3:
                            t.wait_ge(s["pt_lo_done"], g * 3 * NU + (3 * u + i + 1))
                        src = slice(TOFF[i], TOFF[i + 1])
                        m = triple(ps[O_BANK][:, i * P:C], (v_hi[:, b * NQ + i, :], v_lo[:, b * NQ + i, :]),
                                   (pt_hi[:, sl, src], pt_lo[:, sl, src]), i == 0, i == NQ - 1)
                    m.then_inc(s["o_ready"], 1)

                for k in ks:
                    score, turn, value, ahead = steps_of(k)
                    if score is not None:
                        scores(score)
                    if ahead is not None:
                        query(g, ahead)
                    if pending:
                        project(g - 1, 3)
                    elif k == 0:
                        keep_busy(t, pm, ps[4], 8)
                    if k == NU - 1 and not last:
                        t.wait_ge(s["wkv_lo_done"], g + 2)
                        t.wait_ge(s["qt_lo_done"], g * NU + NU)
                        keys_and_values(g + 1, (0,))
                    if k == 1:
                        t.wait_ge(s["acc_free"], g * 4 + 4)
                    if k == NU and not last:
                        t.wait_ge(s["exp_done"], g * NU * NQ + NU * NQ)
                        keys_and_values(g + 1, (1, 2))
                    if value is not None:
                        values(value)
                    if turn is not None:
                        transposes(turn)
                    if ahead is not None:
                        query_sum(g, ahead)
                if NU in ks:
                    if not last:
                        keys_and_values(g + 1, (3,))
                    values(NU - 1)

            def project(g, q):
                b, j0 = divmod(2 * q, NQ)
                t.wait_ge(s["ot_lo_done"], g * NU + (REP * (b + 1)))
                for j in range(2):
                    tok = slice((j0 + j) * P, (j0 + j + 1) * P)
                    for h in range(REP):
                        m = triple(ps[Y_BANK + q][:, j * D:(j + 1) * D],
                                   (ot_hi[:, b * REP + h, tok], ot_lo[:, b * REP + h, tok]),
                                   (wo_hi[:, h, :], wo_lo[:, h, :]), h == 0, h == REP - 1)
                m.then_inc(s["y_ready"], 1)

            def group(g, last):
                group_steps(g, range(1, NU + 1), last)
                t.wait_ge(s["wo_lo_done"], g + 1)
                t.wait_ge(s["pt_lo_done"], g * 3 * NU + 3 * NU)
                project(g, 0)
                project(g, 1)
                if last:
                    project(g, 2)
                    project(g, 3)
                else:
                    open_group(g + 1)
                    project(g, 2)
                    t.wait_ge(s["kt_lo_done"], g * B + 2 * B)
                    query_sum(g + 1, 0)
                    group_steps(g + 1, (0,), False, pending=True)

            t.wait_ge(s["wkv_lo_done"], 1)
            t.wait_ge(xt_done, KH)
            keys_and_values(0, (0,))
            ln["tensor"](t, 1)
            keys_and_values(0, (1,))
            t.wait_ge(xt_done, 2 * KH)
            keys_and_values(0, (2, 3))
            keep_busy(t, pm, ps[4], 12)
            open_group(0)
            t.wait_ge(s["kt_lo_done"], B)
            keep_busy(t, pm, ps[4], 8)
            query_sum(0, 0)
            group_steps(0, (0,), False)
            with t.Fori(0, NKV - 1) as g:
                group(g, False)
            group(NKV - 1, True)


def build(nc, ins, out):
    with ExitStack() as ctx:
        cm = lambda n: ctx.enter_context(nc.semaphore(n))
        sb = lambda n, s, d: ctx.enter_context(nc.sbuf_tensor(n, s, d))
        ps = [ctx.enter_context(nc.psum_tensor(f"bank{i}", [P, 512], F32)) for i in range(8)]
        pm = {
            "X": sb("X", [P, NT, D], F32),
            "ident": sb("ident", [P, P], F32),
            "ident_b": sb("ident_b", [P, P], BF16),
            "causal": sb("causal", [P, P], BF16),
            "zeros": sb("zeros", [P, B * D], BF16),
            "ones": sb("ones", [P, 1], F32),
            "minus_half": sb("minus_half", [P, B * NCB], F32),
        }
        conv_phase(nc, cm, pm, ps, ins, ins["wconv"])
        ffn_phase(nc, cm, pm, ps, ins, "f1", None)
        attention_phase(nc, cm, pm, ps, ins)
        ffn_phase(nc, cm, pm, ps, ins, "f2", out)


def kernel(**inputs):
    import numpy as np
    import concourse.bacc as bacc
    from concourse.bass_utils import run_bass_kernel_spmd as run

    a = {k.replace("L0_", ""): np.asarray(v) for k, v in inputs.items()}
    routed13 = a["ffn_w13"].reshape(NE, 2, EI, KH, P)
    shared13 = a["ffn_sw13"].reshape(2, SI, KH, P)
    layouts = {
        "x": a["attn_a_x"],
        "cols": a["attn_a_cols"],
        "rows": a["attn_a_rows"],
        "wconv": a["attn_a_block_values"].reshape(NBLK, 2, HO, BS, NST, 2).transpose(4, 1, 0, 2, 5, 3)
                 .reshape(2 * NST, NBLK, HO * P),
        "gate_w": a["ffn_gate_w"].reshape(NE, KH, P).transpose(2, 1, 0).reshape(P, KH * NE),
        "w13": routed13.transpose(1, 2, 0, 3, 4).reshape(2, NRT, P, KH, P).transpose(1, 4, 3, 0, 2)
               .reshape(NRT, P, KH * 2 * P),
        "w2": a["ffn_w2"].transpose(2, 0, 1).reshape(NRT, P, D),
        "sw2": a["ffn_sw2"].T,
        "q_scale": a["attn_b_q_scale"],
        "k_scale": a["attn_b_k_scale"],
        "wqkv": np.concatenate([a["attn_b_Wq"].reshape(NKV, REP * HD, KH, P), a["attn_b_Wk"].reshape(NKV, HD, KH, P),
                                a["attn_b_Wv"].reshape(NKV, HD, KH, P)], axis=1).transpose(0, 3, 2, 1)
                .reshape(NKV, P, KH * (REP + 2) * HD),
        "wo": a["attn_b_Wo"].reshape(D, NKV, REP, HD).transpose(1, 3, 2, 0).reshape(NKV, HD, REP * D),
    }
    r0 = 0
    for m, rows in enumerate(SHARED):
        layouts[f"sw13_{m}"] = shared13[:, r0:r0 + rows].transpose(3, 2, 0, 1).reshape(P, KH * 2 * rows)
        r0 += rows

    nc = bacc.Bacc("TRN2", target_bir_lowering=False, num_devices=1)
    arrays, ins = {}, {}
    for name, value in layouts.items():
        value = np.ascontiguousarray(value)
        arrays[f"in_{name}"] = value
        ins[name] = nc.dram_tensor(f"in_{name}", value.shape, mybir.dt.from_np(value.dtype), kind="ExternalInput").ap()
    out = nc.dram_tensor("out", (B, C, D), F32, kind="ExternalOutput").ap()
    build(nc, ins, out)
    return run(nc, [arrays], core_ids=[0]).results[0]["out"]
```

```python
from contextlib import ExitStack

import concourse.bass as bass
from concourse import mybir

F32 = mybir.dt.float32
F32R = mybir.dt.float32r
BF16 = mybir.dt.bfloat16
I32 = mybir.dt.int32
ALU = mybir.AluOpType
ACT = mybir.ActivationFunctionType
AX_X = mybir.AxisListType.X

P = 128
B, C, D = 2, 512, 256
NT = B * C // P
GC = C // P
KH = D // P
NBLK, BS, KS = 128, 64, 16
NCB = C // BS
NST = KS // 2
HO = BS // 2
XPITCH = 272
NE, EI, TOPK = 16, 176, 6
NRT = NE * EI // P
SI = 2 * EI
SHARED = (SI - 2 * P, P, P)
NSH = len(SHARED)
NTILE = NSH + NRT
HALF = B * C // 2
HT = NT // 2
NH, NKV, HD = 16, 4, 128
REP = NH // NKV
NU = B * REP
NQ = C // P
POFF = [P * (j * (j + 1) // 2) for j in range(NQ + 1)]
TOFF = [P * sum(NQ - i for i in range(k)) for k in range(NQ + 1)]
FIRST_W2 = KH * 2 * SHARED[0]
LN_EPS = 1e-5
QK_EPS = 1e-6
MASKED = -1e30


def keep_busy(t, pm, bank, count):
    for _ in range(count):
        t.matmul(bank[:], pm["zeros"][:, 0:P], pm["zeros"][:], start=True, stop=True)


def layernorm_factors(tag, cm, pm):
    stats, moments, var_eps, rstd, X = (pm[n] for n in ("stats", "moments", "var_eps", "rstd", "X"))
    s = {n: cm(f"{tag}_{n}") for n in ("stats_done", "moments_done", "var_ready", "rstd_ready")}

    def statistics(v, tiles):
        for t in tiles:
            v.bn_stats(stats[:, t, :], X[:, t, :]).then_inc(s["stats_done"], 1)

    def variances(v, half, count):
        part = slice(half * HT, half * HT + HT)
        v.wait_ge(s["stats_done"], count)
        for t in range(half * HT, half * HT + HT):
            v.bn_aggr(moments[:, t, :], stats[:, t, :]).then_inc(s["moments_done"], 1)
        v.wait_ge(s["moments_done"], half * HT + HT)
        v.tensor_scalar(var_eps[:, part], moments[:, part, 1], LN_EPS, None, ALU.add).then_inc(s["var_ready"], 1)

    def powers(g, half):
        part = slice(half * HT, half * HT + HT)
        g.wait_ge(s["var_ready"], half + 1)
        g.tensor_tensor(rstd[:, part], var_eps[:, part], pm["minus_half"][:, part], ALU.pow)\
         .then_inc(s["rstd_ready"], 1)

    return dict(statistics=statistics, variances=variances, powers=powers, rstd_ready=s["rstd_ready"])


def layernorm_engines(tag, factors, early, busy, ctx, nc, cm, pm, ps):
    sb = lambda n, s, d: ctx.enter_context(nc.sbuf_tensor(f"{tag}_{n}", s, d))
    moments, rstd = pm["moments"], pm["rstd"]
    xn = sb("xn", [P, NT, D], F32)
    xt_hi, xt_lo = sb("xt_hi", [P, KH, B * C], F32R), sb("xt_lo", [P, KH, B * C], F32R)
    s = {n: cm(f"{tag}_{n}") for n in ("xn_ready", "xt_ready", "xt_hi_done", "xt_lo_done")}
    X = pm["X"]

    def vector(v, between=None):
        def normalize(half):
            v.wait_ge(factors["rstd_ready"], half + 1)
            for t in range(half * HT, half * HT + HT):
                v.tensor_scalar(xn[:, t, :], X[:, t, :], moments[:, t, 0:1], rstd[:, t:t + 1],
                                ALU.subtract, ALU.mult).then_inc(s["xn_ready"], 1)

        def low_half(half):
            for kh in range(KH):
                b = half * KH + kh
                v.wait_ge(s["xt_hi_done"], b + 1)
                dst = slice(half * HALF, half * HALF + HALF)
                v.tensor_tensor(xt_lo[:, kh, dst], ps[4 + b][:], xt_hi[:, kh, dst].bitcast(F32),
                                ALU.subtract).then_inc(s["xt_lo_done"], 1)

        normalize(0)
        if not early:
            factors["statistics"](v, range(HT, NT))
            factors["variances"](v, 1, NT)
        low_half(0)
        if between is not None:
            between()
        normalize(1)
        low_half(1)

    def tensor(t, half):
        if half == 0:
            keep_busy(t, pm, ps[0], busy[0])
        t.wait_ge(s["xn_ready"], HT * half + HT)
        for kh in range(KH):
            b = half * KH + kh
            for j in range(HT):
                m = t.transpose(ps[4 + b][:, j * P:(j + 1) * P], xn[:, HT * half + j, kh * P:(kh + 1) * P], pm["ident"][:])
            m.then_inc(s["xt_ready"], 1)
        if half == 0:
            keep_busy(t, pm, ps[0], busy[1])

    def scalar(a, halves=range(2)):
        for b in range(halves[0] * KH, halves[-1] * KH + KH):
            half, kh = divmod(b, KH)
            a.wait_ge(s["xt_ready"], b + 1)
            a.activation(xt_hi[:, kh, half * HALF:half * HALF + HALF], ps[4 + b][:], ACT.Copy)\
             .then_inc(s["xt_hi_done"], 1)

    return xt_hi, xt_lo, s["xt_hi_done"], s["xt_lo_done"], dict(vector=vector, tensor=tensor, scalar=scalar)


def conv_phase(nc, cm, pm, ps, ins, wconv, following, prefetch):
    with ExitStack() as ctx:
        sb = lambda n, s, d: ctx.enter_context(nc.sbuf_tensor(f"cv_{n}", s, d))
        x_dup = sb("x_dup", [P, B, NCB, D], F32)
        xc_hi, xc_lo = sb("xc_hi", [P, NCB, B, XPITCH], F32R), sb("xc_lo", [P, NCB, B, XPITCH], F32R)
        raw = [sb(f"raw{i}", [P, HO * P], F32) for i in range(4)]
        ws_hi = [sb(f"ws_hi{i}", [P, NCB * NCB, BS], F32R) for i in range(2)]
        ws_lo = [sb(f"ws_lo{i}", [P, NCB * NCB, BS], F32R) for i in range(2)]
        colrow = sb("colrow", [P, 2], I32)
        colrow_f = sb("colrow_f", [P, 2], F32)
        pair = sb("pair", [P, 1], F32)
        high = sb("high", [P, 1], F32)
        pair_iota, pair_iota_f = sb("pair_iota", [P, NCB * NCB], I32), sb("pair_iota_f", [P, NCB * NCB], F32)
        onehot = sb("onehot", [P, NCB * NCB], F32)
        ones = pm["ones"]
        zeros = pm["zeros"]
        any_high = sb("any_high", [1, 1], I32)
        stats, moments = sb("stats", [P, B * NCB, 6], F32), sb("moments", [P, B * NCB, 2], F32)
        var_eps, rstd = sb("var_eps", [P, B * NCB], F32), sb("rstd", [P, B * NCB], F32)
        s = {n: cm(f"cv_{n}") for n in (
            "x_in", "zeros_ready", "ones_ready", "xd_in", "cr_in", "iota_done", "const_done", "cr_conv", "pair_part", "pair_ready", "onehot_ready",
            "count_ready", "flag_ready", "stats_done", "moments_done", "var_ready", "rstd_ready", "xn_ready",
            "pads_ready", "xc_hi_done", "xc_lo_done", "summed", "ws_hi_done", "ws_lo_done", "ws_free", "conv_done",
            "x_added")}
        raw_in = [cm(f"cv_raw_in{i}") for i in range(4)]
        PARTS = (4, 2, 2, 2)
        first_in = [[cm(f"cv_first_in{i}_{q}") for q in range(n)] for i, n in enumerate(PARTS)]
        X = pm["X"]
        block = ctx.enter_context(nc.Block())
        WARM = 32
        BANKS = 4
        LAST_ORDER = (2, 3, 0, 1)
        OB = HO // BANKS

        @block.sync
        def _(sp):
            sp.dma_start(colrow[:, 0:1], ins["cols"].rearrange("(n a) -> n a", a=1)).then_inc(s["cr_in"], 16)
            sp.dma_start(colrow[:, 1:2], ins["rows"].rearrange("(n a) -> n a", a=1)).then_inc(s["cr_in"], 16)
            for b in range(B):
                for k in range(2):
                    sp.dma_start(x_dup[k * BS:(k + 1) * BS, b, :, :],
                                 ins["x"][b].rearrange("(c i) t -> i c t", i=BS)).then_inc(s["xd_in"], 16)
            for h in range(4):
                n = HO * P // PARTS[h]
                for q in range(PARTS[h]):
                    part = slice(q * n, (q + 1) * n)
                    sp.dma_start(raw[h][:, part], wconv[h][:, part]).then_inc(first_in[h][q], 16)
            with sp.Fori(1, NST // 2) as i:
                for h in range(4):
                    sp.wait_ge(s["summed"], i * 4 * BANKS + (h - 4 + 1) * BANKS)
                    sp.dma_start(raw[h][:], wconv[bass.ds(i * 4 + h, 1)].rearrange("a n f -> (a n) f"))\
                      .then_inc(raw_in[h], 16)
            sp.dma_start(X[:], ins["x"].rearrange("b (g p) t -> p (b g) t", p=P)).then_inc(s["x_in"], 16)
            prefetch[0](sp)

        @block.scalar
        def _(a):

            def round_input(b, k):
                a.wait_ge(s["pads_ready"], 2)
                a.wait_ge(s["xn_ready"], NCB * (b + 1))
                lo = KS - 1 - k
                a.activation(xc_hi[k * BS:(k + 1) * BS, :, b, lo:lo + D], x_dup[k * BS:(k + 1) * BS, b, :, :],
                             ACT.Copy).then_inc(s["xc_hi_done"], 1)

            def round_stage(st, slot, banks=range(2 * BANKS)):
                if 0 in banks:
                    a.wait_ge(s["ws_free"], st + 1)
                for q in banks:
                    a.wait_ge(s["summed"], st * 2 * BANKS + q + 1)
                    h, bk = divmod(q, BANKS)
                    o0 = h * HO + bk * OB
                    a.activation(ws_hi[slot][:, :, o0:o0 + OB].rearrange("p c o -> p o c"),
                                 ps[bk][:].rearrange("p (o c) -> p o c", o=OB), ACT.Copy)\
                     .then_inc(s["ws_hi_done"], 1)

            round_stage(0, 0, range(0, 4))
            round_input(0, 0)
            round_stage(0, 0, range(4, 5))
            round_input(0, 1)
            round_stage(0, 0, range(5, 7))
            round_input(1, 0)
            round_stage(0, 0, range(7, 8))
            round_stage(1, 1, range(0, 1))
            round_input(1, 1)
            round_stage(1, 1, range(1, 8))
            with a.Fori(1, NST // 2) as i:
                for u in range(2):
                    round_stage(i * 2 + u, u)

        def split_input(engine, b, k):
            lo = KS - 1 - k
            engine.wait_ge(s["xc_hi_done"], 2 * b + k + 1)
            engine.tensor_tensor(xc_lo[k * BS:(k + 1) * BS, :, b, lo:lo + D], x_dup[k * BS:(k + 1) * BS, b, :, :],
                                 xc_hi[k * BS:(k + 1) * BS, :, b, lo:lo + D].bitcast(F32),
                                 ALU.subtract).then_inc(s["xc_lo_done"], 1)

        @block.gpsimd
        def _(g):
            g.iota(pair_iota[:], pattern=[[1, NCB * NCB]], base=0, channel_multiplier=0).then_inc(s["iota_done"], 1)
            g.memset(pm["minus_half"][:], -0.5).then_inc(s["const_done"], 1)
            g.memset(pm["ident"][:], 0.0).then_inc(s["const_done"], 1)
            g.memset(pm["ident_b"][:], 0.0).then_inc(s["const_done"], 1)
            g.memset(pm["causal"][:], 0.0).then_inc(s["const_done"], 1)
            for x in (xc_hi, xc_lo):
                g.memset(x[:, :, :, 0:KS - 1].bitcast(F32), 0.0).then_inc(s["pads_ready"], 1)
            g.wait_ge(s["const_done"], 4)
            for m in (pm["ident"], pm["ident_b"]):
                g.affine_select(out=m[:], in_=m[:], compare_op=ALU.not_equal, fill=1.0, base=0,
                                pattern=[[-1, P]], channel_multiplier=1)
            g.affine_select(out=pm["causal"][:], in_=pm["causal"][:], compare_op=ALU.is_ge, fill=MASKED, base=0,
                            pattern=[[-1, P]], channel_multiplier=1)
            for b in range(B):
                part = slice(b * NCB, (b + 1) * NCB)
                g.wait_ge(s["var_ready"], b + 1)
                g.tensor_tensor(rstd[:, part], var_eps[:, part], pm["minus_half"][:, part], ALU.pow)\
                 .then_inc(s["rstd_ready"], 1)
            g.wait_ge(s["rstd_ready"], B)
            for b in range(B):
                split_input(g, b, 1)
            g.wait_ge(s["xc_lo_done"], 2 * B)
            following["powers"](g, 0)

        @block.vector
        def _(v):
            v.memset(zeros[:], 0.0).then_inc(s["zeros_ready"], 1)
            v.memset(ones[:], 1.0).then_inc(s["ones_ready"], 1)
            v.wait_ge(s["cr_in"], 32)
            v.tensor_copy(colrow_f[:], colrow[:]).then_inc(s["cr_conv"], 1)
            v.wait_ge(s["iota_done"], 1)
            v.tensor_copy(pair_iota_f[:], pair_iota[:]).then_inc(s["cr_conv"], 1)
            v.wait_ge(s["cr_conv"], 2)
            v.scalar_tensor_tensor(out=pair[:], in0=colrow_f[:, 0:1], scalar=float(NCB), in1=colrow_f[:, 1:2],
                                   op0=ALU.mult, op1=ALU.add).then_inc(s["pair_part"], 1)
            v.tensor_tensor(high[:], colrow_f[:, 0:1], colrow_f[:, 1:2], ALU.max).then_inc(s["pair_part"], 1)
            v.wait_ge(s["pair_part"], 2)
            v.tensor_scalar(onehot[:], pair_iota_f[:], pair[:, 0:1], None, ALU.is_equal).then_inc(s["onehot_ready"], 1)
            v.tensor_scalar(high[:], high[:], float(NCB // 2), None, ALU.is_ge).then_inc(s["pair_ready"], 1)
            v.wait_ge(s["count_ready"], 1)
            v.tensor_scalar(any_high[:], ps[0][0:1, 0:1], 0.5, None, ALU.is_ge).then_inc(s["flag_ready"], 1)

            def low_stage(st, slot, banks=range(2 * BANKS)):
                for q in banks:
                    v.wait_ge(s["ws_hi_done"], st * 2 * BANKS + q + 1)
                    h, bk = divmod(q, BANKS)
                    o0 = h * HO + bk * OB
                    v.tensor_tensor(ws_lo[slot][:, :, o0:o0 + OB].rearrange("p c o -> p o c"),
                                    ps[bk][:].rearrange("p (o c) -> p o c", o=OB),
                                    ws_hi[slot][:, :, o0:o0 + OB].bitcast(F32).rearrange("p c o -> p o c"),
                                    ALU.subtract).then_inc(s["ws_lo_done"], 1)

            v.wait_ge(s["xd_in"], 64)
            for b in range(B):
                tiles = range(b * NCB, (b + 1) * NCB)
                for n in tiles:
                    v.bn_stats(stats[:, n, :], x_dup[:, b, n % NCB, :]).then_inc(s["stats_done"], 1)
                for n in tiles:
                    v.wait_ge(s["stats_done"], n + 1)
                    v.bn_aggr(moments[:, n, :], stats[:, n, :]).then_inc(s["moments_done"], 1)
                v.wait_ge(s["moments_done"], (b + 1) * NCB)
                part = slice(b * NCB, (b + 1) * NCB)
                v.tensor_scalar(var_eps[:, part], moments[:, part, 1], LN_EPS, None, ALU.add)\
                 .then_inc(s["var_ready"], 1)
            low_stage(0, 0, range(3))
            for b in range(B):
                v.wait_ge(s["rstd_ready"], b + 1)
                for c in range(NCB):
                    n = b * NCB + c
                    v.tensor_scalar(x_dup[:, b, c, :], x_dup[:, b, c, :], moments[:, n, 0:1], rstd[:, n:n + 1],
                                    ALU.subtract, ALU.mult).then_inc(s["xn_ready"], 1)
                low_stage(0, 0, range(3 + b, 4 + b))
            low_stage(0, 0, range(5, 6))
            split_input(v, 0, 0)
            low_stage(0, 0, range(6, 8))
            split_input(v, 1, 0)
            low_stage(1, 1)
            with v.Fori(1, NST // 2) as i:
                for u in range(2):
                    low_stage(i * 2 + u, u)
            v.wait_ge(s["x_in"], 16)
            for n, r in enumerate(LAST_ORDER):
                v.wait_ge(s["conv_done"], n + 1)
                dst = X[:].rearrange("p (b g) t -> p g b t", b=B)[:, r]
                v.tensor_tensor(dst, dst, ps[4 + r][:].rearrange("p (b t) -> p b t", b=B), ALU.add)\
                 .then_inc(s["x_added"], 1)
                v.wait_ge(s["x_added"], n + 1)
                following["statistics"](v, [b * GC + r for b in range(B)])
            for half in range(2):
                following["variances"](v, half, NT)

        @block.tensor
        def _(t):
            t.wait_ge(s["zeros_ready"], 1)

            def open_accumulators(steps):
                for n in steps:
                    t.matmul(ps[4 + n % GC][:], zeros[:, 0:P], zeros[:], start=n < GC, stop=False)

            open_accumulators(range(2 * GC))
            t.wait_ge(s["pair_ready"], 1)
            t.wait_ge(s["ones_ready"], 1)
            t.matmul(ps[0][0:1, 0:1], high[:, 0:1], ones[:, 0:1], start=True, stop=True).then_inc(s["count_ready"], 1)
            open_accumulators(range(2 * GC, WARM))
            t.sem_inc(s["ws_free"], 2)

            def sum_blocks(st, slot, use, first):
                for h in range(2):
                    if use is not None:
                        t.wait_ge(raw_in[2 * slot + h], 16 * use)
                    for bk in range(BANKS):
                        if use is None:
                            t.wait_ge(first_in[2 * slot + h][bk * PARTS[2 * slot + h] // BANKS], 16)
                        if not (first and h == 0):
                            t.wait_ge(s["ws_lo_done"], st * 2 * BANKS + (h - 1) * BANKS + bk + 1)
                        for o in range(OB):
                            w0 = (bk * OB + o) * P
                            m = t.matmul(ps[bk][:, o * NCB * NCB:(o + 1) * NCB * NCB],
                                         raw[2 * slot + h][:, w0:w0 + P], onehot[:], start=True, stop=True)
                        m.then_inc(s["summed"], 1)

            def products(slot, c, r, tap):
                w = c * NCB + 2 * r
                hi, lo = (x[:, c, :, bass.ds(tap, D)] for x in (xc_hi, xc_lo))
                w_hi, w_lo = (x[slot][:, w:w + 2, :].rearrange("p c o -> p (c o)") for x in (ws_hi, ws_lo))
                for lhs, rhs in ((w_hi, hi), (w_lo, hi), (w_hi, lo)):
                    t.matmul(ps[4 + r][:], lhs, rhs, start=False, stop=False)

            def convolve(st, slot, last=False):
                t.wait_ge(s["ws_lo_done"], (st + 1) * 2 * BANKS)
                with t.If(flag != 0):
                    for c in range(NCB):
                        for r in range(GC):
                            if c >= NCB // 2 or r >= GC // 2:
                                products(slot, c, r, st * 2)
                if not last:
                    for c in range(NCB // 2):
                        for r in range(GC // 2):
                            products(slot, c, r, st * 2)
                else:
                    for r in LAST_ORDER:
                        if r < GC // 2:
                            for c in range(NCB // 2):
                                products(slot, c, r, st * 2)
                        t.matmul(ps[4 + r][:], zeros[:, 0:P], zeros[:], start=False,
                                 stop=True).then_inc(s["conv_done"], 1)

            t.wait_ge(s["onehot_ready"], 1)
            t.wait_ge(s["flag_ready"], 1)
            sum_blocks(0, 0, None, True)
            sum_blocks(1, 1, None, False)
            flag = t.value_load(any_high[0:1, 0:1], min_val=0, max_val=1)
            t.wait_ge(s["xc_lo_done"], 2 * B)
            with t.Fori(0, NST // 2 - 1) as i:
                for u in range(2):
                    convolve(i * 2 + u, u)
                    t.sem_inc(s["ws_free"], 1)
                    sum_blocks(i * 2 + u + 2, u, i + 1, False)
            for u in range(2):
                convolve(NST - 2 + u, u, last=u == 1)
            keep_busy(t, pm, ps[1], 8)


def ffn_phase(nc, cm, pm, ps, ins, tag, factors, early, prefetched, following, prefetch, out):
    with ExitStack() as ctx:
        sb = lambda n, s, d: ctx.enter_context(nc.sbuf_tensor(f"{tag}_{n}", s, d))
        xt_hi, xt_lo, xt_hi_done, xt_done, ln = layernorm_engines(tag, factors, early, (8, 4), ctx, nc, cm, pm, ps)
        WC = KH * 2 * P
        wraw = [sb(f"wraw{i}", [P, WC + D], F32) for i in range(2)]
        w_hi = [sb(f"w_hi{i}", [P, WC + D], F32R) for i in range(2)]
        w_lo = [sb(f"w_lo{i}", [P, WC + D], F32R) for i in range(2)]
        gw, gw_hi, gw_lo = pm["gate_w"], sb("gw_hi", [P, KH, NE], F32R), sb("gw_lo", [P, KH, NE], F32R)
        act = [sb(f"act{i}", [P, HALF], F32) for i in range(2)]
        scaled = [sb(f"scaled{i}", [P, HALF], F32) for i in range(2)]
        h_f = [sb(f"h{i}", [P, HALF], F32) for i in range(2)]
        h_hi = [sb(f"h_hi{i}", [P, HALF], F32R) for i in range(4)]
        h_lo = [sb(f"h_lo{i}", [P, HALF], F32R) for i in range(4)]
        gate_rows = sb("gate_rows", [P, B * C], F32)
        lmax, lsh, lexp = sb("lmax", [P, NT], F32), sb("lsh", [P, NT, NE], F32), sb("lexp", [P, NT, NE], F32)
        lsum, lrec = sb("lsum", [P, NT], F32), sb("lrec", [P, NT], F32)
        NEP = NE + 2
        prob, rest = sb("prob", [P, NT, NEP], F32), sb("rest", [P, NT, NEP], F32)
        top8 = sb("top8", [P, NT, 8], F32)
        sel, ssum, srec = sb("sel", [P, NT, NE], F32), sb("ssum", [P, NT], F32), sb("srec", [P, NT], F32)
        logits_t = sb("logits_t", [NE, B * C], F32)
        comb = sb("comb", [P, NT, P // NE, NE], F32)
        s = {n: cm(f"{tag}_{n}") for n in (
            "gw_hi_done", "gw_lo_done", "w13_hi_done", "w13_lo_done", "w2_hi_done", "w2_lo_done",
            "sentinels_ready", "gate_t", "gate_a", "gate_v", "comb_ready", "gate_rows_ready", "gu_ready", "act_done",
            "scaled_done", "h_ready", "h_hi_done", "h_lo_done", "down_done", "y_ready", "x_added", "out_done")}
        LOGITS_T, LOGITS, TOKEN_WEIGHTS = 0, 2, 3
        LOGITS_COPIED, EXPONENTS = 0, 3
        SHIFTED = 2
        w_in = [cm(f"{tag}_w_in{i}") for i in range(2)]
        X = pm["X"]
        pg, pu, py = ps[0:4:2], ps[1:4:2], ps[4:8]
        block = ctx.enter_context(nc.Block())

        @block.sync
        def _(sp):
            def load(m, slot, w13, w2, rows):
                sp.dma_start(wraw[slot][:, 0:KH * 2 * rows], w13).then_inc(w_in[slot], 16)
                sp.dma_start(wraw[slot][0:rows, WC:WC + D], w2).then_inc(w_in[slot], 16)

            r0 = SHARED[0]
            for m in range(1, NSH):
                rows = SHARED[m]
                load(m, m % 2, ins[f"sw13_{m}"], ins["sw2"][r0:r0 + rows, :], rows)
                r0 += rows
            if prefetch is not None:
                sp.wait_ge(s["w2_lo_done"], 1)
                prefetch[0](sp)
            with sp.Fori(0, NRT // 2) as i:
                for u in range(2):
                    sp.wait_ge(s["w2_lo_done"], i * 2 + (NSH + u - 1))
                    load(None, (NSH + u) % 2, ins["w13"][bass.ds(i * 2 + u, 1)].rearrange("a p f -> (a p) f"),
                         ins["w2"][bass.ds(i * 2 + u, 1)].rearrange("a p f -> (a p) f"), P)
            if out is not None:
                for q in range(4):
                    sp.wait_ge(s["x_added"], q + 1)
                    b, g0 = divmod(2 * q, GC)
                    sp.dma_start(out[b].rearrange("(g p) t -> p g t", p=P)[:, g0:g0 + 2, :],
                                 X[:, 2 * q:2 * q + 2, :]).then_inc(s["out_done"], 16)
                sp.wait_ge(s["out_done"], 64)

        def weight_views(slot, rows):
            v13 = [x[slot][:, 0:KH * 2 * rows].rearrange("p (k g f) -> p k g f", k=KH, g=2) for x in (w_hi, w_lo)]
            v2 = [x[slot][0:rows, WC:WC + D] for x in (w_hi, w_lo)]
            return v13, v2

        def columns(part):
            return (slice(0, HALF), 0) if part is None else (slice(part * HALF // 2, (part + 1) * HALF // 2), part)

        def raw_views(m, slot, rows):
            if isinstance(m, int) and m == 0:
                return pm["first_w"][:, 0:FIRST_W2], pm["first_w"][0:rows, FIRST_W2:FIRST_W2 + D]
            return wraw[slot][:, 0:KH * 2 * rows], wraw[slot][0:rows, WC:WC + D]

        @block.scalar
        def _(a):
            prefetched[1](a)
            a.activation(gw_hi[:].rearrange("p k e -> p (k e)"), gw[:], ACT.Copy).then_inc(s["gw_hi_done"], 1)

            def round_w13(m, slot, use, rows, reuse):
                if use is not None:
                    a.wait_ge(w_in[slot], 32 * (use - (slot == 0)))
                if reuse:
                    a.wait_ge(s["gu_ready"], 2 * m - 2)
                a.activation(w_hi[slot][:, 0:KH * 2 * rows], raw_views(m, slot, rows)[0], ACT.Copy)\
                 .then_inc(s["w13_hi_done"], 1)

            def round_w2(m, slot, rows, reuse):
                if reuse:
                    a.wait_ge(s["down_done"], 2 * m - 2)
                a.activation(w_hi[slot][0:rows, WC:WC + D], raw_views(m, slot, rows)[1], ACT.Copy)\
                 .then_inc(s["w2_hi_done"], 1)

            def silu(n, half, rows, reuse, part=None):
                cols, _ = columns(part)
                a.wait_ge(s["gu_ready"], n + 1)
                if reuse:
                    a.wait_ge(s["h_ready"], n - 1)
                a.activation(act[half][0:rows, cols], pg[half][0:rows, cols], ACT.Silu).then_inc(s["act_done"], 1)

            def round_h(n, half, slot, rows, reuse, part=None):
                cols, k = columns(part)
                a.wait_ge(s["h_ready"], n + 1 + k)
                if reuse:
                    a.wait_ge(s["down_done"], n - 3)
                a.activation(h_hi[slot][0:rows, cols], h_f[half][0:rows, cols], ACT.Copy).then_inc(s["h_hi_done"], 1)

            def tile(m, par, u0, next_use, rows, next_rows, opened=False):
                if not opened:
                    silu(2 * m, 0, rows, not isinstance(m, int) or m >= 1)
                if next_use is not None and not opened:
                    round_w13(m + 1, 1 - par, next_use, next_rows, not isinstance(m, int) or m >= 1)
                round_h(2 * m, 0, u0, rows, not isinstance(m, int) or m >= 2)
                round_w2(m, par, rows, not isinstance(m, int) or m >= 2)
                if next_use is None:
                    for part in range(2):
                        silu(2 * m + 1, 1, rows, True, part)
                    for part in range(2):
                        round_h(2 * m + 1, 1, u0 + 1, rows, True, part)
                    return
                silu(2 * m + 1, 1, rows, not isinstance(m, int) or m >= 1)
                if isinstance(m, int) and m == NSH - 1:
                    a.wait_ge(s["gate_t"], TOKEN_WEIGHTS + 1)
                    a.activation(gate_rows[:, 0:HALF], pg[0][:], ACT.Copy).then_inc(s["gate_rows_ready"], 1)
                round_h(2 * m + 1, 1, u0 + 1, rows, not isinstance(m, int) or m >= 2)

            rows_of = list(SHARED) + [P] * NRT
            round_w13(0, 0, None, rows_of[0], False)
            ln["scalar"](a)
            silu(0, 0, rows_of[0], False)
            round_w13(1, 1, 1, rows_of[1], False)
            for half in range(2):
                a.wait_ge(s["gate_t"], LOGITS_T + half + 1)
                a.activation(logits_t[:, half * HALF:(half + 1) * HALF], py[half][0:NE, :], ACT.Copy)\
                 .then_inc(s["gate_a"], 1)
            for m in range(NSH):
                if m == 1:
                    a.wait_ge(s["gate_v"], SHIFTED)
                    a.activation(lexp[:], lsh[:], ACT.Exp).then_inc(s["gate_a"], 1)
                tile(m, m % 2, 2 * (m % 2), (m + 1) // 2 + 1, rows_of[m], rows_of[m + 1], opened=m == 0)
            with a.Fori(0, NRT // 2 - 1) as i:
                for u in range(2):
                    par = (NSH + u) % 2
                    tile(i * 2 + (NSH + u), par, 2 * par, i + ((NSH + u + 1) // 2 + 1), P, P)
            for m in range(NTILE - 2, NTILE):
                tile(m, m % 2, 2 * (m % 2), (m + 1) // 2 + 1 if m + 1 < NTILE else None, P, P)

        @block.gpsimd
        def _(g):
            g.memset(prob[:], -1.0).then_inc(s["sentinels_ready"], 1)

            def low_w13(m, slot, rows):
                g.wait_ge(s["w13_hi_done"], m + 1)
                n = KH * 2 * rows
                g.tensor_tensor(w_lo[slot][:, 0:n], raw_views(m, slot, rows)[0], w_hi[slot][:, 0:n].bitcast(F32),
                                ALU.subtract).then_inc(s["w13_lo_done"], 1)

            def low_w2(m, slot, rows):
                g.wait_ge(s["w2_hi_done"], m + 1)
                g.tensor_tensor(w_lo[slot][0:rows, WC:WC + D], raw_views(m, slot, rows)[1],
                                w_hi[slot][0:rows, WC:WC + D].bitcast(F32), ALU.subtract)\
                 .then_inc(s["w2_lo_done"], 1)

            def scale(n, half, part=None):
                cols, k = columns(part)
                g.wait_ge(s["act_done"], n + 1 + k)
                g.tensor_tensor(scaled[half][:, cols], act[half][:, cols],
                                gate_rows[:, half * HALF + cols.start:half * HALF + cols.stop],
                                ALU.mult).then_inc(s["scaled_done"], 1)

            def tile(m, par, routed, has_next, rows, next_rows):
                if routed:
                    scale(2 * m, 0)
                if has_next:
                    low_w13(m + 1, 1 - par, next_rows)
                low_w2(m, par, rows)
                if routed and has_next:
                    scale(2 * m + 1, 1)
                elif routed:
                    for part in range(2):
                        scale(2 * m + 1, 1, part)

            rows_of = list(SHARED) + [P] * NRT
            low_w13(0, 0, rows_of[0])
            factors["powers"](g, 1)
            for m in range(NSH):
                tile(m, m % 2, False, True, rows_of[m], rows_of[m + 1])
            g.wait_ge(s["gate_rows_ready"], 2)
            with g.Fori(0, NRT // 2 - 1) as i:
                for u in range(2):
                    tile(i * 2 + (NSH + u), (NSH + u) % 2, True, True, P, P)
            for m in range(NTILE - 2, NTILE):
                tile(m, m % 2, True, m + 1 < NTILE, P, P)
            if following is not None:
                following["powers"](g, 0)

        @block.vector
        def _(v):
            def low_gate_weights():
                v.wait_ge(s["gw_hi_done"], 1)
                v.tensor_tensor(gw_lo[:].rearrange("p k e -> p (k e)"), gw[:],
                                gw_hi[:].rearrange("p k e -> p (k e)").bitcast(F32), ALU.subtract)\
                 .then_inc(s["gw_lo_done"], 1)

            ln["vector"](v, low_gate_weights)
            step = s["gate_v"]

            def spread(x, n=NE):
                return x[:].unsqueeze(2).to_broadcast([P, NT, n])

            def gate_shift():
                v.wait_ge(s["gate_t"], LOGITS + 1)
                logits = py[3][:, 0:NT * NE].rearrange("p (t e) -> p t e", t=NT)
                v.tensor_reduce(lmax[:], logits, AX_X, ALU.max).then_inc(step, 1)
                v.wait_ge(step, 1)
                v.tensor_tensor(lsh[:], logits, spread(lmax), ALU.subtract).then_inc(step, 1)

            def gate_softmax():
                v.wait_ge(s["gate_a"], EXPONENTS)
                v.tensor_reduce(lsum[:], lexp[:], AX_X, ALU.add).then_inc(step, 1)
                v.wait_ge(step, 3)
                v.reciprocal(lrec[:], lsum[:]).then_inc(step, 1)
                v.wait_ge(step, 4)
                v.wait_ge(s["sentinels_ready"], 1)
                v.tensor_tensor(prob[:, :, 0:NE], lexp[:], spread(lrec), ALU.mult).then_inc(step, 1)
                v.wait_ge(step, 5)
                for t in range(NT):
                    v.max(top8[:, t, :], prob[:, t, 0:NE]).then_inc(step, 1)

            def gate_select():
                v.wait_ge(step, 5 + NT)
                v.memset(top8[:, :, TOPK:8], -1.0).then_inc(step, 1)
                v.wait_ge(step, 6 + NT)
                for t in range(NT):
                    v.match_replace(out=rest[:, t, :], in_to_replace=top8[:, t, :], in_values=prob[:, t, :],
                                    imm_value=0.0).then_inc(step, 1)
                v.wait_ge(step, 6 + 2 * NT)
                v.tensor_tensor(sel[:], prob[:, :, 0:NE], rest[:, :, 0:NE], ALU.subtract).then_inc(step, 1)

            def gate_weights():
                v.wait_ge(step, 7 + 2 * NT)
                v.tensor_reduce(ssum[:], sel[:], AX_X, ALU.add).then_inc(step, 1)
                v.wait_ge(step, 8 + 2 * NT)
                v.tensor_scalar(ssum[:], ssum[:], 1e-20, None, ALU.add).then_inc(step, 1)
                v.wait_ge(step, 9 + 2 * NT)
                v.reciprocal(srec[:], ssum[:]).then_inc(step, 1)
                v.wait_ge(step, 10 + 2 * NT)
                v.tensor_tensor(sel[:], sel[:], spread(srec), ALU.mult).then_inc(step, 1)
                v.wait_ge(step, 11 + 2 * NT)
                v.tensor_copy(comb[:], sel[:].unsqueeze(2).to_broadcast([P, NT, P // NE, NE]))\
                 .then_inc(s["comb_ready"], 1)

            def unit(n, half, slot, rows, routed, part=None):
                cols, k = columns(part)
                if routed:
                    v.wait_ge(s["scaled_done"], n - (2 * NSH - 1) + k)
                    src = scaled
                else:
                    v.wait_ge(s["act_done"], n + 1)
                    src = act
                if not isinstance(n, int) or n >= 2:
                    v.wait_ge(s["h_hi_done"], n - 1)
                    v.wait_ge(s["h_lo_done"], n - 1)
                v.tensor_tensor(h_f[half][0:rows, cols], src[half][0:rows, cols], pu[half][0:rows, cols], ALU.mult)\
                 .then_inc(s["h_ready"], 1)
                if part is None:
                    low_hidden(n, half, slot, rows)

            def low_hidden(n, half, slot, rows, part=None):
                cols, k = columns(part)
                v.wait_ge(s["h_hi_done"], n + 1 + k)
                v.wait_ge(s["h_ready"], n + 1 + k)
                v.tensor_tensor(h_lo[slot][0:rows, cols], h_f[half][0:rows, cols],
                                h_hi[slot][0:rows, cols].bitcast(F32), ALU.subtract).then_inc(s["h_lo_done"], 1)

            unit(0, 0, 0, SHARED[0], False)
            unit(1, 1, 1, SHARED[0], False)
            gate_shift()
            gate_softmax()
            unit(2, 0, 2, SHARED[1], False)
            gate_select()
            unit(3, 1, 3, SHARED[1], False)
            gate_weights()
            for n in range(4, 2 * NSH - 1):
                unit(n, n % 2, n % 4, SHARED[n // 2], False)
            v.wait_ge(s["gate_t"], TOKEN_WEIGHTS + 2)
            v.tensor_copy(gate_rows[:, HALF:2 * HALF], pu[0][:]).then_inc(s["gate_rows_ready"], 1)
            unit(2 * NSH - 1, 1, (2 * NSH - 1) % 4, SHARED[NSH - 1], False)
            with v.Fori(0, NRT // 2 - 1) as i:
                for k in range(4):
                    n = 2 * NSH + k
                    unit(i * 4 + n, n % 2, n % 4, P, True)
            last = 2 * NTILE - 1
            for n in range(last - 3, last):
                unit(n, n % 2, n % 4, P, True)
            for part in range(2):
                unit(last, last % 2, last % 4, P, True, part)
            for part in range(2):
                low_hidden(last, last % 2, last % 4, P, part)
            for q in range(4):
                v.wait_ge(s["y_ready"], q + 1)
                dst = X[:, 2 * q:2 * q + 2, :].rearrange("p t d -> p (t d)")
                v.tensor_tensor(dst, dst, py[q][:], ALU.add).then_inc(s["x_added"], 1)
                if q == 1 and following is not None:
                    v.wait_ge(s["x_added"], 2)
                    following["statistics"](v, range(HT))
                    following["variances"](v, 0, HT)

        @block.tensor
        def _(t):

            def gate_logits(half):
                tok = slice(half * HALF, (half + 1) * HALF)
                steps = [(w[:, k, :], x[:, k, tok]) for k in range(KH)
                         for w, x in ((gw_hi, xt_hi), (gw_lo, xt_hi), (gw_hi, xt_lo))]
                for q, (w, x) in enumerate(steps):
                    m = t.matmul(py[half][0:NE, :], w, x, start=q == 0, stop=q == len(steps) - 1)
                m.then_inc(s["gate_t"], 1)

            def turn_logits():
                t.wait_ge(s["gate_a"], LOGITS_COPIED + 2)
                for tt in range(NT):
                    m = t.transpose(py[3][:, tt * NE:(tt + 1) * NE], logits_t[:, tt * P:(tt + 1) * P],
                                    pm["ident"][0:NE, 0:NE])
                m.then_inc(s["gate_t"], 1)

            def gate_weights():
                t.wait_ge(s["comb_ready"], 1)
                t.wait_ge(s["h_ready"], 2 * NSH - 1)
                for half, bank in enumerate((pg[0], pu[0])):
                    for j in range(4):
                        mm = t.transpose(bank[:, j * P:(j + 1) * P],
                                         comb[:, 4 * half + j, :, :].rearrange("p r e -> p (r e)"), pm["ident"][:])
                    mm.then_inc(s["gate_t"], 1)

            def gate_up(n, half, m, slot, rows, reuse):
                if half == 0:
                    t.wait_ge(s["w13_lo_done"], m + 1)
                if reuse:
                    t.wait_ge(s["h_ready"], n - 1)
                (vhi, vlo), _ = weight_views(slot, rows)
                tok = slice(half * HALF, (half + 1) * HALF)
                for gu, bank in enumerate((pg, pu)):
                    steps = [(w[:, k, gu, :], xt_hi[:, k, tok]) for k in range(KH) for w in (vhi, vlo)]
                    steps += [(vhi[:, k, gu, :], xt_lo[:, k, tok]) for k in range(KH)]
                    for q, (w, x) in enumerate(steps):
                        if gu == 0 and isinstance(n, int) and n < 2 and q in (0, 2 * KH):
                            t.wait_ge(xt_hi_done if q == 0 else xt_done, KH * (n + 1))
                        mm = t.matmul(bank[half][0:rows, :], w, x, start=q == 0, stop=q == len(steps) - 1)
                mm.then_inc(s["gu_ready"], 1)

            def down(n, half, m, slot, hslot, rows, first, last):
                if half == 0:
                    t.wait_ge(s["w2_lo_done"], m + 1)
                in_parts = last and n == 2 * NTILE - 1
                if not in_parts:
                    t.wait_ge(s["h_lo_done"], n + 1)
                _, (vhi, vlo) = weight_views(slot, rows)
                for j in range(4):
                    if in_parts and j % 2 == 0:
                        t.wait_ge(s["h_lo_done"], n + 1 + j // 2)
                    tok = slice(j * P, (j + 1) * P)
                    bank = py[2 * half + j // 2][:, (j % 2) * D:(j % 2 + 1) * D]
                    trio = ((h_hi, vhi), (h_lo, vhi), (h_hi, vlo))
                    for q, (h, w) in enumerate(trio):
                        mm = t.matmul(bank, h[hslot][0:rows, tok], w, start=first and q == 0 and j % 2 == 0,
                                      stop=last and q == 2, skip_group_check=True)
                    if last and j % 2:
                        mm.then_inc(s["y_ready"], 1)
                if not last:
                    mm.then_inc(s["down_done"], 1)

            ln["tensor"](t, 0)
            for n in range(2 * NSH):
                gate_up(n, n % 2, n // 2, (n // 2) % 2, SHARED[n // 2], n >= 2)
                if n == 0:
                    ln["tensor"](t, 1)
                    t.wait_ge(s["gw_lo_done"], 1)
                    gate_logits(0)
                    t.wait_ge(xt_done, 2 * KH)
                    gate_logits(1)
                if n == 1:
                    turn_logits()
                if n == 3:
                    t.wait_ge(s["gate_v"], SHIFTED)
                if n == 2 * NSH - 1:
                    gate_weights()
                if n >= 2:
                    down(n - 2, n % 2, n // 2 - 1, (n // 2 - 1) % 2, (n - 2) % 4, SHARED[n // 2 - 1], n < 4, False)
            t.wait_ge(s["gate_rows_ready"], 2)
            with t.Fori(0, NRT // 2) as i:
                for k in range(4):
                    n, d = 2 * NSH + k, 2 * NSH + k - 2
                    gate_up(i * 4 + n, n % 2, i * 2 + n // 2, (n // 2) % 2, P, True)
                    down(i * 4 + d, d % 2, i * 2 + d // 2, (d // 2) % 2, d % 4, P, False, False)
            for n in range(2 * NTILE - 2, 2 * NTILE):
                down(n, n % 2, n // 2, (n // 2) % 2, n % 4, P, False, True)
            if following is not None:
                keep_busy(t, pm, ps[1], 8)


def attention_phase(nc, cm, pm, ps, ins, factors, prefetched, following, prefetch):
    with ExitStack() as ctx:
        sb = lambda n, s, d: ctx.enter_context(nc.sbuf_tensor(f"at_{n}", s, d))
        xt_hi, xt_lo, _, xt_done, ln = layernorm_engines("at", factors, False, (8, 9), ctx, nc, cm, pm, ps)
        GW = (REP + 2) * HD
        wraw = sb("wraw", [P, KH * GW], F32)
        wq_hi, wq_lo = sb("wq_hi", [P, KH, REP * HD], F32R), sb("wq_lo", [P, KH, REP * HD], F32R)
        wkv_hi, wkv_lo = sb("wkv_hi", [P, KH, 2 * HD], F32R), sb("wkv_lo", [P, KH, 2 * HD], F32R)
        oraw = sb("oraw", [P, REP * D], F32)
        wo_hi, wo_lo = sb("wo_hi", [P, REP, D], F32R), sb("wo_lo", [P, REP, D], F32R)
        scales, kq_scale = sb("scales", [P, 2], F32), sb("kq_scale", [P, 1], F32)
        ones = pm["ones"]
        ksum, ksum_eps, krs = sb("ksum", [P, NT], F32), sb("ksum_eps", [P, NT], F32), sb("krs", [P, NT], F32)
        ksq = sb("ksq", [P, NT, HD], F32)
        kn = sb("kn", [P, NT, HD], F32)
        kt_hi, kt_lo = sb("kt_hi", [P, B, C], F32R), sb("kt_lo", [P, B, C], F32R)
        v_hi, v_lo = sb("v_hi", [P, NT, HD], F32R), sb("v_lo", [P, NT, HD], F32R)
        qt_hi, qt_lo = sb("qt_hi", [P, 2, C], F32R), sb("qt_lo", [P, 2, C], F32R)
        qsq = sb("qsq", [P, 2, C], F32)
        qsum, qrs = sb("qsum", [P, 2, NQ], F32), sb("qrs", [P, 2, NQ], F32)
        smax, sbias = sb("smax", [P, 2, NQ], F32), sb("sbias", [P, 2, NQ], F32)
        rsum, rrec = sb("rsum", [P, 2, NQ], F32), sb("rrec", [P, 2, NQ], F32)
        prob = sb("prob", [P, 2, POFF[NQ]], F32)
        pt_hi, pt_lo = sb("pt_hi", [P, 2, TOFF[NQ]], F32R), sb("pt_lo", [P, 2, TOFF[NQ]], F32R)
        ot_hi, ot_lo = sb("ot_hi", [P, NU, C], F32R), sb("ot_lo", [P, NU, C], F32R)
        s = {n: cm(f"at_{n}") for n in (
            "scale_in", "scale_ready", "w_in", "o_in", "acc_free", "wq_hi_done", "wq_lo_done", "wkv_hi_done", "wkv_lo_done",
            "wo_hi_done", "wo_lo_done", "kv_ready", "ksum_done", "ksum_eps_done", "krs_done", "kn_done", "kt_ready",
            "kt_hi_done", "kt_lo_done", "v_hi_done", "v_lo_done", "q_ready", "qsq_done", "qt_hi_done", "qt_lo_done",
            "qsum_ready", "qsum_done", "qrs_done", "s_ready", "max_done", "bias_done", "exp_done", "rec_done",
            "prob_done", "pt_ready", "pt_hi_done", "pt_lo_done", "o_ready", "ot_hi_done", "ot_lo_done", "y_ready")}
        X = pm["X"]
        raw_q = wraw[:].rearrange("p (k f) -> p k f", k=KH)[:, :, 0:REP * HD]
        first_kv = pm["first_w"][:, 0:KH * 2 * HD].rearrange("p (k f) -> p k f", k=KH)
        raw_kv = wraw[:].rearrange("p (k f) -> p k f", k=KH)[:, :, REP * HD:GW]
        S_BANK = ((0, 0), (0, P), (1, 0), (2, 0))
        QSUM_COL = 3 * P
        Q_BANK, T_BANK, O_BANK = 3, 4, 7
        Y_BANKS = {False: (4, 5, 6, 7), True: (3, 0, 6, 7)}
        KV_BANK = (3, 0, 1, 2)
        T_CUTS = (0, TOFF[1], TOFF[2], TOFF[4])
        block = ctx.enter_context(nc.Block())

        def steps_of(k):
            return (k if k < NU else None, k - 1 if 1 <= k <= NU else None, k - 2 if 2 <= k <= NU else None,
                    k + 1 if k + 1 < NU else None)

        @block.sync
        def _(sp):
            sp.dma_start(raw_q, ins["wqkv"][0].rearrange("p (k f) -> p k f", k=KH)[:, :, 0:REP * HD])\
              .then_inc(s["w_in"], 16)
            sp.dma_start(scales[:, 0:1], ins["q_scale"].rearrange("(d a) -> d a", a=1)).then_inc(s["scale_in"], 16)
            sp.dma_start(scales[:, 1:2], ins["k_scale"].rearrange("(d a) -> d a", a=1)).then_inc(s["scale_in"], 16)
            sp.dma_start(oraw[:], ins["wo"][0]).then_inc(s["o_in"], 16)
            sp.wait_ge(s["wkv_lo_done"], 1)
            prefetch[0](sp)
            with sp.Fori(1, NKV) as g:
                sp.wait_ge(s["wq_lo_done"], g)
                sp.dma_start(wraw[:], ins["wqkv"][bass.ds(g, 1)].rearrange("a p f -> (a p) f")).then_inc(s["w_in"], 16)
                sp.wait_ge(s["wo_lo_done"], g)
                sp.dma_start(oraw[:], ins["wo"][bass.ds(g, 1)].rearrange("a p f -> (a p) f")).then_inc(s["o_in"], 16)

        @block.scalar
        def _(a):
            def round_kv_weights(g):
                if isinstance(g, int):
                    prefetched[1](a)
                else:
                    a.wait_ge(s["w_in"], g * 16 + 16)
                a.activation(wkv_hi[:], first_kv if isinstance(g, int) else raw_kv, ACT.Copy).then_inc(s["wkv_hi_done"], 1)

            def round_q_weights(g):
                if isinstance(g, int):
                    a.wait_ge(s["w_in"], 16)
                a.activation(wq_hi[:], raw_q, ACT.Copy).then_inc(s["wq_hi_done"], 1)

            def square_keys(g, banks):
                for q in banks:
                    a.wait_ge(s["kv_ready"], g * 4 + (q + 1))
                    kv = ps[KV_BANK[q]][:].rearrange("p (t f) -> p t f", t=2)
                    for j in range(2):
                        tt = 2 * q + j
                        a.activation(ksq[:, tt, :], kv[:, j, 0:HD], ACT.Square, accum_out=ksum[:, tt:tt + 1])\
                         .then_inc(s["ksum_done"], 1)

            def round_values(g, banks=range(4)):
                for q in banks:
                    kv = ps[KV_BANK[q]][:].rearrange("p (t f) -> p t f", t=2)
                    a.activation(v_hi[:, 2 * q:2 * q + 2, :], kv[:, :, HD:2 * HD], ACT.Copy).then_inc(s["v_hi_done"], 1)

            def query(g, u):
                a.wait_ge(s["q_ready"], g * NU + (u + 1))
                a.activation(qsq[:, u % 2, :], ps[Q_BANK][:], ACT.Square).then_inc(s["qsq_done"], 1)
                a.activation(qt_hi[:, u % 2, :], ps[Q_BANK][:], ACT.Copy).then_inc(s["qt_hi_done"], 1)

            def round_keys(g, b):
                a.wait_ge(s["kt_ready"], g * B + (b + 1))
                a.activation(kt_hi[:, b, :], ps[b][:], ACT.Copy, scale=kq_scale[:, 0:1]).then_inc(s["kt_hi_done"], 1)

            def open_group(g):
                for b in range(B):
                    round_keys(g, b)
                query(g, 0)

            def output(g, u):
                a.wait_ge(s["o_ready"], g * NU + (u + 1))
                a.activation(ot_hi[:, u, :], ps[O_BANK][:], ACT.Copy).then_inc(s["ot_hi_done"], 1)

            def group(g, last):
                for k in range(NU + 1):
                    score, turn, value, ahead = steps_of(k)
                    if score is not None:
                        sl = score % 2
                        for j in reversed(range(NQ)):
                            if k <= 1 and j == 1:
                                query(g, ahead)
                            if j % 2:
                                a.wait_ge(s["bias_done"], g * 2 * NU + (2 * score + (NQ - j + 1) // 2))
                            bank, col = S_BANK[j]
                            n = P * (j + 1)
                            a.activation(prob[:, sl, POFF[j]:POFF[j + 1]], ps[bank][:, col:col + n], ACT.Exp,
                                         bias=sbias[:, sl, j:j + 1], scale=qrs[:, sl, j:j + 1],
                                         accum_out=rsum[:, sl, j:j + 1]).then_inc(s["exp_done"], 1)
                    if ahead is not None and k > 1:
                        query(g, ahead)
                    if k == NU and not last:
                        square_keys(g + 1, (0, 1))
                    if value is not None:
                        output(g, value)
                    if turn is not None:
                        for c in range(3):
                            a.wait_ge(s["pt_ready"], g * 3 * NU + (3 * turn + c + 1))
                            n = T_CUTS[c + 1] - T_CUTS[c]
                            a.activation(pt_hi[:, turn % 2, T_CUTS[c]:T_CUTS[c + 1]], ps[T_BANK + c][:, 0:n], ACT.Copy)\
                             .then_inc(s["pt_hi_done"], 1)
                    if k == 1:
                        a.wait_ge(s["o_in"], g * 16 + 16)
                        a.wait_ge(s["acc_free"], g * 4 + 4)
                        a.activation(wo_hi[:].rearrange("p h d -> p (h d)"), oraw[:], ACT.Copy)\
                         .then_inc(s["wo_hi_done"], 1)
                    if k == 2 and not last:
                        round_kv_weights(g + 1)
                    if k == NU - 1 and not last:
                        round_q_weights(g + 1)
                if not last:
                    square_keys(g + 1, (2, 3))
                output(g, NU - 1)
                if not last:
                    round_values(g + 1)
                    open_group(g + 1)

            round_kv_weights(0)
            ln["scalar"](a, (0,))
            round_q_weights(0)
            ln["scalar"](a, (1,))
            for banks in (range(2), range(2, 4)):
                square_keys(0, banks)
                round_values(0, banks)
            a.wait_ge(s["scale_ready"], 1)
            round_keys(0, 0)
            query(0, 0)
            round_keys(0, 1)
            with a.Fori(0, NKV - 1) as g:
                group(g, False)
            group(NKV - 1, True)

        @block.gpsimd
        def _(p):
            def low_kv_weights(g):
                p.wait_ge(s["wkv_hi_done"], g + 1)
                p.tensor_tensor(wkv_lo[:], first_kv if isinstance(g, int) else raw_kv, wkv_hi[:].bitcast(F32), ALU.subtract).then_inc(s["wkv_lo_done"], 1)

            def low_q_weights(g):
                p.wait_ge(s["wq_hi_done"], g + 1)
                p.tensor_tensor(wq_lo[:], raw_q, wq_hi[:].bitcast(F32), ALU.subtract).then_inc(s["wq_lo_done"], 1)

            low_kv_weights(0)
            factors["powers"](p, 1)
            low_q_weights(0)

            def key_factors(g):
                for b in range(B):
                    part = slice(b * NQ, (b + 1) * NQ)
                    p.wait_ge(s["ksum_eps_done"], g * B + (b + 1))
                    p.tensor_tensor(krs[:, part], ksum_eps[:, part], pm["minus_half"][:, part], ALU.pow)\
                     .then_inc(s["krs_done"], 1)

            def query_factor(g, u):
                p.wait_ge(s["qsum_done"], g * NU + (u + 1))
                p.tensor_tensor(qrs[:, u % 2, :], qsum[:, u % 2, :], pm["minus_half"][:, 0:NQ], ALU.pow)\
                 .then_inc(s["qrs_done"], 1)

            def group(g, last):
                for u in range(1, NU):
                    query_factor(g, u)
                    if u == 2:
                        p.wait_ge(s["wo_hi_done"], g + 1)
                        p.tensor_tensor(wo_lo[:].rearrange("p h d -> p (h d)"), oraw[:],
                                        wo_hi[:].rearrange("p h d -> p (h d)").bitcast(F32), ALU.subtract)\
                         .then_inc(s["wo_lo_done"], 1)
                    if u == 4 and not last:
                        low_kv_weights(g + 1)
                if not last:
                    low_q_weights(g + 1)
                    key_factors(g + 1)
                    query_factor(g + 1, 0)

            key_factors(0)
            query_factor(0, 0)
            with p.Fori(0, NKV - 1) as g:
                group(g, False)
            group(NKV - 1, True)
            following["powers"](p, 0)

        @block.vector
        def _(v):
            def key_sums(g, b):
                v.wait_ge(s["ksum_done"], g * NT + NQ * (b + 1))
                part = slice(b * NQ, (b + 1) * NQ)
                v.tensor_scalar(ksum_eps[:, part], ksum[:, part], 1.0 / HD, QK_EPS, ALU.mult, ALU.add)\
                 .then_inc(s["ksum_eps_done"], 1)

            def keys_and_values(g, batches=range(B)):
                for b in batches:
                    v.wait_ge(s["krs_done"], g * B + (b + 1))
                    for tt in range(b * NQ, (b + 1) * NQ):
                        if tt % 2 == 0:
                            v.wait_ge(s["v_hi_done"], g * 4 + (tt // 2 + 1))
                        kv = ps[KV_BANK[tt // 2]][:].rearrange("p (t f) -> p t f", t=2)
                        v.tensor_scalar(kn[:, tt, :], kv[:, tt % 2, 0:HD], krs[:, tt:tt + 1], None, ALU.mult)\
                         .then_inc(s["kn_done"], 1)
                    for q in (2 * b, 2 * b + 1):
                        kv = ps[KV_BANK[q]][:].rearrange("p (t f) -> p t f", t=2)
                        v.tensor_tensor(v_lo[:, 2 * q:2 * q + 2, :], kv[:, :, HD:2 * HD],
                                        v_hi[:, 2 * q:2 * q + 2, :].bitcast(F32), ALU.subtract)\
                         .then_inc(s["v_lo_done"], 1)

            def query_low(g, u):
                v.wait_ge(s["qt_hi_done"], g * NU + (u + 1))
                v.tensor_tensor(qt_lo[:, u % 2, :], ps[Q_BANK][:], qt_hi[:, u % 2, :].bitcast(F32), ALU.subtract)\
                 .then_inc(s["qt_lo_done"], 1)

            def query_sum(g, u):
                v.wait_ge(s["qsum_ready"], g * NU + (u + 1))
                v.tensor_scalar(qsum[:, u % 2, :], ps[1][:, QSUM_COL:QSUM_COL + NQ], HD * QK_EPS, None, ALU.add)\
                 .then_inc(s["qsum_done"], 1)

            def keys_low(g, b):
                v.wait_ge(s["kt_hi_done"], g * B + (b + 1))
                v.scalar_tensor_tensor(out=kt_lo[:, b, :], in0=ps[b][:], scalar=kq_scale[:, 0:1],
                                       in1=kt_hi[:, b, :].bitcast(F32), op0=ALU.mult, op1=ALU.subtract)\
                 .then_inc(s["kt_lo_done"], 1)

            def open_group(g):
                for b in range(B):
                    keys_low(g, b)
                query_low(g, 0)

            def output_low(g, u):
                v.wait_ge(s["ot_hi_done"], g * NU + (u + 1))
                v.tensor_tensor(ot_lo[:, u, :], ps[O_BANK][:], ot_hi[:, u, :].bitcast(F32),
                                ALU.subtract).then_inc(s["ot_lo_done"], 1)

            def transposed_low(g, u, cuts):
                for c in cuts:
                    v.wait_ge(s["pt_hi_done"], g * 3 * NU + (3 * u + c + 1))
                    n = T_CUTS[c + 1] - T_CUTS[c]
                    dst = slice(T_CUTS[c], T_CUTS[c + 1])
                    v.tensor_tensor(pt_lo[:, u % 2, dst], ps[T_BANK + c][:, 0:n],
                                    pt_hi[:, u % 2, dst].bitcast(F32), ALU.subtract)\
                     .then_inc(s["pt_lo_done"], 1)

            def add_output(g, q, last=False):
                v.wait_ge(s["y_ready"], g * 4 + (q + 1))
                dst = X[:, 2 * q:2 * q + 2, :].rearrange("p t d -> p (t d)")
                v.tensor_tensor(dst, dst, ps[Y_BANKS[last][q]][:], ALU.add).then_inc(s["acc_free"], 1)

            def maxima(g, u, tiles):
                sl = u % 2
                for j in tiles:
                    bank, col = S_BANK[j]
                    v.wait_ge(s["s_ready"], g * NU * NQ + (NQ * u + (NQ if j < 2 else NQ - j)))
                    v.tensor_reduce(smax[:, sl, j:j + 1], ps[bank][:, col:col + P * (j + 1)], AX_X, ALU.max)\
                     .then_inc(s["max_done"], 1)
                v.wait_ge(s["qrs_done"], g * NU + (u + 1))
                v.wait_ge(s["max_done"], g * NU * NQ + (NQ * u + NQ - j))
                v.scalar_tensor_tensor(out=sbias[:, sl, j:j + 2], in0=smax[:, sl, j:j + 2], scalar=-1.0,
                                       in1=qrs[:, sl, j:j + 2], op0=ALU.mult, op1=ALU.mult)\
                 .then_inc(s["bias_done"], 1)

            def group_steps(g, ks, pending):
                for k in ks:
                    score, turn, value, ahead = steps_of(k)
                    if value is not None:
                        transposed_low(g, value, (0,))
                    if score is not None:
                        maxima(g, score, (3, 2))
                    if value is not None:
                        transposed_low(g, value, (1,))
                    if score is not None:
                        maxima(g, score, (1, 0))
                    if value is not None:
                        transposed_low(g, value, (2,))
                    if k <= 1:
                        query_low(g, ahead)
                    early_sum = k <= 1 and not pending
                    if early_sum:
                        query_sum(g, ahead)
                    if score is not None:
                        sl = score % 2
                        v.wait_ge(s["exp_done"], g * NU * NQ + NQ * (score + 1))
                        v.reciprocal(rrec[:, sl, :], rsum[:, sl, :]).then_inc(s["rec_done"], 1)
                        v.wait_ge(s["rec_done"], g * NU + (score + 1))
                        for j in range(NQ):
                            pj = prob[:, sl, POFF[j]:POFF[j + 1]]
                            v.tensor_scalar(pj, pj, rrec[:, sl, j:j + 1], None, ALU.mult).then_inc(s["prob_done"], 1)
                    if ahead is not None and k > 1:
                        query_low(g, ahead)
                    if value is not None:
                        output_low(g, value)
                    if ahead is not None and not early_sum:
                        query_sum(g, ahead)
                    if pending:
                        add_output(g - 1, 3)

            def group(g, last):
                group_steps(g, range(1, NU + 1), False)
                if not last:
                    key_sums(g + 1, 0)
                transposed_low(g, NU - 1, (0, 1, 2))
                if not last:
                    key_sums(g + 1, 1)
                output_low(g, NU - 1)
                if not last:
                    keys_and_values(g + 1)
                for q in range(2):
                    add_output(g, q, last)
                if not last:
                    open_group(g + 1)
                if last:
                    v.wait_ge(s["acc_free"], g * 4 + 6)
                    following["statistics"](v, range(HT))
                    following["variances"](v, 0, HT)
                add_output(g, 2, last)
                if not last:
                    query_sum(g + 1, 0)
                    group_steps(g + 1, (0,), True)
                else:
                    add_output(g, 3, last)

            ln["vector"](v)
            v.wait_ge(s["scale_in"], 32)
            v.tensor_tensor(kq_scale[:], scales[:, 0:1], scales[:, 1:2], ALU.mult).then_inc(s["scale_ready"], 1)
            v.sem_inc(s["acc_free"], 4)
            key_sums(0, 0)
            keys_and_values(0, (0,))
            key_sums(0, 1)
            keys_low(0, 0)
            keys_and_values(0, (1,))
            query_low(0, 0)
            keys_low(0, 1)
            query_sum(0, 0)
            group_steps(0, (0,), False)
            with v.Fori(0, NKV - 1) as g:
                v.wait_ge(s["acc_free"], g * 4 + 4)
                group(g, False)
            v.wait_ge(s["acc_free"], 4 * NKV)
            group(NKV - 1, True)

        @block.tensor
        def _(t):
            ln["tensor"](t, 0)

            def triple(dst, lhs, rhs, start, stop):
                (lh, ll), (rh, rl) = lhs, rhs
                for q, (l, r) in enumerate(((lh, rh), (ll, rh), (lh, rl))):
                    m = t.matmul(dst, l, r, start=start and q == 0, stop=stop and q == 2)
                return m

            def keys_and_values(g, banks):
                for q in banks:
                    for j in range(2):
                        tok = slice((2 * q + j) * P, (2 * q + j + 1) * P)
                        for k in range(KH):
                            m = triple(ps[KV_BANK[q]][:, j * 2 * HD:(j + 1) * 2 * HD],
                                       (xt_hi[:, k, tok], xt_lo[:, k, tok]),
                                       (wkv_hi[:, k, :], wkv_lo[:, k, :]), k == 0, k == KH - 1)
                    m.then_inc(s["kv_ready"], 1)

            def query(g, u):
                b, h = divmod(u, REP)
                if u >= 1:
                    t.wait_ge(s["qt_lo_done"], g * NU + u)
                tok = slice(b * C, (b + 1) * C)
                col = slice(h * HD, (h + 1) * HD)
                for k in range(KH):
                    m = triple(ps[Q_BANK][:], (wq_hi[:, k, col], wq_lo[:, k, col]),
                               (xt_hi[:, k, tok], xt_lo[:, k, tok]), k == 0, k == KH - 1)
                m.then_inc(s["q_ready"], 1)

            def query_sum(g, u):
                t.wait_ge(s["qsq_done"], g * NU + (u + 1))
                if u >= 1:
                    t.wait_ge(s["exp_done"], g * NU * NQ + (NQ * (u - 1) + 2))
                for j in range(NQ):
                    m = t.matmul(ps[1][:, QSUM_COL + j:QSUM_COL + j + 1], qsq[:, u % 2, j * P:(j + 1) * P],
                                 ones[:, 0:1], start=True, stop=True)
                m.then_inc(s["qsum_ready"], 1)

            def turn_keys(g, b):
                t.wait_ge(s["v_lo_done"], g * 4 + (2 + b))
                for j in range(NQ):
                    m = t.transpose(ps[b][:, j * P:(j + 1) * P], kn[:, b * NQ + j, :], pm["ident"][:])
                m.then_inc(s["kt_ready"], 1)

            def open_group(g):
                for b in range(B):
                    turn_keys(g, b)
                t.wait_ge(s["wq_lo_done"], g + 1)
                query(g, 0)

            def group_steps(g, ks, last, pending=False):
                def scores(u):
                    b, sl = u // REP, u % 2
                    t.wait_ge(s["qt_lo_done"], g * NU + (u + 1))
                    for j in reversed(range(NQ)):
                        bank, col = S_BANK[j]
                        if u >= 1 and j >= 1:
                            done = NQ * (u - 1) + (NQ if j == 1 else NQ - j)
                            t.wait_ge(s["exp_done"], g * NU * NQ + done)
                        if j == 2:
                            t.wait_ge(s["qsum_done"], g * NU + (u + 1))
                        q = slice(j * P, (j + 1) * P)
                        n = P * (j + 1)
                        triple(ps[bank][:, col:col + n], (qt_hi[:, sl, q], qt_lo[:, sl, q]),
                               (kt_hi[:, b, 0:n], kt_lo[:, b, 0:n]), True, False)
                        t.matmul(ps[bank][:, col + n - P:col + n], pm["ident_b"][:], pm["causal"][:],
                                 start=False, stop=True).then_inc(s["s_ready"], 1)

                def transposes(u):
                    sl = u % 2
                    t.wait_ge(s["prob_done"], g * NU * NQ + NQ * (u + 1))
                    for i in range(NQ):
                        bank = T_BANK + min(i, 2)
                        if u >= 1 and i < 3:
                            t.wait_ge(s["pt_lo_done"], g * 3 * NU + (3 * (u - 1) + i + 1))
                        base = TOFF[i] - T_CUTS[min(i, 2)]
                        for j in range(i, NQ):
                            c = base + (j - i) * P
                            p0 = POFF[j] + i * P
                            m = t.transpose(ps[bank][:, c:c + P], prob[:, sl, p0:p0 + P], pm["ident"][:])
                        if i != 2:
                            m.then_inc(s["pt_ready"], 1)

                def values(u):
                    b, sl = u // REP, u % 2
                    if u >= 1:
                        t.wait_ge(s["ot_lo_done"], g * NU + u)
                    for i in range(NQ):
                        if i < 3:
                            t.wait_ge(s["pt_lo_done"], g * 3 * NU + (3 * u + i + 1))
                        src = slice(TOFF[i], TOFF[i + 1])
                        m = triple(ps[O_BANK][:, i * P:C], (v_hi[:, b * NQ + i, :], v_lo[:, b * NQ + i, :]),
                                   (pt_hi[:, sl, src], pt_lo[:, sl, src]), i == 0, i == NQ - 1)
                    m.then_inc(s["o_ready"], 1)

                for k in ks:
                    score, turn, value, ahead = steps_of(k)
                    if score is not None:
                        scores(score)
                    if ahead is not None:
                        query(g, ahead)
                    if pending:
                        project(g - 1, 3)
                    elif k == 0:
                        keep_busy(t, pm, ps[4], 8)
                    if k == NU - 1 and not last:
                        t.wait_ge(s["wkv_lo_done"], g + 2)
                        t.wait_ge(s["qt_lo_done"], g * NU + NU)
                        keys_and_values(g + 1, (0,))
                    if k == NU and last:
                        t.wait_ge(s["wo_lo_done"], g + 1)
                        t.wait_ge(s["qt_lo_done"], g * NU + NU)
                        project(g, 0, last, (0,))
                    if k == 1:
                        t.wait_ge(s["acc_free"], g * 4 + 4)
                    if k == NU and not last:
                        t.wait_ge(s["exp_done"], g * NU * NQ + NU * NQ)
                        keys_and_values(g + 1, (1, 2))
                    if value is not None:
                        values(value)
                    if turn is not None:
                        transposes(turn)
                    if ahead is not None:
                        query_sum(g, ahead)
                if NU in ks:
                    if not last:
                        keys_and_values(g + 1, (3,))
                    else:
                        project(g, 0, last, (1,))
                    values(NU - 1)
                    if last:
                        t.wait_ge(s["exp_done"], g * NU * NQ + NU * NQ)
                        project(g, 1, last)

            def project(g, q, last=False, tiles=(0, 1)):
                b, j0 = divmod(2 * q, NQ)
                t.wait_ge(s["ot_lo_done"], g * NU + (REP * (b + 1)))
                for j in tiles:
                    tok = slice((j0 + j) * P, (j0 + j + 1) * P)
                    for h in range(REP):
                        m = triple(ps[Y_BANKS[last][q]][:, j * D:(j + 1) * D],
                                   (ot_hi[:, b * REP + h, tok], ot_lo[:, b * REP + h, tok]),
                                   (wo_hi[:, h, :], wo_lo[:, h, :]), h == 0, h == REP - 1)
                if 1 in tiles:
                    m.then_inc(s["y_ready"], 1)

            def group(g, last):
                group_steps(g, range(1, NU + 1), last)
                t.wait_ge(s["wo_lo_done"], g + 1)
                t.wait_ge(s["pt_lo_done"], g * 3 * NU + 3 * NU)
                if last:
                    project(g, 2, last)
                    project(g, 3, last)
                else:
                    project(g, 0)
                    project(g, 1)
                    open_group(g + 1)
                    project(g, 2)
                    t.wait_ge(s["kt_lo_done"], g * B + 2 * B)
                    query_sum(g + 1, 0)
                    group_steps(g + 1, (0,), False, pending=True)

            t.wait_ge(s["wkv_lo_done"], 1)
            t.wait_ge(xt_done, KH)
            keys_and_values(0, (0,))
            ln["tensor"](t, 1)
            keys_and_values(0, (1,))
            t.wait_ge(xt_done, 2 * KH)
            keys_and_values(0, (2, 3))
            keep_busy(t, pm, ps[4], 4)
            turn_keys(0, 0)
            t.wait_ge(s["wq_lo_done"], 1)
            query(0, 0)
            keep_busy(t, pm, ps[4], 9)
            turn_keys(0, 1)
            keep_busy(t, pm, ps[4], 8)
            t.wait_ge(s["kt_lo_done"], B)
            query_sum(0, 0)
            group_steps(0, (0,), False)
            with t.Fori(0, NKV - 1) as g:
                group(g, False)
            group(NKV - 1, True)
            keep_busy(t, pm, ps[1], 6)


def build(nc, ins, out):
    with ExitStack() as ctx:
        cm = lambda n: ctx.enter_context(nc.semaphore(n))
        sb = lambda n, s, d: ctx.enter_context(nc.sbuf_tensor(n, s, d))
        ps = [ctx.enter_context(nc.psum_tensor(f"bank{i}", [P, 512], F32)) for i in range(8)]
        pm = {
            "X": sb("X", [P, NT, D], F32),
            "ident": sb("ident", [P, P], F32),
            "ident_b": sb("ident_b", [P, P], BF16),
            "causal": sb("causal", [P, P], BF16),
            "zeros": sb("zeros", [P, B * D], BF16),
            "ones": sb("ones", [P, 1], F32),
            "stats": sb("stats", [P, NT, 6], F32),
            "moments": sb("moments", [P, NT, 2], F32),
            "var_eps": sb("var_eps", [P, NT], F32),
            "rstd": sb("rstd", [P, NT], F32),
            "gate_w": sb("gate_w", [P, KH * NE], F32),
            "first_w": sb("first_w", [P, FIRST_W2 + D], F32),
            "minus_half": sb("minus_half", [P, B * NCB], F32),
        }
        factors = [layernorm_factors(tag, cm, pm) for tag in ("f1", "at", "f2")]
        first_in = cm("first_in")

        def first_ffn(sp, with_gate):
            if with_gate:
                sp.dma_start(pm["gate_w"][:], ins["gate_w"]).then_inc(first_in, 16)
            rows = SHARED[0]
            sp.dma_start(pm["first_w"][:, 0:KH * 2 * rows], ins["sw13_0"]).then_inc(first_in, 16)
            sp.dma_start(pm["first_w"][0:rows, FIRST_W2:FIRST_W2 + D], ins["sw2"][0:rows, :]).then_inc(first_in, 16)

        def first_attention(sp):
            sp.dma_start(pm["first_w"][:, 0:KH * 2 * HD].rearrange("p (k f) -> p k f", k=KH),
                         ins["wqkv"][0].rearrange("p (k f) -> p k f", k=KH)[:, :, REP * HD:(REP + 2) * HD])\
              .then_inc(first_in, 16)

        prefetch = [(lambda sp: first_ffn(sp, True), lambda e: e.wait_ge(first_in, 48)),
                    (first_attention, lambda e: e.wait_ge(first_in, 64)),
                    (lambda sp: first_ffn(sp, False), lambda e: e.wait_ge(first_in, 96))]
        conv_phase(nc, cm, pm, ps, ins, ins["wconv"], factors[0], prefetch[0])
        ffn_phase(nc, cm, pm, ps, ins, "f1", factors[0], True, prefetch[0], factors[1], prefetch[1], None)
        attention_phase(nc, cm, pm, ps, ins, factors[1], prefetch[1], factors[2], prefetch[2])
        ffn_phase(nc, cm, pm, ps, ins, "f2", factors[2], False, prefetch[2], None, None, out)


def kernel(**inputs):
    import numpy as np
    import concourse.bacc as bacc
    from concourse.bass_utils import run_bass_kernel_spmd as run

    a = {k.replace("L0_", ""): np.asarray(v) for k, v in inputs.items()}
    routed13 = a["ffn_w13"].reshape(NE, 2, EI, KH, P)
    shared13 = a["ffn_sw13"].reshape(2, SI, KH, P)
    layouts = {
        "x": a["attn_a_x"],
        "cols": a["attn_a_cols"],
        "rows": a["attn_a_rows"],
        "wconv": a["attn_a_block_values"].reshape(NBLK, 2, HO, BS, NST, 2).transpose(4, 1, 0, 2, 5, 3)
                 .reshape(2 * NST, NBLK, HO * P),
        "gate_w": a["ffn_gate_w"].reshape(NE, KH, P).transpose(2, 1, 0).reshape(P, KH * NE),
        "w13": routed13.transpose(1, 2, 0, 3, 4).reshape(2, NRT, P, KH, P).transpose(1, 4, 3, 0, 2)
               .reshape(NRT, P, KH * 2 * P),
        "w2": a["ffn_w2"].transpose(2, 0, 1).reshape(NRT, P, D),
        "sw2": a["ffn_sw2"].T,
        "q_scale": a["attn_b_q_scale"],
        "k_scale": a["attn_b_k_scale"],
        "wqkv": np.concatenate([a["attn_b_Wq"].reshape(NKV, REP * HD, KH, P), a["attn_b_Wk"].reshape(NKV, HD, KH, P),
                                a["attn_b_Wv"].reshape(NKV, HD, KH, P)], axis=1).transpose(0, 3, 2, 1)
                .reshape(NKV, P, KH * (REP + 2) * HD),
        "wo": a["attn_b_Wo"].reshape(D, NKV, REP, HD).transpose(1, 3, 2, 0).reshape(NKV, HD, REP * D),
    }
    r0 = 0
    for m, rows in enumerate(SHARED):
        layouts[f"sw13_{m}"] = shared13[:, r0:r0 + rows].transpose(3, 2, 0, 1).reshape(P, KH * 2 * rows)
        r0 += rows

    nc = bacc.Bacc("TRN2", target_bir_lowering=False, num_devices=1)
    arrays, ins = {}, {}
    for name, value in layouts.items():
        value = np.ascontiguousarray(value)
        arrays[f"in_{name}"] = value
        ins[name] = nc.dram_tensor(f"in_{name}", value.shape, mybir.dt.from_np(value.dtype), kind="ExternalInput").ap()
    out = nc.dram_tensor("out", (B, C, D), F32, kind="ExternalOutput").ap()
    build(nc, ins, out)
    return run(nc, [arrays], core_ids=[0]).results[0]["out"]
```
